# Optimizing a Trainium2 kernel written in Bass

```python
import numpy as np
import jax
import jax.numpy as jnp

def _softmax(x, axis=-1):
    return jax.nn.softmax(x, axis=axis)

def _gelu(x):
    return jax.nn.gelu(x, approximate=True)

def _silu(x):
    return jax.nn.silu(x)

def _sigmoid(x):
    return jax.nn.sigmoid(x)

def _layernorm(x, axis=-1, eps=1e-05):
    m = jnp.mean(x, axis=axis, keepdims=True)
    v = jnp.var(x, axis=axis, keepdims=True)
    return (x - m) / jnp.sqrt(v + eps)

def _scatter_add(tgt, idx, src, axis=0):
    return tgt.at[idx].add(src)

def _segment_sum(src, seg, n):
    return jax.ops.segment_sum(src, seg, n)
kernel_name = 'mk_recurrent_d1_jaxref_r4_35f635'

def setup_inputs(seed: int=0):
    np.random.seed(seed)
    _w = jnp.asarray

    def _L0_attn_setup():
        import jax, jax.numpy as jnp
        import numpy as np
        DIM = 256
        HID = int(DIM * 1.5)
        GHID = int(DIM * 2)
        K = 4
        ALPHA_LOG_SCALE = -8.0

        def _rmsnorm(x, gamma):
            n = jnp.linalg.norm(x, axis=-1, keepdims=True)
            return gamma * jnp.sqrt(jnp.asarray(x.shape[-1], x.dtype)) * (x / n)

        def _causal_depthwise_conv(x, w, b):
            xc = jnp.transpose(x, (0, 2, 1))
            xc = jnp.pad(xc, ((0, 0), (0, 0), (K - 1, 0)))
            y = jax.lax.conv_general_dilated(xc, w, window_strides=(1,), padding='VALID', dimension_numbers=('NCH', 'OIH', 'NCH'), feature_group_count=w.shape[0])
            y = y + b[None, :, None]
            return jnp.transpose(y, (0, 2, 1))

        def _linear_scan(alpha, x):

            def combine(c1, c2):
                a1, b1 = c1
                a2, b2 = c2
                return (a1 * a2, a2 * b1 + b2)
            _, h = jax.lax.associative_scan(combine, (alpha, x), axis=1)
            return h
        key = jax.random.key(seed)
        ks = jax.random.split(key, 8)
        N, T = (4, 512)
        x = jax.random.normal(ks[0], (N, T, DIM), jnp.float32)
        W_in = jax.random.normal(ks[1], (2 * HID, DIM), jnp.float32) * DIM ** (-0.5)
        conv_w = jax.random.normal(ks[2], (HID, 1, K), jnp.float32) * 0.25
        conv_b = jnp.zeros((HID,), jnp.float32)
        W_gates = jax.random.normal(ks[3], (2 * HID, HID), jnp.float32) * HID ** (-0.5)
        b_gates = jnp.zeros((2 * HID,), jnp.float32)
        forget_base = jnp.linspace(-4.323, -9.0, HID, dtype=jnp.float32)
        W_out = jax.random.normal(ks[4], (DIM, HID), jnp.float32) * HID ** (-0.5)
        W_grow = jax.random.normal(ks[5], (2 * GHID, DIM), jnp.float32) * DIM ** (-0.5)
        W_shrink = jax.random.normal(ks[6], (DIM, GHID), jnp.float32) * GHID ** (-0.5)
        gamma1 = jnp.ones((DIM,), jnp.float32)
        gamma2 = jnp.ones((DIM,), jnp.float32)
        return {'x': x, 'gamma1': gamma1, 'W_in': W_in, 'conv_w': conv_w, 'conv_b': conv_b, 'W_gates': W_gates, 'b_gates': b_gates, 'forget_base': forget_base, 'W_out': W_out, 'gamma2': gamma2, 'W_grow': W_grow, 'W_shrink': W_shrink}
    _L0_attn_in = _L0_attn_setup()

    def _L0_ffn_setup():
        import jax, jax.numpy as jnp
        import numpy as np
        B, T, D, E, H, K = (4, 512, 256, 8, 512, 2)
        key = jax.random.key(seed)
        k0, k1, k2, k3 = jax.random.split(key, 4)
        x = jax.random.normal(k0, (B, T, D), dtype=jnp.float32)
        router_w = jax.random.normal(k1, (E, D), dtype=jnp.float32) * D ** (-0.5)
        w1 = jax.random.normal(k2, (E, D, H), dtype=jnp.float32) * D ** (-0.5)
        w2 = jax.random.normal(k3, (E, H, D), dtype=jnp.float32) * H ** (-0.5)
        return {'x': x, 'router_w': router_w, 'w1': w1, 'w2': w2}
    _L0_ffn_in = _L0_ffn_setup()
    _d = {'L0_attn_x': _L0_attn_in['x'], 'L0_attn_gamma1': _L0_attn_in['gamma1'], 'L0_attn_W_in': _L0_attn_in['W_in'], 'L0_attn_conv_w': _L0_attn_in['conv_w'], 'L0_attn_conv_b': _L0_attn_in['conv_b'], 'L0_attn_W_gates': _L0_attn_in['W_gates'], 'L0_attn_b_gates': _L0_attn_in['b_gates'], 'L0_attn_forget_base': _L0_attn_in['forget_base'], 'L0_attn_W_out': _L0_attn_in['W_out'], 'L0_attn_gamma2': _L0_attn_in['gamma2'], 'L0_attn_W_grow': _L0_attn_in['W_grow'], 'L0_attn_W_shrink': _L0_attn_in['W_shrink'], 'L0_ffn_router_w': _L0_ffn_in['router_w'], 'L0_ffn_w1': _L0_ffn_in['w1'], 'L0_ffn_w2': _L0_ffn_in['w2']}
    _x0 = _d['L0_attn_x']
    _d['L0_attn_x'] = jax.random.normal(jax.random.fold_in(jax.random.key(seed), 1), (8, 1024, 256), dtype=_x0.dtype)
    del _x0
    return _d

def reference(L0_attn_x, L0_attn_gamma1, L0_attn_W_in, L0_attn_conv_w, L0_attn_conv_b, L0_attn_W_gates, L0_attn_b_gates, L0_attn_forget_base, L0_attn_W_out, L0_attn_gamma2, L0_attn_W_grow, L0_attn_W_shrink, L0_ffn_router_w, L0_ffn_w1, L0_ffn_w2):

    def _L0_attn_ref(x, gamma1, W_in, conv_w, conv_b, W_gates, b_gates, forget_base, W_out, gamma2, W_grow, W_shrink):
        import jax, jax.numpy as jnp
        import numpy as np
        DIM = 256
        HID = int(DIM * 1.5)
        GHID = int(DIM * 2)
        K = 4
        ALPHA_LOG_SCALE = -8.0

        def _rmsnorm(x, gamma):
            n = jnp.linalg.norm(x, axis=-1, keepdims=True)
            return gamma * jnp.sqrt(jnp.asarray(x.shape[-1], x.dtype)) * (x / n)

        def _causal_depthwise_conv(x, w, b):
            xc = jnp.transpose(x, (0, 2, 1))
            xc = jnp.pad(xc, ((0, 0), (0, 0), (K - 1, 0)))
            y = jax.lax.conv_general_dilated(xc, w, window_strides=(1,), padding='VALID', dimension_numbers=('NCH', 'OIH', 'NCH'), feature_group_count=w.shape[0])
            y = y + b[None, :, None]
            return jnp.transpose(y, (0, 2, 1))

        def _linear_scan(alpha, x):

            def combine(c1, c2):
                a1, b1 = c1
                a2, b2 = c2
                return (a1 * a2, a2 * b1 + b2)
            _, h = jax.lax.associative_scan(combine, (alpha, x), axis=1)
            return h
        xn = _rmsnorm(x, gamma1)
        u = jnp.einsum('btd,hd->bth', xn, W_in)
        gate, v = jnp.split(u, 2, axis=-1)
        v = _causal_depthwise_conv(v, conv_w, conv_b)
        g = jnp.einsum('bth,gh->btg', v, W_gates) + b_gates
        forget, inp = jnp.split(g, 2, axis=-1)
        log_alpha = ALPHA_LOG_SCALE * jax.nn.softplus(forget_base) * jax.nn.sigmoid(forget)
        alpha = jnp.exp(log_alpha)
        beta = jnp.sqrt(1.0 - alpha ** 2 + 1e-06)
        xg = beta * jax.nn.sigmoid(inp) * v
        h = _linear_scan(alpha, xg)
        hawk_out = jnp.einsum('bth,dh->btd', jax.nn.gelu(gate, approximate=False) * h, W_out)
        x = x + hawk_out
        xn2 = _rmsnorm(x, gamma2)
        grow = jnp.einsum('btd,gd->btg', xn2, W_grow)
        gate2, v2 = jnp.split(grow, 2, axis=-1)
        mlp = jnp.einsum('btg,dg->btd', jax.nn.gelu(gate2, approximate=False) * v2, W_shrink)
        return x + mlp

    def _L0_ffn_ref(x, router_w, w1, w2):
        import jax, jax.numpy as jnp
        import numpy as np
        B, T, D, E, H, K = (4, 512, 256, 8, 512, 2)
        Bb, Tt, Dd = x.shape
        N = Bb * Tt
        logits = jnp.einsum('btd,ed->bte', x, router_w)
        top_vals, top_idx = jax.lax.top_k(logits, K)
        top_w = jax.nn.softmax(top_vals, axis=-1)
        xf = x.reshape(N, Dd)
        h = jnp.einsum('nd,edh->enh', xf, w1)
        h = jnp.square(jax.nn.relu(h))
        y = jnp.einsum('enh,ehd->end', h, w2)
        idx_f = top_idx.reshape(N, K)
        w_f = top_w.reshape(N, K)
        y_sel = y[idx_f, jnp.arange(N)[:, None]]
        out = jnp.einsum('nk,nkd->nd', w_f, y_sel)
        return out.reshape(Bb, Tt, Dd)
    x = L0_attn_x
    xn = _layernorm(x, axis=-1)
    s = _L0_attn_ref(xn, L0_attn_gamma1, L0_attn_W_in, L0_attn_conv_w, L0_attn_conv_b, L0_attn_W_gates, L0_attn_b_gates, L0_attn_forget_base, L0_attn_W_out, L0_attn_gamma2, L0_attn_W_grow, L0_attn_W_shrink)
    g = _silu(_L0_ffn_ref(xn, L0_ffn_router_w, L0_ffn_w1, L0_ffn_w2))
    x = x + s * g
    return x

_drawn_inputs = setup_inputs


def setup_inputs(seed=0):
    import zlib

    import numpy as np

    out = dict(_drawn_inputs(seed))
    spreads = {'L0_attn_gamma1': (1.0, 0.2),
     'L0_attn_conv_b': (0.0, 0.1),
     'L0_attn_b_gates': (0.0, 0.535),
     'L0_attn_gamma2': (1.0, 0.2)}
    factors = {}
    for name, (base, spread) in spreads.items():
        noise = np.random.default_rng([zlib.crc32(name.encode()), seed]).standard_normal(out[name].shape)
        drawn = base * np.exp(spread * noise) if base else spread * noise
        out[name] = jnp.asarray(drawn.astype(out[name].dtype))
    for name, factor in factors.items():
        out[name] = (out[name] * factor).astype(out[name].dtype)
    return out
```

```python
from contextlib import ExitStack

import concourse.bass as bass
from concourse import mybir

P = 128
F32 = mybir.dt.float32
F32R = mybir.dt.float32r
BF16 = mybir.dt.bfloat16
U32 = mybir.dt.uint32
I32 = mybir.dt.int32
ALU = mybir.AluOpType
ACT = mybir.ActivationFunctionType
AX_X = mybir.AxisListType.X
ds = bass.ds

LN_EPS = 1e-5
BETA_EPS = 1e-6
ALPHA_LOG_SCALE = -8.0
BIG = 3.0e38
GROUP = 4


class Chain:

    def __init__(self, eng, sem):
        self.eng, self.sem, self.n, self.base = eng, sem, 0, None

    def link(self, ins):
        ins.then_inc(self.sem, 1)
        self.n += 1
        self.eng.wait_ge(self.sem, self.n if self.base is None else self.base + self.n)

    def repeat(self, i, first, per_turn):
        self.base = (i - first) * per_turn
        self.mark = self.n

    def end_turn(self, turns, per_turn):
        assert self.n - self.mark == per_turn, (self.n - self.mark, per_turn)
        self.base = None
        self.n = self.mark + turns * per_turn


def normalise_and_route(nc, sb, t, x, router_w, w1, w2, xn_dram):
    N, D = x.shape
    E, _, H = w1.shape
    NT = N // P
    NG = NT // GROUP
    KD, KH = D // P, H // P
    GC = GROUP * P
    T = t["tiles"]
    WD = KD * H

    x_v = x.rearrange("(g q p) d -> g p q d", q=GROUP, p=P)
    xn_v = xn_dram.rearrange("(g q p) d -> g p q d", q=GROUP, p=P)
    w1_v = w1.rearrange("e (k p) h -> e p k h", p=P)
    w2_v = w2.rearrange("e (k p) d -> e p k d", p=P)

    with ExitStack() as ctx:
        def sem(name):
            return ctx.enter_context(nc.semaphore(name))

        def tile(name, shape, dt=F32):
            return ctx.enter_context(nc.sbuf_tensor(name, shape, dt))

        xa = tile("xa", [P, 2, GROUP, D])
        xn = tile("xn", [P, 2, GROUP, D])
        xT = tile("xT", [P, 2, KD, GC])
        stage1 = tile("stage1", [P, WD])
        stage2 = tile("stage2", [P, WD])
        bn6 = tile("bn6", [P, 2, GROUP, 6])
        mv = tile("mv", [P, 2, GROUP, 2])
        std = tile("std", [P, 2, GROUP])
        sv = tile("sv", [P, 2, GROUP])
        rstd = tile("rstd", [P, 2, GROUP])
        isv = tile("isv", [P, 2, GROUP])
        rrow = tile("rrow", [E, D])
        rT = tile("rT", [P, KD, E])
        eps = tile("eps", [P, 1])
        logit = tile("logit", [P, NT, E])
        row_f = tile("row_f", [P, P])
        col_f = tile("col_f", [P, 1])
        tri = tile("tri", [P, P], BF16)
        ones = tile("ones", [P, P], BF16)
        iota_e = tile("iota_e", [P, E])
        iota_cap = tile("iota_cap", [P, NT])
        iota_a = tile("iota_a", [P, T])
        iota_ab = tile("iota_ab", [P, T], BF16)
        iota_b = tile("iota_b", [P, P], BF16)
        iota_t = tile("iota_t", [P, NT])
        wk = [tile(f"wk{n}", [P, NT, E]) for n in range(4)]
        oh = [tile(f"oh{n}", [P, NT, E]) for n in range(2)]
        chosen = tile("chosen", [P, NT, E], BF16)
        best = [tile(f"best{n}", [P, NT]) for n in range(2)]
        ix = tile("ix", [P, NT])
        tot = tile("tot", [P, E, NT])
        inc = tile("inc", [P, E, NT])
        zeros_nt = tile("zeros_nt", [P, NT])
        tiles_e = tile("tiles_e", [P, E])
        end_e = tile("end_e", [P, E])
        start_e = tile("start_e", [P, E])
        slot_f = tile("slot_f", [P, 2, NT])
        a_i = tile("a_i", [P, 2, NT], I32)
        b_i = tile("b_i", [P, 2, NT], I32)
        a_f = tile("a_f", [P, 2, NT])
        b_f = tile("b_f", [P, 2, NT])
        ohb = tile("ohb", [P, 2, 2, P], BF16)
        oha = tile("oha", [P, 2, 2, 2, T], BF16)
        texp_f = tile("texp_f", [1, T])
        cmp_e = tile("cmp_e", [1, T, E])
        tokf = tile("tokf", [P, T])
        dexp = tile("dexp", [P, NT])
        den = tile("den", [P, NT])
        spare = tile("spare_1", [1, 1])

        x_in = [sem(f"x_in{j}") for j in range(2)]
        small_in = sem("small_in")
        w1_in, w2_in = sem("w1_in"), sem("w2_in")
        w_hi, w_lo = sem("w_hi"), sem("w_lo")
        pool_const, dve_const = sem("pool_const"), sem("dve_const")
        stats_ready, std_ready = sem("stats_ready"), sem("std_ready")
        xn_ready = sem("xn_ready")
        xn_stored = [sem(f"xn_stored{j}") for j in range(2)]
        xT_psum, xT_ready = sem("xT_psum"), sem("xT_ready")
        rT_psum, rT_ready = sem("rT_psum"), sem("rT_ready")
        lg_psum, logits_copied = sem("lg_psum"), sem("logits_copied")
        chosen_ready, prefix_psum = sem("chosen_ready"), sem("prefix_psum")
        score_gap, gap_exp = sem("score_gap"), sem("gap_exp")
        onehot_ready, onehot_used, perm_psum = sem("onehot_ready"), sem("onehot_used"), sem("perm_psum")
        dve_chain = sem("dve_chain_1")
        routed = sem("routed")

        xT_ps = ctx.enter_context(nc.psum_tensor("xT_ps", [P, 2, KD, GC], F32))
        lg_ps = ctx.enter_context(nc.psum_tensor("lg_ps", [P, 2, GC], F32))
        pf_ps = ctx.enter_context(nc.psum_tensor("pf_ps", [P, 2, NT * E], F32))

        ident = t["ident"]
        block = ctx.enter_context(nc.Block())
        TURNS = NG // 2

        @block.sync
        def _(sp):
            def group_of(view, g):
                return view[g] if isinstance(g, int) else view[ds(g, 1)].rearrange("o p q d -> (o p) q d")

            def expert_in(i):
                for src, dst, landed in ((w1_v, stage1, w1_in), (w2_v, stage2, w2_in)):
                    if not (isinstance(i, int) and i == 0):
                        sp.wait_ge(w_lo, 2 * i)
                    s = group_of(src, i)
                    sp.dma_start(dst[:].rearrange("p (k n) -> p k n", k=s.shape[1]), s).then_inc(landed, 16)

            def turn(i, last):
                for j in range(2):
                    g = 2 * i + j
                    sp.wait_ge(xn_ready, g + 1)
                    sp.dma_start(group_of(xn_v, g), xn[:, j]).then_inc(xn_stored[j], 16)
                    if not last:
                        sp.dma_start(xa[:, j], group_of(x_v, g + 2)).then_inc(x_in[j], 16)

            for j in range(2):
                sp.dma_start(xa[:, j], group_of(x_v, j)).then_inc(x_in[j], 16)
            sp.dma_start(rrow[:], router_w).then_inc(small_in, 16)
            expert_in(0)
            turn(0, False)
            with sp.Fori(1, TURNS - 1) as i:
                expert_in(i)
                turn(i, False)
            expert_in(E - 1)
            turn(TURNS - 1, True)
            for j in range(2):
                sp.wait_ge(xn_stored[j], 16 * TURNS)

        @block.gpsimd
        def _(pool):
            pool.iota(row_f[:], pattern=[[1, P]], base=0, channel_multiplier=0, allow_small_or_imprecise_dtypes=True)
            pool.iota(col_f[:], pattern=[[0, 1]], base=0, channel_multiplier=1, allow_small_or_imprecise_dtypes=True)
            pool.iota(iota_e[:], pattern=[[1, E]], base=-E, channel_multiplier=0, allow_small_or_imprecise_dtypes=True)
            pool.iota(iota_cap[:], pattern=[[P, NT]], base=0, channel_multiplier=0, allow_small_or_imprecise_dtypes=True)
            pool.iota(iota_a[:], pattern=[[1, T]], base=0, channel_multiplier=0, allow_small_or_imprecise_dtypes=True)
            pool.iota(iota_ab[:], pattern=[[1, T]], base=0, channel_multiplier=0, allow_small_or_imprecise_dtypes=True)
            pool.iota(iota_b[:], pattern=[[1, P]], base=0, channel_multiplier=0, allow_small_or_imprecise_dtypes=True)
            pool.iota(iota_t[:], pattern=[[1, NT]], base=0, channel_multiplier=0, allow_small_or_imprecise_dtypes=True)
            pool.memset(ones[:], 1.0)
            pool.memset(zeros_nt[:], 0.0)
            pool.memset(eps[:], LN_EPS).then_inc(pool_const, 1)

            def split_low(i, first):
                for n, (stage, landed) in enumerate(((stage1, w1_in), (stage2, w2_in))):
                    pool.wait_ge(w_hi, 2 * i + n + 1)
                    at = ds(i * 2 * WD + n * WD, WD)
                    pool.tensor_tensor(t["w_lo"][:, at], stage[:], t["w_hi"][:, at].bitcast(F32),
                                       ALU.subtract).then_inc(w_lo, 1)

            with pool.Fori(0, E) as i:
                split_low(i, False)

        @block.scalar
        def _(act):
            def deviations(g, j, first):
                act.wait_ge(stats_ready, g + 1)
                if not first:
                    act.wait_ge(xn_ready, g - 1)
                act.activation(std[:, j], mv[:, j, :, 1], ACT.Sqrt, bias=eps[:])
                act.activation(sv[:, j], mv[:, j, :, 1], ACT.Sqrt).then_inc(std_ready, 1)

            def turn(i, first, last):
                for j in range(2):
                    g = 2 * i + j
                    if not (last and j == 1):
                        deviations(g + 1, 1 - j, first and j == 0)
                    act.wait_ge(xT_psum, g + 1)
                    if not first:
                        act.wait_ge(lg_psum, g - 1)
                    for k in range(KD):
                        ev = act.activation(xT[:, j, k], xT_ps[:, j, k], ACT.Copy)
                    ev.then_inc(xT_ready, 1)
                    stage, landed = ((stage1, w1_in), (stage2, w2_in))[j]
                    act.wait_ge(landed, 16 * (i + 1))
                    act.activation(t["w_hi"][:, ds(i * 2 * WD + j * WD, WD)], stage[:], ACT.Copy).then_inc(w_hi, 1)

            act.wait_ge(pool_const, 1)
            deviations(0, 0, True)
            turn(0, True, False)
            with act.Fori(1, TURNS - 1) as i:
                turn(i, False, False)
            turn(TURNS - 1, False, True)
            act.wait_ge(score_gap, 1)
            act.activation(dexp[:], ix[:], ACT.Exp).then_inc(gap_exp, 1)

        @block.tensor
        def _(pe):
            pe.wait_ge(small_in, 16)
            pe.wait_ge(dve_const, 1)
            for k in range(KD):
                tr = pe.transpose(pf_ps[:, 0, k * E:(k + 1) * E], rrow[:, k * P:(k + 1) * P], ident[0:E, 0:E])
            tr.then_inc(rT_psum, 1)

            def transposes(g, j, first):
                pe.wait_ge(xn_ready, g + 1)
                if not first:
                    pe.wait_ge(xT_ready, g - 1)
                for k in range(KD):
                    for q in range(GROUP):
                        tr = pe.transpose(xT_ps[:, j, k, q * P:(q + 1) * P], xn[:, j, q, k * P:(k + 1) * P], ident[:])
                tr.then_inc(xT_psum, 1)

            def logits(g, j, copied):
                pe.wait_ge(xT_ready, g + 1)
                if copied is not None:
                    pe.wait_ge(logits_copied, copied)
                for q in range(GROUP):
                    for k in range(KD):
                        mm = pe.matmul(lg_ps[:, j, q * E:(q + 1) * E], xT[:, j, k, q * P:(q + 1) * P], rT[:, k],
                                       start=(k == 0), stop=(k == KD - 1))
                mm.then_inc(lg_psum, 1)

            transposes(0, 0, True)
            pe.wait_ge(rT_ready, 1)
            transposes(1, 1, True)
            logits(0, 0, None)
            with pe.Fori(1, TURNS) as i:
                transposes(2 * i, 0, False)
                logits(2 * i - 1, 1, 2 * i - 1)
                transposes(2 * i + 1, 1, False)
                logits(2 * i, 0, 2 * i - 1)
            logits(NG - 1, 1, NG - 2)

            pe.wait_ge(chosen_ready, 1)
            pe.matmul(pf_ps[:, 0], tri[:], chosen[:], start=True, stop=True)
            pe.matmul(pf_ps[:, 1], ones[:], chosen[:], start=True, stop=True).then_inc(prefix_psum, 1)

            perm = lg_ps[:, 0, 0:2 * T]

            def place(i, j, n, flags):
                pe.wait_ge(onehot_ready, 2 * i + j + 1)
                for c in range(2):
                    mm = pe.matmul(perm, ohb[:, j, c], oha[:, j, c].rearrange("p v a -> p (v a)"),
                                   start=flags[0] and c == 0, stop=flags[1] and c == 1)
                mm.then_inc(onehot_used, 1)

            place(0, 0, 0, (True, False))
            place(0, 1, 1, (False, False))
            with pe.Fori(1, NT // 2 - 1) as i:
                place(i, 0, 0, (False, False))
                place(i, 1, 0, (False, False))
            place(NT // 2 - 1, 0, 0, (False, False))
            place(NT // 2 - 1, 1, 0, (False, True))

        @block.vector
        def _(dve):
            ch = Chain(dve, dve_chain)
            dve.wait_ge(pool_const, 1)
            dve.tensor_scalar(ident[:], row_f[:], col_f[:], None, ALU.is_equal).then_inc(dve_const, 1)
            dve.tensor_scalar(tri[:], row_f[:], col_f[:], None, ALU.is_gt)

            def stats(g, i, j):
                dve.wait_ge(x_in[j], 16 * (i + 1))
                for q in range(GROUP):
                    ins = dve.bn_stats(bn6[:, j, q], xa[:, j, q])
                ch.link(ins)
                dve.memset(spare[:], 0.0)
                for q in range(GROUP):
                    ins = dve.bn_aggr(mv[:, j, q], bn6[:, j, q])
                ins.then_inc(stats_ready, 1)

            def finish(g, i, j, first):
                dve.wait_ge(std_ready, g + 1)
                dve.reciprocal(rstd[:, j], std[:, j])
                ch.link(dve.reciprocal(isv[:, j], sv[:, j]))
                dve.tensor_tensor(t["r1"][:, ds(g * GROUP, GROUP)], std[:, j], isv[:, j], ALU.mult)
                if not first:
                    dve.wait_ge(xn_stored[j], 16 * i)
                    dve.wait_ge(xT_psum, g - 1)
                for q in range(GROUP):
                    ins = dve.tensor_scalar(xn[:, j, q], xa[:, j, q], mv[:, j, q, 0:1], rstd[:, j, q:q + 1],
                                            ALU.subtract, ALU.mult)
                ins.then_inc(xn_ready, 1)

            def keep_logits(g, j):
                dve.wait_ge(lg_psum, g + 1)
                dve.tensor_copy(logit[:, ds(g * GROUP, GROUP)],
                                lg_ps[:, j, 0:GROUP * E].rearrange("p (q e) -> p q e", q=GROUP)).then_inc(logits_copied, 1)

            stats(0, 0, 0)
            stats(1, 0, 1)
            finish(0, 0, 0, True)
            dve.wait_ge(rT_psum, 1)
            dve.tensor_copy(rT[:], pf_ps[:, 0, 0:KD * E].rearrange("p (k e) -> p k e", k=KD)).then_inc(rT_ready, 1)

            def turn(i, first):
                stats(2 * i + 2, i + 1, 0)
                finish(2 * i + 1, i, 1, first)
                keep_logits(2 * i, 0)
                stats(2 * i + 3, i + 1, 1)
                finish(2 * i + 2, i + 1, 0, False)
                keep_logits(2 * i + 1, 1)

            n0 = ch.n
            turn(0, True)
            per_turn = ch.n - n0
            with dve.Fori(1, TURNS - 1) as i:
                ch.repeat(i, 1, per_turn)
                turn(i, False)
            ch.end_turn(TURNS - 2, per_turn)
            finish(NG - 1, TURNS - 1, 1, False)
            keep_logits(NG - 2, 0)
            keep_logits(NG - 1, 1)
            dve.wait_ge(logits_copied, NG)

            def spread_e(ap):
                return ap.unsqueeze(2).to_broadcast([P, NT, E])

            def spread_t(ap):
                return ap.unsqueeze(1).to_broadcast([P, NT, E])

            score = logit
            for n in range(2):
                ch.link(dve.tensor_reduce(best[n][:], score[:], AX_X, ALU.max))
                ch.link(dve.tensor_tensor(wk[0][:], score[:], spread_e(best[n][:]), ALU.is_equal))
                ch.link(dve.scalar_tensor_tensor(wk[1][:], wk[0][:], float(E), spread_t(iota_e[:]), ALU.mult, ALU.subtract))
                ch.link(dve.tensor_reduce(ix[:], wk[1][:], AX_X, ALU.max))
                ch.link(dve.tensor_tensor(wk[2][:], wk[1][:], spread_e(ix[:]), ALU.is_equal))
                ch.link(dve.tensor_tensor(oh[n][:], wk[2][:], wk[0][:], ALU.mult))
                if n == 0:
                    ch.link(dve.tensor_scalar(wk[1][:], oh[0][:], -0.5, -BIG, ALU.add, ALU.mult))
                    ch.link(dve.tensor_tensor(wk[3][:], logit[:], wk[1][:], ALU.min))
                    score = wk[3]
            dve.tensor_tensor(chosen[:], oh[0][:], oh[1][:], ALU.add).then_inc(chosen_ready, 1)
            dve.tensor_tensor(ix[:], best[1][:], best[0][:], ALU.subtract).then_inc(score_gap, 1)

            dve.wait_ge(prefix_psum, 1)
            ch.link(dve.tensor_copy(tot[:], pf_ps[:, 1].rearrange("p (t e) -> p e t", e=E)))
            for e in range(E):
                ins = dve.tensor_tensor_scan(inc[:, e], tot[:, e], zeros_nt[:], 0.0, ALU.add, ALU.add)
            ch.link(ins)
            ch.link(dve.tensor_tensor(wk[1][:].rearrange("p t e -> p (t e)").rearrange("p (e t) -> p e t", e=E),
                                      inc[:, :, NT - 1:NT].to_broadcast([P, E, NT]),
                                      iota_cap[:].unsqueeze(1).to_broadcast([P, E, NT]), ALU.is_gt))
            ch.link(dve.tensor_reduce(tiles_e[:], wk[1][:].rearrange("p t e -> p (t e)").rearrange("p (e t) -> p e t", e=E),
                                      AX_X, ALU.add))
            ch.link(dve.tensor_tensor_scan(end_e[:], tiles_e[:], zeros_nt[:, 0:E], 0.0, ALU.add, ALU.add))
            ch.link(dve.tensor_tensor(start_e[:], end_e[:], tiles_e[:], ALU.subtract))
            ch.link(dve.tensor_tensor(inc[:], inc[:], tot[:], ALU.subtract))
            ch.link(dve.scalar_tensor_tensor(tot[:], start_e[:].unsqueeze(2).to_broadcast([P, E, NT]), float(P),
                                             inc[:], ALU.mult, ALU.add))
            ch.link(dve.tensor_tensor(wk[3][:], pf_ps[:, 0].rearrange("p (t e) -> p t e", e=E),
                                      tot[:].rearrange("p e t -> p t e"), ALU.add))
            for n in range(2):
                ch.link(dve.tensor_tensor(wk[0][:], oh[n][:], wk[3][:], ALU.mult))
                ch.link(dve.tensor_reduce(slot_f[:, n], wk[0][:], AX_X, ALU.add))
            ch.link(dve.tensor_copy(t["slots"][:], slot_f[:]))
            dve.tensor_scalar(a_i[:], t["slots"][:].bitcast(I32), 7, None, ALU.logical_shift_right)
            ch.link(dve.tensor_scalar(b_i[:], t["slots"][:].bitcast(I32), P - 1, None, ALU.bitwise_and))
            dve.tensor_copy(a_f[:], a_i[:])
            ch.link(dve.tensor_copy(b_f[:], b_i[:]))

            def onehots(i, j, first):
                tt = 2 * i + j
                if not first:
                    dve.wait_ge(onehot_used, tt - 1)
                for c in range(2):
                    dve.tensor_scalar(ohb[:, j, c], iota_b[:], b_f[:, c, ds(tt, 1)], None, ALU.is_equal)
                    dve.tensor_scalar(oha[:, j, c, 0], iota_ab[:], a_f[:, c, ds(tt, 1)], col_f[:], ALU.is_equal, ALU.mult)
                    ins = dve.tensor_scalar(oha[:, j, c, 1], iota_ab[:], a_f[:, c, ds(tt, 1)], iota_t[:, ds(tt, 1)],
                                            ALU.is_equal, ALU.mult)
                ins.then_inc(onehot_ready, 1)

            onehots(0, 0, True)
            onehots(0, 1, True)
            with dve.Fori(1, NT // 2) as i:
                onehots(i, 0, False)
                onehots(i, 1, False)

            dve.wait_ge(gap_exp, 1)
            ch.link(dve.tensor_scalar(den[:], dexp[:], 1.0, None, ALU.add))
            ch.link(dve.reciprocal(t["wts"][:, 0], den[:]))
            dve.tensor_tensor(t["wts"][:, 1], t["wts"][:, 0], dexp[:], ALU.mult)
            ch.link(dve.tensor_tensor(cmp_e[:], end_e[0:1].unsqueeze(1).to_broadcast([1, T, E]),
                                      iota_a[0:1].unsqueeze(2).to_broadcast([1, T, E]), ALU.is_le))
            ch.link(dve.tensor_reduce(texp_f[:], cmp_e[:], AX_X, ALU.add))
            dve.tensor_scalar(t["tile_expert"][:], texp_f[:], float(E - 1), None, ALU.min)
            dve.wait_ge(onehot_used, NT)
            ch.link(dve.tensor_copy(tokf[:], lg_ps[:, 0, T:2 * T]))
            dve.scalar_tensor_tensor(t["token_of_slot"][:], tokf[:], float(P), lg_ps[:, 0, 0:T],
                                     ALU.mult, ALU.add).then_inc(routed, 1)
            dve.wait_ge(routed, 1)


def experts(nc, t, xn_dram, y_dram, raw_loads):
    T = t["tiles"]
    D = xn_dram.shape[1]
    KD = D // P
    H = t["H"]
    KH = H // P
    WD = KD * H
    E = t["E"]
    RING = 4

    with ExitStack() as ctx:
        def sem(name):
            return ctx.enter_context(nc.semaphore(name))

        def tile(name, shape, dt=F32):
            return ctx.enter_context(nc.sbuf_tensor(name, shape, dt))

        idx = [tile(f"idx{n}", [P, 1], U32) for n in range(RING)]
        xg = [tile(f"xg{n}", [P, D]) for n in range(RING)]
        x_hi = tile("x_hi", [P, 2, D], F32R)
        x_lo = tile("x_lo", [P, 2, D], F32R)
        relu = tile("relu", [P, 2, H])
        h2 = tile("h2", [P, 2, H])
        h_hi = tile("h_hi", [P, 2, H], F32R)
        h_lo = tile("h_lo", [P, 2, H], F32R)
        y_sb = tile("y_sb", [P, RING, D])
        spare = tile("spare_2", [1, 1])
        minus_half = tile("minus_half_2", [1, 1])
        x_ps = ctx.enter_context(nc.psum_tensor("x_ps", [P, 2, 512], F32))
        h_ps = ctx.enter_context(nc.psum_tensor("h_ps", [P, 2, 512], F32))
        hT_ps = ctx.enter_context(nc.psum_tensor("hT_ps", [P, 2, 512], F32))
        y_ps = ctx.enter_context(nc.psum_tensor("y_ps", [P, 2, 512], F32))

        raw_in = t["raw_in"]
        idx_ready = sem("idx_ready")
        gathered = [sem(f"gathered{n}") for n in range(RING)]
        x_turned, h_done, h_turned, y_done = sem("x_turned"), sem("h_done"), sem("h_turned"), sem("y_done")
        x_hi_ready, relu_ready, h_hi_ready = sem("x_hi_ready"), sem("relu_ready"), sem("h_hi_ready")
        x_lo_ready, h2_ready, h_lo_ready, y_copied = sem("x_lo_ready"), sem("h2_ready"), sem("h_lo_ready"), sem("y_copied")
        y_stored = [sem(f"y_stored{n}") for n in range(RING)]
        ident, w_hi, w_lo = t["ident"], t["w_hi"], t["w_lo"]
        block = ctx.enter_context(nc.Block())
        TURNS = T // RING
        assert T % RING == 0


        @block.gpsimd
        def _(pool):
            def step(a, n, i):
                if a is not n:
                    pool.wait_ge(gathered[n], 16 * i)
                    pool.wait_ge(x_turned, a - RING + 1)
                pool.tensor_copy(idx[n][:], t["token_of_slot"][:, ds(a, 1)]).then_inc(idx_ready, 1)
                pool.wait_ge(idx_ready, a + 1)
                pool.tensor_tensor(spare[:], minus_half[:], minus_half[:], ALU.add)
                pool.indirect_dma_start(xg[n][:], None, xn_dram,
                                        bass.IndirectOffsetOnAxis(ap=idx[n][:], axis=0)).then_inc(gathered[n], 16)

            pool.memset(minus_half[:], -0.5)
            for n in range(RING):
                step(n, n, 0)
            with pool.Fori(1, TURNS) as i:
                for n in range(RING):
                    step(RING * i + n, n, i)

        @block.tensor
        def _(pe):
            def turn_x(a, n, i):
                pe.wait_ge(gathered[n % RING], 16 * (i + n // RING + 1))
                if not (isinstance(a, int) and a < 2):
                    pe.wait_ge(x_lo_ready, a - 1)
                for k in range(KD):
                    tr = pe.transpose(x_ps[:, n % 2, k * P:(k + 1) * P], xg[n % RING][:, k * P:(k + 1) * P], ident[:])
                tr.then_inc(x_turned, 1)

            def expert_of(a):
                return pe.value_load(t["tile_expert"][0:1, ds(a, 1)], min_val=0, max_val=E - 1)

            def first_product(a, n):
                e = expert_of(a)
                pe.wait_ge(x_lo_ready, a + 1)
                if not (isinstance(a, int) and a < 2):
                    pe.wait_ge(h2_ready, a - 1)
                for k in range(KD):
                    at = ds(e * (2 * WD) + k * H, H)
                    xs = slice(k * P, (k + 1) * P)
                    out = h_ps[:, n % 2, 0:H]
                    pe.matmul(out, x_hi[:, n % 2, xs], w_hi[:, at], start=(k == 0), stop=False)
                    pe.matmul(out, x_hi[:, n % 2, xs], w_lo[:, at], start=False, stop=False)
                    mm = pe.matmul(out, x_lo[:, n % 2, xs], w_hi[:, at], start=False, stop=(k == KD - 1))
                mm.then_inc(h_done, 1)

            def turn_h(a, n):
                pe.wait_ge(h2_ready, a + 1)
                if not (isinstance(a, int) and a < 2):
                    pe.wait_ge(h_lo_ready, a - 1)
                for k in range(KH):
                    tr = pe.transpose(hT_ps[:, n % 2, k * P:(k + 1) * P], h2[:, n % 2, k * P:(k + 1) * P], ident[:])
                tr.then_inc(h_turned, 1)

            def second_product(a, n):
                e = expert_of(a)
                pe.wait_ge(h_lo_ready, a + 1)
                if not (isinstance(a, int) and a < 2):
                    pe.wait_ge(y_copied, a - 1)
                for k in range(KH):
                    at = ds(e * (2 * WD) + WD + k * D, D)
                    hs = slice(k * P, (k + 1) * P)
                    out = y_ps[:, n % 2, 0:D]
                    pe.matmul(out, h_hi[:, n % 2, hs], w_hi[:, at], start=(k == 0), stop=False)
                    pe.matmul(out, h_hi[:, n % 2, hs], w_lo[:, at], start=False, stop=False)
                    mm = pe.matmul(out, h_lo[:, n % 2, hs], w_hi[:, at], start=False, stop=(k == KH - 1))
                mm.then_inc(y_done, 1)

            def step(a, n, i):
                if not (isinstance(a, int) and a + 2 >= T):
                    turn_x(a + 2, n + 2, i)
                turn_h(a, n)
                if not (isinstance(a, int) and a + 1 >= T):
                    first_product(a + 1, n + 1)
                second_product(a, n)

            turn_x(0, 0, 0)
            turn_x(1, 1, 0)
            first_product(0, 0)
            for n in range(RING):
                step(n, n, 0)
            with pe.Fori(1, TURNS - 1) as i:
                for n in range(RING):
                    step(RING * i + n, n, i)
            for n in range(RING):
                step(T - RING + n, n, TURNS - 1)

        @block.scalar
        def _(act):
            def high_x(a, n):
                act.wait_ge(x_turned, a + 1)
                if not (isinstance(a, int) and a < 2):
                    act.wait_ge(h_done, a - 1)
                act.activation(x_hi[:, n % 2], x_ps[:, n % 2, 0:D], ACT.Copy).then_inc(x_hi_ready, 1)

            def relu_h(a, n):
                act.wait_ge(h_done, a + 1)
                if not (isinstance(a, int) and a < 2):
                    act.wait_ge(h2_ready, a - 1)
                act.activation(relu[:, n % 2], h_ps[:, n % 2, 0:H], ACT.Relu).then_inc(relu_ready, 1)

            def high_h(a, n):
                act.wait_ge(h_turned, a + 1)
                if not (isinstance(a, int) and a < 2):
                    act.wait_ge(y_done, a - 1)
                act.activation(h_hi[:, n % 2], hT_ps[:, n % 2, 0:H], ACT.Copy).then_inc(h_hi_ready, 1)

            def step(a, n):
                if not (isinstance(a, int) and a + 2 >= T):
                    high_x(a + 2, n + 2)
                high_h(a, n)
                if not (isinstance(a, int) and a + 1 >= T):
                    relu_h(a + 1, n + 1)

            high_x(0, 0)
            high_x(1, 1)
            relu_h(0, 0)
            for n in range(RING):
                step(n, n)
            with act.Fori(1, TURNS - 1) as i:
                for n in range(RING):
                    step(RING * i + n, n)
            for n in range(RING):
                step(T - RING + n, n)

        @block.vector
        def _(dve):
            def low_x(a, n):
                dve.wait_ge(x_hi_ready, a + 1)
                if not (isinstance(a, int) and a < 2):
                    dve.wait_ge(h_done, a - 1)
                dve.tensor_tensor(x_lo[:, n % 2], x_ps[:, n % 2, 0:D], x_hi[:, n % 2].bitcast(F32),
                                  ALU.subtract).then_inc(x_lo_ready, 1)

            def square(a, n):
                dve.wait_ge(relu_ready, a + 1)
                if not (isinstance(a, int) and a < 2):
                    dve.wait_ge(h_turned, a - 1)
                dve.tensor_tensor(h2[:, n % 2], h_ps[:, n % 2, 0:H], relu[:, n % 2], ALU.mult).then_inc(h2_ready, 1)

            def low_h(a, n):
                dve.wait_ge(h_hi_ready, a + 1)
                if not (isinstance(a, int) and a < 2):
                    dve.wait_ge(y_done, a - 1)
                dve.tensor_tensor(h_lo[:, n % 2], hT_ps[:, n % 2, 0:H], h_hi[:, n % 2].bitcast(F32),
                                  ALU.subtract).then_inc(h_lo_ready, 1)

            def copy_y(a, n, i):
                dve.wait_ge(y_done, a + 1)
                if not (isinstance(i, int) and i == 0):
                    dve.wait_ge(y_stored[n], 16 * i)
                dve.tensor_copy(y_sb[:, n], y_ps[:, n % 2, 0:D]).then_inc(y_copied, 1)

            def step(a, n, i):
                if not (isinstance(a, int) and a + 2 >= T):
                    low_x(a + 2, n + 2)
                low_h(a, n)
                if not (isinstance(a, int) and a + 1 >= T):
                    square(a + 1, n + 1)
                copy_y(a, n, i)

            low_x(0, 0)
            low_x(1, 1)
            square(0, 0)
            for n in range(RING):
                step(n, n, 0)
            with dve.Fori(1, TURNS - 1) as i:
                for n in range(RING):
                    step(RING * i + n, n, i)
            for n in range(RING):
                step(T - RING + n, n, TURNS - 1)

        @block.sync
        def _(sp):
            for dst, src in raw_loads:
                sp.dma_start(dst, src).then_inc(raw_in, 16)

            def store(a, n):
                sp.wait_ge(y_copied, a + 1)
                sp.dma_start(y_dram[ds(a * P, P), :], y_sb[:, n]).then_inc(y_stored[n], 16)

            for n in range(RING):
                store(n, n)
            with sp.Fori(1, TURNS) as i:
                for n in range(RING):
                    store(RING * i + n, n)
            for n in range(RING):
                sp.wait_ge(y_stored[n], 16 * TURNS)
            sp.wait_ge(raw_in, 16 * len(raw_loads))


def weight_plan(D, HID, GHID):
    plan, at = {}, 0
    for name, cols, chunks in (("in", 2 * HID, D // P), ("gates", 2 * HID, HID // P), ("out", D, HID // P),
                               ("grow", 2 * GHID, D // P), ("shrink", D, GHID // P)):
        plan[name] = (at, cols, chunks)
        at += cols * chunks
    return plan, at


def prepare_weights(nc, t):
    plan, total = t["plan"], t["plan_columns"]
    raw, w_hi, w_lo, ident = t["raw"], t["wa_hi"], t["wa_lo"], t["ident"]
    BANKS, PER = 4, 512 // P
    blocks = []
    for name, (at, cols, chunks) in plan.items():
        rows_in = chunks * P
        for k in range(chunks):
            for m in range(cols // P):
                blocks.append(at + m * rows_in + k * P)
    assert len(blocks) * P == total and len(blocks) % PER == 0
    batches = len(blocks) // PER

    with ExitStack() as ctx:
        w_ps = ctx.enter_context(nc.psum_tensor("w_ps", [P, BANKS, 512], F32))
        turned = ctx.enter_context(nc.semaphore("w_turned"))
        hi_done = ctx.enter_context(nc.semaphore("w_hi_done"))
        lo_done = ctx.enter_context(nc.semaphore("w_lo_done"))
        rate = ctx.enter_context(nc.semaphore("rate"))
        absf = ctx.enter_context(nc.sbuf_tensor("absf", [P, 3], F32))
        ex = ctx.enter_context(nc.sbuf_tensor("ex", [P, 3], F32))
        z = ctx.enter_context(nc.sbuf_tensor("z", [P, 3], F32))
        z2 = ctx.enter_context(nc.sbuf_tensor("z2", [P, 3], F32))
        poly = ctx.enter_context(nc.sbuf_tensor("poly", [P, 3], F32))
        chain = ctx.enter_context(nc.semaphore("dve_chain_2b"))
        block = ctx.enter_context(nc.Block())

        @block.tensor
        def _(pe):
            for n in range(batches):
                if n >= BANKS:
                    pe.wait_ge(lo_done, n - BANKS + 1)
                for q in range(PER):
                    at = blocks[n * PER + q]
                    tr = pe.transpose(w_ps[:, n % BANKS, q * P:(q + 1) * P], raw[:, at:at + P], ident[:])
                tr.then_inc(turned, 1)

        @block.scalar
        def _(act):
            act.activation(absf[:], t["forget_base"][:], ACT.Abs).then_inc(rate, 1)
            act.wait_ge(rate, 1)
            act.activation(ex[:], absf[:], ACT.Exp, scale=-1.0).then_inc(rate, 1)
            for n in range(batches):
                act.wait_ge(turned, n + 1)
                act.activation(w_hi[:, n * 512:(n + 1) * 512], w_ps[:, n % BANKS], ACT.Copy).then_inc(hi_done, 1)

        @block.vector
        def _(dve):
            ch = Chain(dve, chain)
            dve.wait_ge(rate, 2)
            ch.link(dve.tensor_scalar(z[:], ex[:], 2.0, None, ALU.add))
            ch.link(dve.reciprocal(z2[:], z[:]))
            ch.link(dve.tensor_tensor(z[:], ex[:], z2[:], ALU.mult))
            ch.link(dve.tensor_tensor(z2[:], z[:], z[:], ALU.mult))
            ch.link(dve.tensor_scalar(poly[:], z2[:], 1.0 / 17, 1.0 / 15, ALU.mult, ALU.add))
            for odd in (13, 11, 9, 7, 5, 3, 1):
                ch.link(dve.tensor_tensor(poly[:], poly[:], z2[:], ALU.mult))
                ch.link(dve.tensor_scalar(poly[:], poly[:], 1.0 / odd, None, ALU.add))
            ch.link(dve.tensor_tensor(poly[:], poly[:], z[:], ALU.mult))
            ch.link(dve.tensor_scalar(z[:], t["forget_base"][:], 0.0, None, ALU.max))
            ch.link(dve.scalar_tensor_tensor(poly[:], poly[:], 2.0, z[:], ALU.mult, ALU.add))
            ch.link(dve.tensor_scalar(t["log_rate"][:], poly[:], ALPHA_LOG_SCALE, None, ALU.mult))
            for n in range(batches):
                dve.wait_ge(hi_done, n + 1)
                at = slice(n * 512, (n + 1) * 512)
                dve.tensor_tensor(w_lo[:, at], w_ps[:, n % BANKS], w_hi[:, at].bitcast(F32),
                                  ALU.subtract).then_inc(lo_done, 1)
            dve.wait_ge(lo_done, batches)


def recurrent_and_mix(nc, t, x, xn_dram, y_dram, out, blocks_per_batch):
    N, D = x.shape
    B = GROUP * P
    NB = N // B
    plan = t["plan"]
    KD = D // P
    KV = plan["gates"][2]
    KG = plan["shrink"][2]
    HALO = 3
    assert blocks_per_batch == 2

    def rows(dram, b):
        v = dram.rearrange("(b q p) d -> b p q d", q=GROUP, p=P)
        return v[b] if isinstance(b, int) else v[ds(b, 1)].rearrange("o p q d -> (o p) q d")

    def room(eng, sem, value):
        if not isinstance(value, int) or value > 0:
            eng.wait_ge(sem, value)

    def real(b):
        return not isinstance(b, int) or 0 <= b < NB

    with ExitStack() as ctx:
        def sem(name):
            return ctx.enter_context(nc.semaphore(name))

        def tile(name, shape, dt=F32):
            return ctx.enter_context(nc.sbuf_tensor(name, shape, dt))

        xn_t = tile("xn_t", [P, 2, GROUP, D])
        scaled = tile("scaled", [P, GROUP, D])
        xT_hi = tile("xT_hi", [P, KD, B], F32R)
        xT_lo = tile("xT_lo", [P, KD, B], F32R)
        x2T_hi = tile("x2T_hi", [P, KD, B], F32R)
        x2T_lo = tile("x2T_lo", [P, KD, B], F32R)
        vraw = tile("vraw", [P, KV, HALO + B])
        vc = tile("vc", [P, KV, B])
        v_hi = tile("v_hi", [P, KV, B], F32R)
        v_lo = tile("v_lo", [P, KV, B], F32R)
        gate = tile("gate", [P, 2, KV, B])
        sigf = tile("sigf", [P, KV, B])
        alpha = tile("alpha", [P, KV, B])
        beta_h = tile("beta_h", [P, KV, B])
        inj = tile("inj", [P, KV, B])
        gh_hi = tile("gh_hi", [P, KV, B], F32R)
        gh_lo = tile("gh_lo", [P, KV, B], F32R)
        x2 = tile("x2", [P, GROUP, D])
        gelu2 = tile("gelu2", [P, 2, B])
        gv = tile("gv", [P, 2, B])
        gv_hi = tile("gv_hi", [P, KG, B], F32R)
        gv_lo = tile("gv_lo", [P, KG, B], F32R)
        ya = tile("ya", [P, GROUP, D])
        yb = tile("yb", [P, GROUP, D])
        mix = tile("mix", [P, GROUP, D])
        x_t = tile("x_t", [P, GROUP, D])
        hlast = tile("hlast", [P, KV])
        n2 = tile("n2", [P, GROUP])
        r2 = tile("r2", [P, GROUP])
        minus_half = tile("minus_half", [P, GROUP])
        beta_eps = tile("beta_eps", [P, 1])
        yidx = tile("yidx", [P, 2, GROUP], U32)
        spare = tile("spare_3", [1, 1])

        A_ps = ctx.enter_context(nc.psum_tensor("A_ps", [P, 4, 512], F32))
        T_ps = ctx.enter_context(nc.psum_tensor("T_ps", [P, KD, 512], F32))
        O_ps = ctx.enter_context(nc.psum_tensor("O_ps", [P, 2, 512], F32))

        const_ready = sem("const_ready")
        xn_in = [sem(f"xn_in{n}") for n in range(2)]
        x_in = sem("x_in_3")
        y_in = [sem(f"y_in{n}") for n in range(2)]
        yidx_ready = sem("yidx_ready")
        out_stored = sem("out_stored")
        x_turned, in_done, g_done, hawk_done = sem("x_turned_3"), sem("in_done"), sem("g_done"), sem("hawk_done")
        x2_turned, grow_done, mlp_done = sem("x2_turned"), sem("grow_done"), sem("mlp_done")
        x_hi_ready, v_copied, gate_done, v_hi_ready = sem("x_hi_ready_3"), sem("v_copied"), sem("gate_done"), sem("v_hi_ready")
        alpha_ready, a2_ready, beta_ready, sig_done = sem("alpha_ready"), sem("a2_ready"), sem("beta_ready"), sem("sig_done")
        sg_ready, gh_hi_ready, n2_ready = sem("sg_ready"), sem("gh_hi_ready"), sem("n2_ready")
        x2_hi_ready, gelu2_done, gv_hi_ready = sem("x2_hi_ready"), sem("gelu2_done"), sem("gv_hi_ready")
        xr_ready, x_lo_ready, conv_done, v_lo_ready = sem("xr_ready"), sem("x_lo_ready_3"), sem("conv_done"), sem("v_lo_ready")
        om_ready, scan_done, gh_ready, gh_lo_ready = sem("om_ready"), sem("scan_done"), sem("gh_ready"), sem("gh_lo_ready")
        moe_ready, mlp_added, hawk_added, x2r_ready = sem("moe_ready"), sem("mlp_added"), sem("hawk_added"), sem("x2r_ready")
        x2_lo_ready, gv_ready, gv_lo_ready = sem("x2_lo_ready"), sem("gv_ready"), sem("gv_lo_ready")
        dve_chain = sem("dve_chain_3")
        xg1_ready, xg_ready, r2_ready = sem("xg1_ready"), sem("xg_ready"), sem("r2_ready")
        gated, out_mult, out_done = sem("gated"), sem("out_mult"), sem("out_done")

        w_hi, w_lo, ident = t["wa_hi"], t["wa_lo"], t["ident"]
        block = ctx.enter_context(nc.Block())

        def run(eng, period, chain=None):
            period(0, 0)
            period(1, 1)
            n0 = chain.n if chain else 0
            period(2, 0)
            period(3, 1)
            per_turn = chain.n - n0 if chain else 0
            with eng.Fori(2, NB // 2 - 1) as i:
                if chain:
                    chain.repeat(i, 2, per_turn)
                period(2 * i, 0)
                period(2 * i + 1, 1)
            if chain:
                chain.end_turn(NB // 2 - 3, per_turn)
            for p in range(NB - 2, NB + 2):
                period(p, p % 2)

        @block.sync
        def _(sp):
            def load_xn(b, par):
                if real(b):
                    room(sp, hawk_added, 2 * (b - 1))
                    turn = b // 2 if isinstance(b, int) else None
                    sp.dma_start(xn_t[:, par], rows(xn_dram, b)).then_inc(xn_in[par], 16)

            def period(p, par):
                if real(p - 2):
                    room(sp, out_done, p - 2)
                    sp.dma_start(x_t[:], rows(x, p - 2)).then_inc(x_in, 16)
                    sp.wait_ge(out_done, p - 1)
                    sp.dma_start(rows(out, p - 2), mix[:]).then_inc(out_stored, 16)
                load_xn(p + 1, 1 - par)

            load_xn(0, 0)
            run(sp, period)
            sp.wait_ge(out_stored, 16 * NB)

        @block.tensor
        def _(pe):
            def product(out, lhs_hi, lhs_lo, rhs_hi, rhs_lo, first, last):
                pe.matmul(out, lhs_hi, rhs_hi, start=first, stop=False)
                pe.matmul(out, lhs_hi, rhs_lo, start=False, stop=False)
                return pe.matmul(out, lhs_lo, rhs_hi, start=False, stop=last)

            def channels(name, m, bank, a_hi, a_lo):
                at, cols, chunks = plan[name]
                for k in range(chunks):
                    w = slice(at + k * cols + m * P, at + k * cols + (m + 1) * P)
                    mm = product(A_ps[:, bank], w_hi[:, w], w_lo[:, w], a_hi[:, k], a_lo[:, k], k == 0, k == chunks - 1)
                return mm

            def tokens(name, q, a_hi, a_lo):
                at, cols, chunks = plan[name]
                for k in range(chunks):
                    w = slice(at + k * cols, at + (k + 1) * cols)
                    a = slice(q * P, (q + 1) * P)
                    mm = product(O_ps[:, q // 2, (q % 2) * D:(q % 2 + 1) * D], a_hi[:, k, a], a_lo[:, k, a],
                                 w_hi[:, w], w_lo[:, w], k == 0, k == chunks - 1)
                return mm

            def turn(src, done):
                for k in range(KD):
                    for q in range(GROUP):
                        tr = pe.transpose(T_ps[:, k, q * P:(q + 1) * P], src[:, q, k * P:(k + 1) * P], ident[:])
                tr.then_inc(done, 1)

            def turn_x(b):
                if real(b):
                    pe.wait_ge(xr_ready, b + 1)
                    room(pe, x2_lo_ready, b - 1)
                    room(pe, x_lo_ready, b)
                    turn(scaled, x_turned)

            def s1(b):
                if not real(b):
                    return
                pe.wait_ge(x_lo_ready, b + 1)
                room(pe, sig_done, 2 * KV * b)
                for n in range(2 * KV):
                    if n < 4:
                        room(pe, (gelu2_done, gv_ready)[n % 2], KG * (b - 2) + 3 + n // 2)
                    else:
                        pe.wait_ge(v_copied, KV * b + n - 3)
                    m = (n + KV) % (2 * KV)
                    channels("in", m, n % 4, xT_hi, xT_lo).then_inc(in_done, 1)

            def s2(b, ms):
                if not real(b):
                    return
                for m in ms:
                    if m == 0:
                        pe.wait_ge(v_lo_ready, KV * (b + 1))
                    if m == 0:
                        pe.wait_ge(v_copied, KV * b + 3)
                    elif m < 4:
                        pe.wait_ge(gate_done, KV * b + m)
                    else:
                        pe.wait_ge(sig_done, 2 * KV * b + m - 3)
                    channels("gates", m, (m + 2) % 4, v_hi, v_lo).then_inc(g_done, 1)

            def s3(b):
                if not real(b):
                    return
                pe.wait_ge(gh_lo_ready, KV * (b + 1))
                for q in range(GROUP):
                    if q % 2 == 0:
                        room(pe, mlp_added, 2 * (b - 1) + q // 2 + 1)
                    mm = tokens("out", q, gh_hi, gh_lo)
                    if q % 2:
                        mm.then_inc(hawk_done, 1)

            def s4(b):
                if real(b):
                    pe.wait_ge(x2r_ready, b + 1)
                    room(pe, x_lo_ready, min(b + 2, NB) if isinstance(b, int) else b + 2)
                    turn(scaled, x2_turned)

            def s5(b, cs):
                if not real(b):
                    return
                pe.wait_ge(x2_lo_ready, b + 1)
                for c in cs:
                    for half in range(2):
                        n = 2 * c + half
                        if c < 2:
                            if real(b + 1):
                                pe.wait_ge(sig_done, 2 * KV * (b + 1) + n + 3)
                            else:
                                pe.wait_ge((gelu2_done, gv_ready)[half], KG * (b - 1) + 3 + c)
                        else:
                            pe.wait_ge((gelu2_done, gv_ready)[half], KG * b + c - 1)
                        channels("grow", c + half * KG, n % 4, x2T_hi, x2T_lo).then_inc(grow_done, 1)

            def s6(b):
                if not real(b):
                    return
                pe.wait_ge(gv_lo_ready, KG * (b + 1))
                for q in range(GROUP):
                    if q % 2 == 0:
                        pe.wait_ge(hawk_added, 2 * b + q // 2 + 1)
                    mm = tokens("shrink", q, gv_hi, gv_lo)
                    if q % 2:
                        mm.then_inc(mlp_done, 1)

            def period(p, par):
                s1(p)
                s6(p - 2)
                s2(p, range(0, 4))
                s3(p - 1)
                s2(p, range(4, 2 * KV))
                s4(p - 1)
                s5(p - 1, (0, 1))
                turn_x(p + 1)
                s5(p - 1, (2, 3))

            turn_x(0)
            run(pe, period)

        @block.scalar
        def _(act):
            def high_x(b):
                if real(b):
                    act.wait_ge(x_turned, b + 1)
                    room(act, in_done, 2 * KV * b)
                    for k in range(KD):
                        ins = act.activation(xT_hi[:, k], T_ps[:, k], ACT.Copy, scale=t["gamma1"][:, k:k + 1])
                    ins.then_inc(x_hi_ready, 1)

            def period(p, par):
                b = p
                if real(b):
                    for c in range(KV):
                        act.wait_ge(in_done, 2 * KV * b + c + 1)
                        room(act, conv_done, KV * (b - 1) + c + 1)
                        act.activation(vraw[:, c, HALO:], A_ps[:, c % 4], ACT.Copy).then_inc(v_copied, 1)
                    for c in range(KV):
                        act.wait_ge(in_done, 2 * KV * b + KV + c + 1)
                        room(act, gh_ready, KV * (b - 2) + c + 1)
                        act.activation(gate[:, par, c], A_ps[:, (KV + c) % 4], ACT.Gelu).then_inc(gate_done, 1)
                b = p - 1
                if real(b):
                    for c in range(KV):
                        act.wait_ge(sig_done, 2 * KV * b + c + 1)
                        room(act, scan_done, KV * (b - 1) + c + 1)
                        act.activation(alpha[:, c], sigf[:, c], ACT.Exp,
                                       scale=t["log_rate"][:, c:c + 1]).then_inc(alpha_ready, 1)
                    for c in range(KV):
                        act.wait_ge(alpha_ready, KV * b + c + 1)
                        room(act, gh_lo_ready, KV * (b - 1) + c + 1)
                        act.activation(beta_h[:, c], alpha[:, c], ACT.Square).then_inc(a2_ready, 1)
                if real(p):
                    for c in range(KV):
                        act.wait_ge(conv_done, KV * p + c + 1)
                        room(act, g_done, 2 * KV * p)
                        act.activation(v_hi[:, c], vc[:, c], ACT.Copy).then_inc(v_hi_ready, 1)
                if real(b):
                    for c in range(KV):
                        act.wait_ge(om_ready, KV * b + c + 1)
                        act.activation(beta_h[:, c], beta_h[:, c], ACT.Sqrt, bias=beta_eps[:]).then_inc(beta_ready, 1)
                if real(p - 2):
                    act.wait_ge(moe_ready, p - 1)
                    room(act, out_stored, 16 * (p - 2))
                    act.activation(mix[:], ya[:], ACT.Sigmoid).then_inc(sg_ready, 1)

                def gates(ms):
                    for m in ms:
                        act.wait_ge(g_done, 2 * KV * p + m + 1)
                        dst = sigf[:, m] if m < KV else inj[:, m - KV]
                        if m < KV:
                            room(act, alpha_ready, KV * p)
                        else:
                            room(act, scan_done, KV * (p - 1) + m - KV + 1)
                        act.activation(dst, A_ps[:, (m + 2) % 4], ACT.Sigmoid,
                                       bias=t["b_gates"][:, m:m + 1]).then_inc(sig_done, 1)

                if real(p):
                    gates(range(0, KV))
                if real(b):
                    for c in range(KV):
                        act.wait_ge(gh_ready, KV * b + c + 1)
                        room(act, hawk_done, 2 * b)
                        act.activation(gh_hi[:, c], beta_h[:, c], ACT.Copy).then_inc(gh_hi_ready, 1)
                if real(p):
                    gates(range(KV, 2 * KV))
                if real(b):
                    act.wait_ge(hawk_added, 2 * b + 2)
                    act.wait_ge(x_turned, min(b + 2, NB) if isinstance(b, int) else b + 2)
                    for q in range(GROUP):
                        ins = act.activation(scaled[:, q], x2[:, q], ACT.Square, accum_out=n2[:, q:q + 1])
                    ins.then_inc(n2_ready, 1)
                    act.wait_ge(x2_turned, b + 1)
                    room(act, grow_done, 2 * KG * b)
                    for k in range(KD):
                        ins = act.activation(x2T_hi[:, k], T_ps[:, k], ACT.Copy, scale=t["gamma2"][:, k:k + 1])
                    ins.then_inc(x2_hi_ready, 1)

                    def gelu(c):
                        act.wait_ge(grow_done, 2 * KG * b + 2 * c + 1)
                        room(act, gv_ready, KG * b + c - 1)
                        act.activation(gelu2[:, c % 2], A_ps[:, 2 * c % 4], ACT.Gelu).then_inc(gelu2_done, 1)

                    def high(c):
                        act.wait_ge(gv_ready, KG * b + c + 1)
                        room(act, mlp_done, 2 * b)
                        act.activation(gv_hi[:, c], gv[:, c % 2], ACT.Copy).then_inc(gv_hi_ready, 1)

                    gelu(0)
                    gelu(1)
                    high_x(p + 1)
                    high(0)
                    gelu(2)
                    high(1)
                    gelu(3)
                    high(2)
                    high(3)
                else:
                    high_x(p + 1)

            act.wait_ge(const_ready, 1)
            high_x(0)
            run(act, period)

        @block.vector
        def _(dve):
            ch = Chain(dve, dve_chain)
            dve.memset(beta_eps[:], BETA_EPS)
            dve.memset(minus_half[:], -0.5)
            ch.link(dve.memset(vraw[:, :, 0:HALO], 0.0))
            dve.memset(hlast[:], 0.0).then_inc(const_ready, 1)

            def landed(b, par):
                dve.wait_ge(xn_in[par], 16 * (b // 2 + 1) if isinstance(b, int) else (b - par) * 8 + 16)

            def scale_x(b, par):
                if real(b):
                    landed(b, par)
                    room(dve, x2_turned, b - 1)
                    room(dve, x_turned, b)
                    for q in range(GROUP):
                        ins = dve.tensor_scalar(scaled[:, q], xn_t[:, par, q], t["r1"][:, ds(GROUP * b + q, 1)],
                                                None, ALU.mult)
                    ins.then_inc(xr_ready, 1)

            def low(b, gamma, hi, lo, hi_ready, lo_ready, used, value):
                dve.wait_ge(hi_ready, b + 1)
                room(dve, used, value)
                for k in range(KD):
                    ins = dve.scalar_tensor_tensor(lo[:, k], T_ps[:, k], gamma[:, k:k + 1], hi[:, k].bitcast(F32),
                                                   ALU.mult, ALU.subtract)
                ins.then_inc(lo_ready, 1)

            def low_x(b):
                if real(b):
                    low(b, t["gamma1"], xT_hi, xT_lo, x_hi_ready, x_lo_ready, in_done, 2 * KV * b)

            def convolve(b, par):
                for c in range(KV):
                    dve.wait_ge(v_copied, KV * b + c + 1)
                    room(dve, xg1_ready, KV * (b - 1) + c + 1)
                    room(dve, v_lo_ready, KV * (b - 1) + c + 1)
                    ch.link(dve.tensor_scalar(vc[:, c], vraw[:, c, 0:B], t["conv_w"][:, c, 0:1], t["conv_b"][:, c:c + 1],
                                              ALU.mult, ALU.add))
                    for k in range(1, HALO + 1):
                        ch.link(dve.scalar_tensor_tensor(vc[:, c], vraw[:, c, k:k + B], t["conv_w"][:, c, k:k + 1],
                                                         vc[:, c], ALU.mult, ALU.add))
                    if par == 0:
                        ins = dve.tensor_copy(vraw[:, c, 0:HALO], vraw[:, c, B:B + HALO])
                    else:
                        ins = dve.memset(vraw[:, c, 0:HALO], 0.0)
                    ins.then_inc(conv_done, 1)

            def mixture(b):
                for n in range(2):
                    dve.wait_ge(y_in[n], 16 * GROUP * (b + 1))
                for q in range(GROUP):
                    ins = dve.tensor_scalar(ya[:, q], ya[:, q], t["wts"][:, 0, ds(GROUP * b + q, 1)], None, ALU.mult)
                ch.link(ins)
                for q in range(GROUP):
                    ins = dve.scalar_tensor_tensor(ya[:, q], yb[:, q], t["wts"][:, 1, ds(GROUP * b + q, 1)], ya[:, q],
                                                   ALU.mult, ALU.add)
                ins.then_inc(moe_ready, 1)

            def period(p, par):
                b = p - 1
                if real(p):
                    convolve(p, par)
                if real(b):
                    for c in range(KV):
                        dve.wait_ge(a2_ready, KV * b + c + 1)
                        dve.tensor_scalar(beta_h[:, c], beta_h[:, c], -1.0, 1.0, ALU.mult, ALU.add).then_inc(om_ready, 1)
                if real(p):
                    for c in range(KV):
                        dve.wait_ge(v_hi_ready, KV * p + c + 1)
                        room(dve, g_done, 2 * KV * p)
                        dve.tensor_tensor(v_lo[:, c], vc[:, c], v_hi[:, c].bitcast(F32),
                                          ALU.subtract).then_inc(v_lo_ready, 1)
                if real(p - 2):
                    mixture(p - 2)
                    for n in range(2):
                        dve.wait_ge(mlp_done, 2 * (p - 2) + n + 1)
                        xs = x2[:, 2 * n:2 * n + 2].rearrange("p q d -> p (q d)")
                        dve.tensor_tensor(xs, O_ps[:, n], xs, ALU.add).then_inc(mlp_added, 1)
                if real(b):
                    bpar = 1 - par
                    for c in range(KV):
                        dve.wait_ge(xg_ready, KV * b + c + 1)
                        dve.tensor_tensor_scan(beta_h[:, c], alpha[:, c], inj[:, c],
                                               0.0 if bpar == 0 else hlast[:, c:c + 1],
                                               ALU.mult, ALU.add).then_inc(scan_done, 1)
                    for c in range(KV):
                        dve.wait_ge(scan_done, KV * b + c + 1)
                        if bpar == 0:
                            ch.link(dve.tensor_copy(hlast[:, c:c + 1], beta_h[:, c, B - 1:B]))
                        dve.wait_ge(gate_done, KV * b + c + 1)
                        dve.tensor_tensor(beta_h[:, c], gate[:, bpar, c], beta_h[:, c], ALU.mult).then_inc(gh_ready, 1)
                    for c in range(KV):
                        dve.wait_ge(gh_hi_ready, KV * b + c + 1)
                        room(dve, hawk_done, 2 * b)
                        dve.tensor_tensor(gh_lo[:, c], beta_h[:, c], gh_hi[:, c].bitcast(F32),
                                          ALU.subtract).then_inc(gh_lo_ready, 1)
                    room(dve, out_mult, b)
                    for n in range(2):
                        dve.wait_ge(hawk_done, 2 * b + n + 1)
                        dve.tensor_tensor(x2[:, 2 * n:2 * n + 2].rearrange("p q d -> p (q d)"), O_ps[:, n],
                                          xn_t[:, bpar, 2 * n:2 * n + 2].rearrange("p q d -> p (q d)"),
                                          ALU.add).then_inc(hawk_added, 1)
                    dve.wait_ge(r2_ready, b + 1)
                    for q in range(GROUP):
                        ins = dve.tensor_scalar(scaled[:, q], x2[:, q], r2[:, q:q + 1], float(D) ** 0.5, ALU.mult, ALU.mult)
                    ins.then_inc(x2r_ready, 1)
                    low(b, t["gamma2"], x2T_hi, x2T_lo, x2_hi_ready, x2_lo_ready, grow_done, 2 * KG * b)

                    def multiply(c):
                        dve.wait_ge(gelu2_done, KG * b + c + 1)
                        dve.wait_ge(grow_done, 2 * KG * b + 2 * c + 2)
                        room(dve, gv_lo_ready, KG * b + c - 1)
                        dve.tensor_tensor(gv[:, c % 2], A_ps[:, (2 * c + 1) % 4], gelu2[:, c % 2],
                                          ALU.mult).then_inc(gv_ready, 1)

                    def low_gv(c):
                        dve.wait_ge(gv_hi_ready, KG * b + c + 1)
                        room(dve, mlp_done, 2 * b)
                        dve.tensor_tensor(gv_lo[:, c], gv[:, c % 2], gv_hi[:, c].bitcast(F32),
                                          ALU.subtract).then_inc(gv_lo_ready, 1)

                    scale_x(p + 1, 1 - par)
                    multiply(0)
                    multiply(1)
                    low_x(p + 1)
                    low_gv(0)
                    multiply(2)
                    low_gv(1)
                    multiply(3)
                    low_gv(2)
                    low_gv(3)
                else:
                    scale_x(p + 1, 1 - par)
                    low_x(p + 1)

            scale_x(0, 0)
            low_x(0)
            run(dve, period, ch)

        @block.gpsimd
        def _(pool):
            def period(p, par):
                b = p - 1
                if real(b):
                    for c in range(KV):
                        pool.wait_ge(xg1_ready, KV * b + c + 1)
                        pool.wait_ge(beta_ready, KV * b + c + 1)
                        pool.tensor_tensor(inj[:, c], inj[:, c], beta_h[:, c], ALU.mult).then_inc(xg_ready, 1)
                if real(p - 2):
                    e = p - 2
                    pool.wait_ge(sg_ready, e + 1)
                    pool.tensor_tensor(mix[:], mix[:], ya[:], ALU.mult).then_inc(gated, 1)
                    pool.wait_ge(gated, e + 1)
                    pool.wait_ge(mlp_added, 2 * e + 2)
                    pool.tensor_tensor(mix[:], mix[:], x2[:], ALU.mult).then_inc(out_mult, 1)
                    pool.wait_ge(out_mult, e + 1)
                    pool.wait_ge(x_in, 16 * (e + 1))
                    pool.tensor_tensor(mix[:], mix[:], x_t[:], ALU.add).then_inc(out_done, 1)
                if real(b):
                    pool.wait_ge(n2_ready, b + 1)
                    pool.tensor_tensor(r2[:], n2[:], minus_half[:], ALU.pow).then_inc(r2_ready, 1)
                if real(p):
                    for c in range(KV):
                        pool.wait_ge(sig_done, 2 * KV * p + KV + c + 1)
                        pool.tensor_tensor(inj[:, c], inj[:, c], vc[:, c], ALU.mult).then_inc(xg1_ready, 1)
                if real(b):
                    room(pool, moe_ready, b)
                    room(pool, gated, b)
                    for n in range(2):
                        room(pool, y_in[n], 16 * GROUP * b)
                    pool.tensor_copy(yidx[:], t["slots"][:, :, ds(GROUP * b, GROUP)]).then_inc(yidx_ready, 1)
                    pool.wait_ge(yidx_ready, b + 1)
                    pool.tensor_tensor(spare[:], minus_half[0:1, 0:1], minus_half[0:1, 0:1], ALU.add)
                    for n, dst in enumerate((ya, yb)):
                        for q in range(GROUP):
                            pool.indirect_dma_start(dst[:, q], None, y_dram,
                                                    bass.IndirectOffsetOnAxis(ap=yidx[:, n, q:q + 1], axis=0)
                                                    ).then_inc(y_in[n], 16)

            pool.wait_ge(const_ready, 1)
            run(pool, period)


def build(nc, x, gamma1, W_in, conv_w, conv_b, W_gates, b_gates, forget_base, W_out, gamma2, W_grow, W_shrink,
          router_w, w1, w2, out, xn_dram, y_dram):
    batches, S, D = x.shape
    N = batches * S
    E, _, H = w1.shape
    HID, GHID = W_out.shape[1], W_shrink.shape[1]
    T = 2 * N // P + E
    T = -(-T // 4) * 4
    xf = x.rearrange("b s d -> (b s) d")
    of = out.rearrange("b s d -> (b s) d")
    plan, columns = weight_plan(D, HID, GHID)

    with ExitStack() as ctx:
        def keep(name, shape, dt=F32):
            return ctx.enter_context(nc.sbuf_tensor(name, shape, dt))

        t = dict(tiles=T, E=E, H=H, plan=plan, plan_columns=columns)
        t["ident"] = keep("ident", [P, P])
        t["r1"] = keep("r1", [P, N // P])
        t["slots"] = keep("slots", [P, 2, N // P], U32)
        t["wts"] = keep("wts", [P, 2, N // P])
        t["token_of_slot"] = keep("token_of_slot", [P, T], U32)
        t["tile_expert"] = keep("tile_expert", [1, T], I32)
        t["conv_w"] = keep("conv_w_sb", [P, HID // P, 4])
        t["conv_b"] = keep("conv_b_sb", [P, HID // P])
        t["b_gates"] = keep("b_gates_sb", [P, 2 * HID // P])
        t["forget_base"] = keep("forget_sb", [P, HID // P])
        t["log_rate"] = keep("log_rate", [P, HID // P])
        t["gamma1"] = keep("gamma1_sb", [P, D // P])
        t["gamma2"] = keep("gamma2_sb", [P, D // P])
        t["raw_in"] = ctx.enter_context(nc.semaphore("raw_in"))
        ctx.enter_context(nc.allow_non_contiguous_dma(reason="small vectors, one element a partition"))

        with ExitStack() as moe:
            WE = E * 2 * (D // P) * H
            t["w_hi"] = moe.enter_context(nc.sbuf_tensor("w_hi", [P, WE], F32R))
            t["w_lo"] = moe.enter_context(nc.sbuf_tensor("w_lo", [P, WE], F32R))
            normalise_and_route(nc, None, t, xf, router_w, w1, w2, xn_dram)
            t["raw"] = moe.enter_context(nc.sbuf_tensor("raw", [P, columns], F32))
            loads = []
            for name, w in (("in", W_in), ("gates", W_gates), ("out", W_out), ("grow", W_grow), ("shrink", W_shrink)):
                at, cols, chunks = plan[name]
                loads.append((t["raw"][:, at:at + cols * chunks].rearrange("p (m k) -> p m k", k=chunks * P),
                              w.rearrange("(m p) k -> p m k", p=P)))
            loads.append((t["conv_w"][:], conv_w.rearrange("(c p) o k -> p c (o k)", p=P)))
            for name, v in (("conv_b", conv_b), ("b_gates", b_gates), ("forget_base", forget_base),
                            ("gamma1", gamma1), ("gamma2", gamma2)):
                loads.append((t[name][:], v.rearrange("(c p) -> p c", p=P)))
            experts(nc, t, xn_dram, y_dram, loads)
        t["wa_hi"] = keep("wa_hi", [P, columns], F32R)
        t["wa_lo"] = keep("wa_lo", [P, columns], F32R)
        prepare_weights(nc, t)
        recurrent_and_mix(nc, t, xf, xn_dram, y_dram, of, S // (GROUP * P))


INPUTS = ["L0_attn_x", "L0_attn_gamma1", "L0_attn_W_in", "L0_attn_conv_w", "L0_attn_conv_b", "L0_attn_W_gates",
          "L0_attn_b_gates", "L0_attn_forget_base", "L0_attn_W_out", "L0_attn_gamma2", "L0_attn_W_grow",
          "L0_attn_W_shrink", "L0_ffn_router_w", "L0_ffn_w1", "L0_ffn_w2"]


def kernel(**inputs):
    import numpy as np
    import concourse.bacc as bacc
    from concourse.bass_utils import run_bass_kernel_spmd

    nc = bacc.Bacc("TRN2", target_bir_lowering=False, num_devices=1)
    arrays, args = {}, []
    for name in INPUTS:
        a = np.ascontiguousarray(inputs[name])
        arrays[f"in_{name}"] = a
        args.append(nc.dram_tensor(f"in_{name}", a.shape, mybir.dt.from_np(a.dtype), kind="ExternalInput").ap())
    b, s, d = inputs["L0_attn_x"].shape
    e = inputs["L0_ffn_w1"].shape[0]
    tiles = -(-(2 * b * s // P + e) // 4) * 4
    out = nc.dram_tensor("out_0", (b, s, d), F32, kind="ExternalOutput").ap()
    xn_dram = nc.dram_tensor("xn_rows", (b * s, d), F32, kind="Internal").ap()
    y_dram = nc.dram_tensor("y_rows", (tiles * P, d), F32, kind="Internal").ap()
    build(nc, *args, out, xn_dram, y_dram)
    r = run_bass_kernel_spmd(nc, [arrays], core_ids=[0])
    return r.results[0]["out_0"]
```

```python
from contextlib import ExitStack

import concourse.bass as bass
from concourse import mybir

P = 128
F32 = mybir.dt.float32
F32R = mybir.dt.float32r
BF16 = mybir.dt.bfloat16
F16 = mybir.dt.float16
U32 = mybir.dt.uint32
I32 = mybir.dt.int32
ALU = mybir.AluOpType
ACT = mybir.ActivationFunctionType
AX_X = mybir.AxisListType.X
ds = bass.ds

LN_EPS = 1e-5
BETA_EPS = 1e-6
ALPHA_LOG_SCALE = -8.0
BIG = 3.0e38
CODES = 2048
GROUP = 4
RING = 8


class Chain:

    def __init__(self, eng, sem):
        self.eng, self.sem, self.n, self.base = eng, sem, 0, None

    def link(self, ins):
        ins.then_inc(self.sem, 1)
        self.n += 1
        self.eng.wait_ge(self.sem, self.n if self.base is None else self.base + self.n)

    def repeat(self, i, first, per_turn):
        self.base = (i - first) * per_turn
        self.mark = self.n

    def end_turn(self, turns, per_turn):
        assert self.n - self.mark == per_turn, (self.n - self.mark, per_turn)
        self.base = None
        self.n = self.mark + turns * per_turn


def normalise_and_route(nc, sb, t, x, router_w, w1, w2, xn_dram):
    N, D = x.shape
    E, _, H = w1.shape
    NT = N // P
    NG = NT // GROUP
    KD, KH = D // P, H // P
    GC = GROUP * P
    AHEAD = 4
    T = t["tiles"]
    WD = KD * H

    x_v = x.rearrange("(g q p) d -> g p q d", q=GROUP, p=P)
    xn_v = xn_dram.rearrange("(g q p) d -> g p q d", q=GROUP, p=P)
    w1_v = w1.rearrange("e (k p) h -> e p k h", p=P)
    w2_v = w2.rearrange("e (k p) d -> e p k d", p=P)

    with ExitStack() as ctx:
        def sem(name):
            return ctx.enter_context(nc.semaphore(name))

        def tile(name, shape, dt=F32):
            return ctx.enter_context(nc.sbuf_tensor(name, shape, dt))

        xa = tile("xa", [P, AHEAD, GROUP, D])
        xn = tile("xn", [P, 2, GROUP, D])
        xT = tile("xT", [P, 2, KD, GC])
        stage1 = tile("stage1", [P, WD])
        stage2 = tile("stage2", [P, WD])
        bn6 = tile("bn6", [P, 2, GROUP, 6])
        mv = tile("mv", [P, 2, GROUP, 2])
        std = tile("std", [P, 2, GROUP])
        sv = tile("sv", [P, 2, GROUP])
        rstd = tile("rstd", [P, 2, GROUP])
        isv = tile("isv", [P, 2, GROUP])
        rrow = tile("rrow", [E, D])
        rT = tile("rT", [P, KD, E])
        eps = tile("eps", [P, 1])
        logit = tile("logit", [P, NT, E])
        row_f = tile("row_f", [P, P])
        col_f = tile("col_f", [P, 1])
        tri = tile("tri", [P, P], BF16)
        ones = tile("ones", [P, P], BF16)
        iota_e = tile("iota_e", [P, E])
        iota_cap = tile("iota_cap", [P, NT])
        iota_a = tile("iota_a", [P, T])
        code = tile("code", [P, NT])
        one = tile("one", [P, 1])
        minus_b = tile("minus_b", [P, NT])
        offset2 = tile("offset2", [P, 2, 2, P])
        wk = [tile(f"wk{n}", [P, NT, E]) for n in range(4)]
        oh = [tile(f"oh{n}", [P, NT, E]) for n in range(2)]
        chosen = tile("chosen", [P, NT, E], BF16)
        best = [tile(f"best{n}", [P, NT]) for n in range(2)]
        ix = tile("ix", [P, NT])
        tot = tile("tot", [P, E, NT])
        inc = tile("inc", [P, E, NT])
        zeros_nt = tile("zeros_nt", [P, NT])
        tiles_e = tile("tiles_e", [P, E])
        end_e = tile("end_e", [P, E])
        start_e = tile("start_e", [P, E])
        slot_f = tile("slot_f", [P, 2, NT])
        a_i = tile("a_i", [P, 2, NT], I32)
        b_i = tile("b_i", [P, 2, NT], I32)
        a_f = tile("a_f", [P, 2, NT])
        b_f = tile("b_f", [P, 2, NT])
        ohb = tile("ohb", [P, 2, 2, 2, P], F16)
        oha = tile("oha", [P, 2, 2, 2, T], F16)
        texp_f = tile("texp_f", [1, T])
        ended = xa[0:1].rearrange("p a q d -> p (a q d)")[:, 0:T * E].rearrange("p (t e) -> p t e", e=E)
        flat = [w[:].rearrange("p t e -> p (t e)") for w in wk]
        coded, token = (flat[n][:, 0:2 * T].rearrange("p (h t) -> p h t", h=2) for n in (0, 1))
        positive, negative = flat[2][:, 0:T], flat[3][:, 0:T]
        dexp = tile("dexp", [P, NT])
        den = tile("den", [P, NT])
        spare = tile("spare_1", [1, 1])

        x_in = [sem(f"x_in{j}") for j in range(AHEAD)]
        small_in = sem("small_in")
        w1_in, w2_in = sem("w1_in"), sem("w2_in")
        w_hi, w_lo = sem("w_hi"), sem("w_lo")
        pool_const, dve_const = sem("pool_const"), sem("dve_const")
        stats_ready, std_ready = sem("stats_ready"), sem("std_ready")
        xn_ready = sem("xn_ready")
        xn_stored = [sem(f"xn_stored{j}") for j in range(2)]
        xT_psum, xT_ready = sem("xT_psum"), sem("xT_ready")
        rT_psum, rT_ready = sem("rT_psum"), sem("rT_ready")
        lg_psum, logits_copied = sem("lg_psum"), sem("logits_copied")
        chosen_ready, prefix_psum = sem("chosen_ready"), sem("prefix_psum")
        score_gap, gap_exp = sem("score_gap"), sem("gap_exp")
        slots_split, slot_onehot, squared = sem("slots_split"), sem("slot_onehot"), sem("squared")
        tile_onehot, onehot_used = sem("tile_onehot"), sem("onehot_used")
        dve_chain = sem("dve_chain_1")
        routed = sem("routed")

        xT_ps = ctx.enter_context(nc.psum_tensor("xT_ps", [P, 2, KD, GC], F32))
        lg_ps = ctx.enter_context(nc.psum_tensor("lg_ps", [P, 2, GC], F32))
        pf_ps = ctx.enter_context(nc.psum_tensor("pf_ps", [P, 2, NT * E], F32))

        ident = t["ident"]
        block = ctx.enter_context(nc.Block())
        TURNS = NG // AHEAD
        assert NG % AHEAD == 0 and 2 * E == NG and N == 4 * CODES

        @block.sync
        def _(sp):
            def group_of(view, g):
                return view[g] if isinstance(g, int) else view[ds(g, 1)].rearrange("o p q d -> (o p) q d")

            def expert_in(e):
                for src, dst, landed in ((w1_v, stage1, w1_in), (w2_v, stage2, w2_in)):
                    if not (isinstance(e, int) and e == 0):
                        sp.wait_ge(w_lo, 2 * e)
                    s = group_of(src, e)
                    sp.dma_start(dst[:].rearrange("p (k n) -> p k n", k=s.shape[1]), s).then_inc(landed, 16)

            def turn(i, last):
                for j in range(AHEAD):
                    g = AHEAD * i + j
                    sp.wait_ge(xn_ready, g + 1)
                    if not last:
                        sp.dma_start(xa[:, j], group_of(x_v, g + AHEAD)).then_inc(x_in[j], 16)
                    sp.dma_start(group_of(xn_v, g), xn[:, j % 2]).then_inc(xn_stored[j % 2], 16)
                    if j % 2:
                        if not (last and j == AHEAD - 1):
                            expert_in((AHEAD * i + j) // 2 + 1 if isinstance(i, int) else (AHEAD // 2) * i + j // 2 + 1)

            for j in range(AHEAD):
                sp.dma_start(xa[:, j], group_of(x_v, j)).then_inc(x_in[j], 16)
                if j == 1:
                    sp.dma_start(rrow[:], router_w).then_inc(small_in, 16)
                    expert_in(0)
            turn(0, False)
            with sp.Fori(1, TURNS - 1) as i:
                turn(i, False)
            turn(TURNS - 1, True)
            for j in range(2):
                sp.wait_ge(xn_stored[j], 8 * NG)

        @block.gpsimd
        def _(pool):
            pool.iota(row_f[:], pattern=[[1, P]], base=0, channel_multiplier=0, allow_small_or_imprecise_dtypes=True)
            pool.iota(col_f[:], pattern=[[0, 1]], base=0, channel_multiplier=1, allow_small_or_imprecise_dtypes=True)
            pool.iota(iota_e[:], pattern=[[1, E]], base=-E, channel_multiplier=0, allow_small_or_imprecise_dtypes=True)
            pool.iota(iota_cap[:], pattern=[[P, NT]], base=0, channel_multiplier=0, allow_small_or_imprecise_dtypes=True)
            pool.iota(iota_a[:], pattern=[[1, T]], base=0, channel_multiplier=0, allow_small_or_imprecise_dtypes=True)
            pool.iota(code[:], pattern=[[0, NT * P // CODES], [P, CODES // P]], base=1, channel_multiplier=1,
                      allow_small_or_imprecise_dtypes=True)
            pool.memset(ones[:], 1.0)
            pool.memset(zeros_nt[:], 0.0)
            pool.memset(one[:], 1.0)
            pool.memset(eps[:], LN_EPS).then_inc(pool_const, 1)

            def split_low(i, first):
                for n, (stage, landed) in enumerate(((stage1, w1_in), (stage2, w2_in))):
                    pool.wait_ge(w_hi, 2 * i + n + 1)
                    at = ds(i * 2 * WD + n * WD, WD)
                    pool.tensor_tensor(t["w_lo"][:, at], stage[:], t["w_hi"][:, at].bitcast(F32),
                                       ALU.subtract).then_inc(w_lo, 1)

            with pool.Fori(0, E) as i:
                split_low(i, False)

        @block.scalar
        def _(act):
            def deviations(g, j, first):
                act.wait_ge(stats_ready, g + 1)
                if not first:
                    act.wait_ge(xn_ready, g - 1)
                act.activation(std[:, j], mv[:, j, :, 1], ACT.Sqrt, bias=eps[:])
                act.activation(sv[:, j], mv[:, j, :, 1], ACT.Sqrt).then_inc(std_ready, 1)

            def turn(i, first, last):
                for j in range(AHEAD):
                    g = AHEAD * i + j
                    if not (last and j == AHEAD - 1):
                        deviations(g + 1, (j + 1) % 2, first and j == 0)
                    act.wait_ge(xT_psum, g + 1)
                    if not (first and j < 2):
                        act.wait_ge(lg_psum, g - 1)
                    for k in range(KD):
                        ev = act.activation(xT[:, j % 2, k], xT_ps[:, j % 2, k], ACT.Copy)
                    ev.then_inc(xT_ready, 1)
                    e = AHEAD // 2 * i + j // 2
                    stage, landed = ((stage1, w1_in), (stage2, w2_in))[j % 2]
                    act.wait_ge(landed, 16 * (e + 1))
                    act.activation(t["w_hi"][:, ds(e * 2 * WD + j % 2 * WD, WD)], stage[:], ACT.Copy).then_inc(w_hi, 1)

            act.wait_ge(pool_const, 1)
            deviations(0, 0, True)
            turn(0, True, False)
            with act.Fori(1, TURNS - 1) as i:
                turn(i, False, False)
            turn(TURNS - 1, False, True)
            act.wait_ge(score_gap, 1)
            act.activation(dexp[:], ix[:], ACT.Exp).then_inc(gap_exp, 1)

            def slots_onehot(i, j, first):
                if not first:
                    act.wait_ge(onehot_used, 2 * i + j - 1)
                for n in range(2):
                    ins = act.activation(offset2[:, j, n], row_f[:], ACT.Square,
                                         bias=minus_b[:, ds(2 * (2 * i + j) + n, 1)])
                ins.then_inc(squared, 1)
                act.wait_ge(squared, 2 * i + j + 1)
                act.activation(ohb[:, j, 1], offset2[:, j], ACT.Relu, scale=-1.0, bias=one[:]).then_inc(slot_onehot, 1)

            act.wait_ge(slots_split, 1)
            slots_onehot(0, 0, True)
            slots_onehot(0, 1, True)
            with act.Fori(1, NT // 4) as i:
                slots_onehot(i, 0, False)
                slots_onehot(i, 1, False)

        @block.tensor
        def _(pe):
            pe.wait_ge(small_in, 16)
            pe.wait_ge(dve_const, 1)
            for k in range(KD):
                tr = pe.transpose(pf_ps[:, 0, k * E:(k + 1) * E], rrow[:, k * P:(k + 1) * P], ident[0:E, 0:E])
            tr.then_inc(rT_psum, 1)

            def transposes(g, j, first):
                pe.wait_ge(xn_ready, g + 1)
                if not first:
                    pe.wait_ge(xT_ready, g - 1)
                for k in range(KD):
                    for q in range(GROUP):
                        tr = pe.transpose(xT_ps[:, j, k, q * P:(q + 1) * P], xn[:, j, q, k * P:(k + 1) * P], ident[:])
                tr.then_inc(xT_psum, 1)

            def logits(g, j, copied):
                pe.wait_ge(xT_ready, g + 1)
                if copied is not None:
                    pe.wait_ge(logits_copied, copied)
                for q in range(GROUP):
                    for k in range(KD):
                        mm = pe.matmul(lg_ps[:, j, q * E:(q + 1) * E], xT[:, j, k, q * P:(q + 1) * P], rT[:, k],
                                       start=(k == 0), stop=(k == KD - 1))
                mm.then_inc(lg_psum, 1)

            def pair(i, first):
                transposes(2 * i, 0, False)
                logits(2 * i - 1, 1, None if first else 2 * i - 2)
                transposes(2 * i + 1, 1, False)
                logits(2 * i, 0, 2 * i - 1)

            transposes(0, 0, True)
            pe.wait_ge(rT_ready, 1)
            transposes(1, 1, True)
            logits(0, 0, None)
            pair(1, True)
            with pe.Fori(2, NG // 2) as i:
                pair(i, False)
            logits(NG - 1, 1, NG - 2)

            pe.wait_ge(chosen_ready, 1)
            pe.matmul(pf_ps[:, 0], tri[:], chosen[:], start=True, stop=True)
            pe.matmul(pf_ps[:, 1], ones[:], chosen[:], start=True, stop=True).then_inc(prefix_psum, 1)

            def place(i, j, half, first, last):
                pe.wait_ge(slot_onehot, 2 * i + j + 1)
                pe.wait_ge(tile_onehot, 2 * i + j + 1)
                for n in range(2):
                    for c in range(2):
                        mm = pe.matmul(lg_ps[:, half, 0:T], ohb[:, j, c, n], oha[:, j, c, n],
                                       start=first and n == 0 and c == 0, stop=last and n == 1 and c == 1)
                mm.then_inc(onehot_used, 1)

            for half in range(2):
                start, end = half * NT // 8, (half + 1) * NT // 8
                place(start, 0, half, True, False)
                place(start, 1, half, False, False)
                with pe.Fori(start + 1, end - 1) as i:
                    place(i, 0, half, False, False)
                    place(i, 1, half, False, False)
                place(end - 1, 0, half, False, False)
                place(end - 1, 1, half, False, True)

        @block.vector
        def _(dve):
            ch = Chain(dve, dve_chain)
            dve.wait_ge(pool_const, 1)
            dve.tensor_scalar(ident[:], row_f[:], col_f[:], None, ALU.is_equal).then_inc(dve_const, 1)
            dve.tensor_scalar(tri[:], row_f[:], col_f[:], None, ALU.is_gt)

            def stats(g, i, a):
                dve.wait_ge(x_in[a], 16 * (i + 1))
                j = a % 2
                for q in range(GROUP):
                    ins = dve.bn_stats(bn6[:, j, q], xa[:, a, q])
                ch.link(ins)
                dve.memset(spare[:], 0.0)
                for q in range(GROUP):
                    ins = dve.bn_aggr(mv[:, j, q], bn6[:, j, q])
                ins.then_inc(stats_ready, 1)

            def finish(g, i, a, first):
                j = a % 2
                dve.wait_ge(std_ready, g + 1)
                dve.reciprocal(rstd[:, j], std[:, j])
                ch.link(dve.reciprocal(isv[:, j], sv[:, j]))
                dve.tensor_tensor(t["r1"][:, ds(g * GROUP, GROUP)], std[:, j], isv[:, j], ALU.mult)
                if not first:
                    dve.wait_ge(xn_stored[j], 16 * (AHEAD // 2 * i + a // 2))
                    dve.wait_ge(xT_psum, g - 1)
                for q in range(GROUP):
                    ins = dve.tensor_scalar(xn[:, j, q], xa[:, a, q], mv[:, j, q, 0:1], rstd[:, j, q:q + 1],
                                            ALU.subtract, ALU.mult)
                ins.then_inc(xn_ready, 1)

            def keep_logits(g, j):
                dve.wait_ge(lg_psum, g + 1)
                dve.tensor_copy(logit[:, ds(g * GROUP, GROUP)],
                                lg_ps[:, j, 0:GROUP * E].rearrange("p (q e) -> p q e", q=GROUP)).then_inc(logits_copied, 1)

            stats(0, 0, 0)
            stats(1, 0, 1)
            finish(0, 0, 0, True)
            dve.wait_ge(rT_psum, 1)
            dve.tensor_copy(rT[:], pf_ps[:, 0, 0:KD * E].rearrange("p (k e) -> p k e", k=KD)).then_inc(rT_ready, 1)

            def turn(i, first):
                for j in range(AHEAD):
                    g = AHEAD * i + j
                    ahead, wrap = (j + 2) % AHEAD, (j + 2) // AHEAD
                    stats(g + 2, i + wrap, ahead)
                    finish(g + 1, i + (j + 1) // AHEAD, (j + 1) % AHEAD, first and j == 0)
                    if not (first and j == 0):
                        keep_logits(g - 1, (j + 1) % 2)

            n0 = ch.n
            turn(0, True)
            per_turn = ch.n - n0
            with dve.Fori(1, TURNS - 1) as i:
                ch.repeat(i, 1, per_turn)
                turn(i, False)
            ch.end_turn(TURNS - 2, per_turn)
            for g in range(NG - AHEAD, NG - 1):
                if g + 2 < NG:
                    stats(g + 2, TURNS - 1, (g + 2) % AHEAD)
                finish(g + 1, TURNS - 1, (g + 1) % AHEAD, False)
                keep_logits(g - 1, (g + 1) % 2)
            keep_logits(NG - 2, 0)
            keep_logits(NG - 1, 1)
            dve.wait_ge(logits_copied, NG)

            def spread_e(ap):
                return ap.unsqueeze(2).to_broadcast([P, NT, E])

            def spread_t(ap):
                return ap.unsqueeze(1).to_broadcast([P, NT, E])

            score = logit
            for n in range(2):
                ch.link(dve.tensor_reduce(best[n][:], score[:], AX_X, ALU.max))
                ch.link(dve.tensor_tensor(wk[0][:], score[:], spread_e(best[n][:]), ALU.is_equal))
                ch.link(dve.scalar_tensor_tensor(wk[1][:], wk[0][:], float(E), spread_t(iota_e[:]), ALU.mult, ALU.subtract))
                ch.link(dve.tensor_reduce(ix[:], wk[1][:], AX_X, ALU.max))
                ch.link(dve.tensor_tensor(wk[2][:], wk[1][:], spread_e(ix[:]), ALU.is_equal))
                ch.link(dve.tensor_tensor(oh[n][:], wk[2][:], wk[0][:], ALU.mult))
                if n == 0:
                    ch.link(dve.tensor_scalar(wk[1][:], oh[0][:], -0.5, -BIG, ALU.add, ALU.mult))
                    ch.link(dve.tensor_tensor(wk[3][:], logit[:], wk[1][:], ALU.min))
                    score = wk[3]
            dve.tensor_tensor(chosen[:], oh[0][:], oh[1][:], ALU.add).then_inc(chosen_ready, 1)
            dve.tensor_tensor(ix[:], best[1][:], best[0][:], ALU.subtract).then_inc(score_gap, 1)

            dve.wait_ge(prefix_psum, 1)
            ch.link(dve.tensor_copy(tot[:], pf_ps[:, 1].rearrange("p (t e) -> p e t", e=E)))
            for e in range(E):
                ins = dve.tensor_tensor_scan(inc[:, e], tot[:, e], zeros_nt[:], 0.0, ALU.add, ALU.add)
            ch.link(ins)
            ch.link(dve.tensor_tensor(wk[1][:].rearrange("p t e -> p (t e)").rearrange("p (e t) -> p e t", e=E),
                                      inc[:, :, NT - 1:NT].to_broadcast([P, E, NT]),
                                      iota_cap[:].unsqueeze(1).to_broadcast([P, E, NT]), ALU.is_gt))
            ch.link(dve.tensor_reduce(tiles_e[:], wk[1][:].rearrange("p t e -> p (t e)").rearrange("p (e t) -> p e t", e=E),
                                      AX_X, ALU.add))
            ch.link(dve.tensor_tensor_scan(end_e[:], tiles_e[:], zeros_nt[:, 0:E], 0.0, ALU.add, ALU.add))
            ch.link(dve.tensor_tensor(start_e[:], end_e[:], tiles_e[:], ALU.subtract))
            ch.link(dve.tensor_tensor(inc[:], inc[:], tot[:], ALU.subtract))
            ch.link(dve.scalar_tensor_tensor(tot[:], start_e[:].unsqueeze(2).to_broadcast([P, E, NT]), float(P),
                                             inc[:], ALU.mult, ALU.add))
            ch.link(dve.tensor_tensor(wk[3][:], pf_ps[:, 0].rearrange("p (t e) -> p t e", e=E),
                                      tot[:].rearrange("p e t -> p t e"), ALU.add))
            for n in range(2):
                ch.link(dve.tensor_tensor(wk[0][:], oh[n][:], wk[3][:], ALU.mult))
                ch.link(dve.tensor_reduce(slot_f[:, n], wk[0][:], AX_X, ALU.add))
            ch.link(dve.tensor_copy(t["slots"][:], slot_f[:]))
            dve.tensor_scalar(a_i[:], t["slots"][:].bitcast(I32), 7, None, ALU.logical_shift_right)
            ch.link(dve.tensor_scalar(b_i[:], t["slots"][:].bitcast(I32), P - 1, None, ALU.bitwise_and))
            dve.tensor_copy(a_f[:], a_i[:])
            ch.link(dve.tensor_copy(b_f[:], b_i[:]))
            dve.tensor_scalar(minus_b[:], b_f[:, 1], -1.0, None, ALU.mult).then_inc(slots_split, 1)

            for n in range(1, NT * P // CODES, 2):
                at = slice(n * (CODES // P), (n + 1) * (CODES // P))
                ins = dve.tensor_scalar(code[:, at], code[:, at], -1.0, None, ALU.mult)
            ch.link(ins)

            def tiles_onehot(i, j, first):
                if not first:
                    dve.wait_ge(onehot_used, 2 * i + j - 1)
                for n in range(2):
                    tt = 2 * (2 * i + j) + n
                    dve.tensor_scalar(ohb[:, j, 0, n], row_f[:], b_f[:, 0, ds(tt, 1)], None, ALU.is_equal)
                    for c in range(2):
                        ins = dve.tensor_scalar(oha[:, j, c, n], iota_a[:], a_f[:, c, ds(tt, 1)], code[:, ds(tt, 1)],
                                                ALU.is_equal, ALU.mult)
                ins.then_inc(tile_onehot, 1)

            tiles_onehot(0, 0, True)
            tiles_onehot(0, 1, True)
            with dve.Fori(1, NT // 4) as i:
                tiles_onehot(i, 0, False)
                tiles_onehot(i, 1, False)

            dve.wait_ge(gap_exp, 1)
            ch.link(dve.tensor_scalar(den[:], dexp[:], 1.0, None, ALU.add))
            ch.link(dve.reciprocal(t["wts"][:, 0], den[:]))
            dve.tensor_tensor(t["wts"][:, 1], t["wts"][:, 0], dexp[:], ALU.mult)
            ch.link(dve.tensor_tensor(ended, end_e[0:1].unsqueeze(1).to_broadcast([1, T, E]),
                                      iota_a[0:1].unsqueeze(2).to_broadcast([1, T, E]), ALU.is_le))
            ch.link(dve.tensor_reduce(texp_f[:], ended, AX_X, ALU.add))
            dve.tensor_scalar(t["tile_expert"][:], texp_f[:], float(E - 1), float(2 * WD), ALU.min, ALU.mult)
            dve.wait_ge(onehot_used, NT // 2)
            for half in range(2):
                base = half * 2 * CODES
                ch.link(dve.tensor_copy(coded[:, half], lg_ps[:, half, 0:T]))
                dve.tensor_scalar(positive, coded[:, half], 0.0, float(base - 1), ALU.is_gt, ALU.mult)
                dve.tensor_scalar(negative, coded[:, half], 0.0, float(base + CODES - 1), ALU.is_lt, ALU.mult)
                ch.link(dve.scalar_tensor_tensor(token[:, half], coded[:, half], -1.0, coded[:, half], ALU.mult, ALU.max))
                ch.link(dve.tensor_tensor(token[:, half], token[:, half], positive, ALU.add))
                ch.link(dve.tensor_tensor(token[:, half], token[:, half], negative, ALU.add))
            dve.tensor_tensor(t["token_of_slot"][:], token[:, 0], token[:, 1], ALU.add).then_inc(routed, 1)
            dve.wait_ge(routed, 1)


def experts(nc, t, xn_dram, y_dram, raw_loads):
    T = t["tiles"]
    D = xn_dram.shape[1]
    KD = D // P
    H = t["H"]
    KH = H // P
    WD = KD * H
    E = t["E"]

    with ExitStack() as ctx:
        def sem(name):
            return ctx.enter_context(nc.semaphore(name))

        def tile(name, shape, dt=F32):
            return ctx.enter_context(nc.sbuf_tensor(name, shape, dt))

        idx = [tile(f"idx{n}", [P, 1], U32) for n in range(RING)]
        xg = [tile(f"xg{n}", [P, D]) for n in range(RING)]
        x_hi = tile("x_hi", [P, 2, D], F32R)
        x_lo = tile("x_lo", [P, 2, D], F32R)
        relu = tile("relu", [P, 2, H])
        h2 = tile("h2", [P, 2, H])
        h_hi = tile("h_hi", [P, 2, H], F32R)
        h_lo = tile("h_lo", [P, 2, H], F32R)
        y_sb = tile("y_sb", [P, RING, D])
        spare = tile("spare_2", [1, RING])
        minus_half = tile("minus_half_2", [1, 1])
        x_ps = ctx.enter_context(nc.psum_tensor("x_ps", [P, 2, 512], F32))
        h_ps = ctx.enter_context(nc.psum_tensor("h_ps", [P, 2, 512], F32))
        hT_ps = ctx.enter_context(nc.psum_tensor("hT_ps", [P, 2, 512], F32))
        y_ps = ctx.enter_context(nc.psum_tensor("y_ps", [P, 2, 512], F32))

        raw_in = t["raw_in"]
        idx_ready = sem("idx_ready")
        gathered = [sem(f"gathered{n}") for n in range(RING)]
        x_turned, h_done, h_turned, y_done = sem("x_turned"), sem("h_done"), sem("h_turned"), sem("y_done")
        x_hi_ready, relu_ready, h_hi_ready = sem("x_hi_ready"), sem("relu_ready"), sem("h_hi_ready")
        x_lo_ready, h2_ready, h_lo_ready, y_copied = sem("x_lo_ready"), sem("h2_ready"), sem("h_lo_ready"), sem("y_copied")
        y_stored = [sem(f"y_stored{n}") for n in range(RING)]
        ident, w_hi, w_lo = t["ident"], t["w_hi"], t["w_lo"]
        block = ctx.enter_context(nc.Block())
        TURNS = T // RING
        assert T % RING == 0


        @block.gpsimd
        def _(pool):
            def pick(a, n, i):
                if not (isinstance(i, int) and i == 0):
                    pool.wait_ge(gathered[n], 16 * i)
                pool.tensor_copy(idx[n][:], t["token_of_slot"][:, ds(a, 1)]).then_inc(idx_ready, 1)

            def gather(a, n, i):
                if not (isinstance(i, int) and i == 0):
                    pool.wait_ge(x_turned, a - RING + 1)
                pool.wait_ge(idx_ready, a + 1)
                pool.tensor_tensor(spare[:, n:n + 1], minus_half[:], minus_half[:], ALU.add)
                pool.indirect_dma_start(xg[n][:], None, xn_dram,
                                        bass.IndirectOffsetOnAxis(ap=idx[n][:], axis=0)).then_inc(gathered[n], 16)

            pool.memset(minus_half[:], -0.5)
            pick(0, 0, 0)
            for n in range(RING):
                pick(n + 1, (n + 1) % RING, (n + 1) // RING)
                gather(n, n, 0)
            with pool.Fori(1, TURNS - 1) as i:
                for n in range(RING):
                    pick(RING * i + n + 1, (n + 1) % RING, i + (n + 1) // RING)
                    gather(RING * i + n, n, i)
            for n in range(RING):
                if n + 1 < RING:
                    pick(T - RING + n + 1, n + 1, TURNS - 1)
                gather(T - RING + n, n, TURNS - 1)

        @block.tensor
        def _(pe):
            def turn_x(a, n, i):
                pe.wait_ge(gathered[n % RING], 16 * (i + n // RING + 1))
                if not (isinstance(a, int) and a < 2):
                    pe.wait_ge(x_lo_ready, a - 1)
                for k in range(KD):
                    tr = pe.transpose(x_ps[:, n % 2, k * P:(k + 1) * P], xg[n % RING][:, k * P:(k + 1) * P], ident[:])
                tr.then_inc(x_turned, 1)

            def weights_of(a, count):
                _, starts = nc.values_load_multi_w_load_instructions(
                    t["tile_expert"][0:1, ds(a, count)], engines=[mybir.EngineType.PE],
                    min_val=0, max_val=(E - 1) * 2 * WD,
                    skip_runtime_bounds_check_because="block 1 caps the expert at E - 1")
                return starts

            def first_product(a, n, start):
                pe.wait_ge(x_lo_ready, a + 1)
                if not (isinstance(a, int) and a < 2):
                    pe.wait_ge(h2_ready, a - 1)
                for k in range(KD):
                    at = ds(start + k * H, H)
                    xs = slice(k * P, (k + 1) * P)
                    out = h_ps[:, n % 2, 0:H]
                    pe.matmul(out, x_hi[:, n % 2, xs], w_hi[:, at], start=(k == 0), stop=False)
                    pe.matmul(out, x_hi[:, n % 2, xs], w_lo[:, at], start=False, stop=False)
                    mm = pe.matmul(out, x_lo[:, n % 2, xs], w_hi[:, at], start=False, stop=(k == KD - 1))
                mm.then_inc(h_done, 1)

            def turn_h(a, n):
                pe.wait_ge(h2_ready, a + 1)
                if not (isinstance(a, int) and a < 1):
                    pe.wait_ge(h_lo_ready, 2 * a)
                for k in range(KH):
                    part, at = k // (KH // 2), k % (KH // 2) * P
                    tr = pe.transpose(hT_ps[:, part, at:at + P], h2[:, n % 2, k * P:(k + 1) * P], ident[:])
                tr.then_inc(h_turned, 1)

            def second_product(a, n, start):
                if not (isinstance(a, int) and a < 2):
                    pe.wait_ge(y_copied, a - 1)
                for k in range(KH):
                    if k % (KH // 2) == 0:
                        pe.wait_ge(h_lo_ready, 2 * a + k // (KH // 2) + 1)
                    at = ds(start + WD + k * D, D)
                    hs = slice(k * P, (k + 1) * P)
                    out = y_ps[:, n % 2, 0:D]
                    pe.matmul(out, h_hi[:, n % 2, hs], w_hi[:, at], start=(k == 0), stop=False)
                    pe.matmul(out, h_hi[:, n % 2, hs], w_lo[:, at], start=False, stop=False)
                    mm = pe.matmul(out, h_lo[:, n % 2, hs], w_hi[:, at], start=False, stop=(k == KH - 1))
                mm.then_inc(y_done, 1)

            def step(a, n, i, starts):
                last = isinstance(a, int) and a + 1 >= T
                if not (isinstance(a, int) and a + 2 >= T):
                    turn_x(a + 2, n + 2, i)
                turn_h(a, n)
                if not last:
                    first_product(a + 1, n + 1, starts[n + 1])
                second_product(a, n, starts[n])

            turn_x(0, 0, 0)
            turn_x(1, 1, 0)
            starts = weights_of(0, RING + 1)
            first_product(0, 0, starts[0])
            for n in range(RING):
                step(n, n, 0, starts)
            with pe.Fori(1, TURNS - 1) as i:
                starts = weights_of(RING * i, RING + 1)
                for n in range(RING):
                    step(RING * i + n, n, i, starts)
            starts = weights_of(T - RING, RING)
            for n in range(RING):
                step(T - RING + n, n, TURNS - 1, starts)

        @block.scalar
        def _(act):
            def high_x(a, n):
                act.wait_ge(x_turned, a + 1)
                if not (isinstance(a, int) and a < 2):
                    act.wait_ge(h_done, a - 1)
                act.activation(x_hi[:, n % 2], x_ps[:, n % 2, 0:D], ACT.Copy).then_inc(x_hi_ready, 1)

            def relu_h(a, n):
                act.wait_ge(h_done, a + 1)
                if not (isinstance(a, int) and a < 2):
                    act.wait_ge(h2_ready, a - 1)
                act.activation(relu[:, n % 2], h_ps[:, n % 2, 0:H], ACT.Relu).then_inc(relu_ready, 1)

            def high_h(a, n):
                act.wait_ge(h_turned, a + 1)
                if not (isinstance(a, int) and a < 2):
                    act.wait_ge(y_done, a - 1)
                for part, half in enumerate((slice(0, H // 2), slice(H // 2, H))):
                    act.activation(h_hi[:, n % 2, half], hT_ps[:, part, 0:H // 2], ACT.Copy).then_inc(h_hi_ready, 1)

            def step(a, n):
                if not (isinstance(a, int) and a + 2 >= T):
                    high_x(a + 2, n + 2)
                high_h(a, n)
                if not (isinstance(a, int) and a + 1 >= T):
                    relu_h(a + 1, n + 1)

            high_x(0, 0)
            high_x(1, 1)
            relu_h(0, 0)
            for n in range(RING):
                step(n, n)
            with act.Fori(1, TURNS - 1) as i:
                for n in range(RING):
                    step(RING * i + n, n)
            for n in range(RING):
                step(T - RING + n, n)

        @block.vector
        def _(dve):
            def low_x(a, n):
                dve.wait_ge(x_hi_ready, a + 1)
                if not (isinstance(a, int) and a < 2):
                    dve.wait_ge(h_done, a - 1)
                dve.tensor_tensor(x_lo[:, n % 2], x_ps[:, n % 2, 0:D], x_hi[:, n % 2].bitcast(F32),
                                  ALU.subtract).then_inc(x_lo_ready, 1)

            def square(a, n):
                dve.wait_ge(relu_ready, a + 1)
                if not (isinstance(a, int) and a < 2):
                    dve.wait_ge(h_turned, a - 1)
                dve.tensor_tensor(h2[:, n % 2], h_ps[:, n % 2, 0:H], relu[:, n % 2], ALU.mult).then_inc(h2_ready, 1)

            def low_h(a, n):
                if not (isinstance(a, int) and a < 2):
                    dve.wait_ge(y_done, a - 1)
                for part, half in enumerate((slice(0, H // 2), slice(H // 2, H))):
                    dve.wait_ge(h_hi_ready, 2 * a + part + 1)
                    dve.tensor_tensor(h_lo[:, n % 2, half], hT_ps[:, part, 0:H // 2], h_hi[:, n % 2, half].bitcast(F32),
                                      ALU.subtract).then_inc(h_lo_ready, 1)

            def copy_y(a, n, i):
                dve.wait_ge(y_done, a + 1)
                if not (isinstance(i, int) and i == 0):
                    dve.wait_ge(y_stored[n], 16 * i)
                dve.tensor_copy(y_sb[:, n], y_ps[:, n % 2, 0:D]).then_inc(y_copied, 1)

            def step(a, n, i):
                if not (isinstance(a, int) and a + 2 >= T):
                    low_x(a + 2, n + 2)
                low_h(a, n)
                if not (isinstance(a, int) and a + 1 >= T):
                    square(a + 1, n + 1)
                copy_y(a, n, i)

            low_x(0, 0)
            low_x(1, 1)
            square(0, 0)
            for n in range(RING):
                step(n, n, 0)
            with dve.Fori(1, TURNS - 1) as i:
                for n in range(RING):
                    step(RING * i + n, n, i)
            for n in range(RING):
                step(T - RING + n, n, TURNS - 1)

        @block.sync
        def _(sp):
            for dst, src in raw_loads:
                sp.dma_start(dst, src).then_inc(raw_in, 16)

            def store(a, n):
                sp.wait_ge(y_copied, a + 1)
                sp.dma_start(y_dram[ds(a * P, P), :], y_sb[:, n]).then_inc(y_stored[n], 16)

            for n in range(RING):
                store(n, n)
            with sp.Fori(1, TURNS) as i:
                for n in range(RING):
                    store(RING * i + n, n)
            for n in range(RING):
                sp.wait_ge(y_stored[n], 16 * TURNS)
            sp.wait_ge(raw_in, 16 * len(raw_loads))


def weight_plan(D, HID, GHID):
    plan, at = {}, 0
    for name, cols, chunks in (("in", 2 * HID, D // P), ("gates", 2 * HID, HID // P), ("out", D, HID // P),
                               ("grow", 2 * GHID, D // P), ("shrink", D, GHID // P)):
        plan[name] = (at, cols, chunks)
        at += cols * chunks
    return plan, at


def prepare_weights(nc, t):
    plan, total = t["plan"], t["plan_columns"]
    raw, w_hi, w_lo, ident = t["raw"], t["wa_hi"], t["wa_lo"], t["ident"]
    BANKS, PER = 4, 512 // P
    blocks = []
    for name, (at, cols, chunks) in plan.items():
        rows_in = chunks * P
        for k in range(chunks):
            for m in range(cols // P):
                blocks.append(at + m * rows_in + k * P)
    assert len(blocks) * P == total and len(blocks) % PER == 0
    batches = len(blocks) // PER

    with ExitStack() as ctx:
        w_ps = ctx.enter_context(nc.psum_tensor("w_ps", [P, BANKS, 512], F32))
        turned = ctx.enter_context(nc.semaphore("w_turned"))
        hi_done = ctx.enter_context(nc.semaphore("w_hi_done"))
        lo_done = ctx.enter_context(nc.semaphore("w_lo_done"))
        rate = ctx.enter_context(nc.semaphore("rate"))
        absf = ctx.enter_context(nc.sbuf_tensor("absf", [P, 3], F32))
        ex = ctx.enter_context(nc.sbuf_tensor("ex", [P, 3], F32))
        z = ctx.enter_context(nc.sbuf_tensor("z", [P, 3], F32))
        z2 = ctx.enter_context(nc.sbuf_tensor("z2", [P, 3], F32))
        poly = ctx.enter_context(nc.sbuf_tensor("poly", [P, 3], F32))
        chain = ctx.enter_context(nc.semaphore("dve_chain_2b"))
        block = ctx.enter_context(nc.Block())

        @block.tensor
        def _(pe):
            for n in range(batches):
                if n >= BANKS:
                    pe.wait_ge(lo_done, n - BANKS + 1)
                for q in range(PER):
                    at = blocks[n * PER + q]
                    tr = pe.transpose(w_ps[:, n % BANKS, q * P:(q + 1) * P], raw[:, at:at + P], ident[:])
                tr.then_inc(turned, 1)

        @block.scalar
        def _(act):
            act.activation(absf[:], t["forget_base"][:], ACT.Abs).then_inc(rate, 1)
            act.wait_ge(rate, 1)
            act.activation(ex[:], absf[:], ACT.Exp, scale=-1.0).then_inc(rate, 1)
            for n in range(batches):
                act.wait_ge(turned, n + 1)
                act.activation(w_hi[:, n * 512:(n + 1) * 512], w_ps[:, n % BANKS], ACT.Copy).then_inc(hi_done, 1)

        @block.vector
        def _(dve):
            ch = Chain(dve, chain)
            dve.wait_ge(rate, 2)
            ch.link(dve.tensor_scalar(z[:], ex[:], 2.0, None, ALU.add))
            ch.link(dve.reciprocal(z2[:], z[:]))
            ch.link(dve.tensor_tensor(z[:], ex[:], z2[:], ALU.mult))
            ch.link(dve.tensor_tensor(z2[:], z[:], z[:], ALU.mult))
            ch.link(dve.tensor_scalar(poly[:], z2[:], 1.0 / 17, 1.0 / 15, ALU.mult, ALU.add))
            for odd in (13, 11, 9, 7, 5, 3, 1):
                ch.link(dve.tensor_tensor(poly[:], poly[:], z2[:], ALU.mult))
                ch.link(dve.tensor_scalar(poly[:], poly[:], 1.0 / odd, None, ALU.add))
            ch.link(dve.tensor_tensor(poly[:], poly[:], z[:], ALU.mult))
            ch.link(dve.tensor_scalar(z[:], t["forget_base"][:], 0.0, None, ALU.max))
            ch.link(dve.scalar_tensor_tensor(poly[:], poly[:], 2.0, z[:], ALU.mult, ALU.add))
            ch.link(dve.tensor_scalar(t["log_rate"][:], poly[:], ALPHA_LOG_SCALE, None, ALU.mult))
            for n in range(batches):
                dve.wait_ge(hi_done, n + 1)
                at = slice(n * 512, (n + 1) * 512)
                dve.tensor_tensor(w_lo[:, at], w_ps[:, n % BANKS], w_hi[:, at].bitcast(F32),
                                  ALU.subtract).then_inc(lo_done, 1)
            dve.wait_ge(lo_done, batches)


def recurrent_and_mix(nc, t, x, xn_dram, y_dram, out, blocks_per_batch):
    N, D = x.shape
    B = GROUP * P
    NB = N // B
    plan = t["plan"]
    KD = D // P
    KV = plan["gates"][2]
    KG = plan["shrink"][2]
    HALO = 3
    assert blocks_per_batch == 2

    def rows(dram, b):
        v = dram.rearrange("(b q p) d -> b p q d", q=GROUP, p=P)
        return v[b] if isinstance(b, int) else v[ds(b, 1)].rearrange("o p q d -> (o p) q d")

    def room(eng, sem, value):
        if not isinstance(value, int) or value > 0:
            eng.wait_ge(sem, value)

    def real(b):
        return not isinstance(b, int) or 0 <= b < NB

    with ExitStack() as ctx:
        def sem(name):
            return ctx.enter_context(nc.semaphore(name))

        def tile(name, shape, dt=F32):
            return ctx.enter_context(nc.sbuf_tensor(name, shape, dt))

        xn_t = tile("xn_t", [P, GROUP, D])
        scaled = tile("scaled", [P, GROUP, D])
        xT_hi = tile("xT_hi", [P, KD, B], F32R)
        xT_lo = tile("xT_lo", [P, KD, B], F32R)
        x2T_hi = tile("x2T_hi", [P, KD, B], F32R)
        x2T_lo = tile("x2T_lo", [P, KD, B], F32R)
        vraw = tile("vraw", [P, KV, HALO + B])
        vc = tile("vc", [P, KV, B])
        v_hi = tile("v_hi", [P, KV, B], F32R)
        v_lo = tile("v_lo", [P, KV, B], F32R)
        gate = tile("gate", [P, 2, KV, B])
        sigf = tile("sigf", [P, KV, B])
        alpha = tile("alpha", [P, KV, B])
        beta_h = tile("beta_h", [P, KV, B])
        inj = tile("inj", [P, KV, B])
        gh_hi = tile("gh_hi", [P, KV, B], F32R)
        gh_lo = tile("gh_lo", [P, KV, B], F32R)
        x2 = tile("x2", [P, 2, GROUP, D])
        gelu2 = tile("gelu2", [P, 2, B])
        gv = tile("gv", [P, 2, B])
        gv_hi = tile("gv_hi", [P, KG, B], F32R)
        gv_lo = tile("gv_lo", [P, KG, B], F32R)
        ya = tile("ya", [P, GROUP, D])
        yb = tile("yb", [P, GROUP, D])
        mix = tile("mix", [P, GROUP, D])
        x_t = tile("x_t", [P, GROUP, D])
        hlast = tile("hlast", [P, KV])
        n2 = tile("n2", [P, GROUP])
        r2 = tile("r2", [P, GROUP])
        minus_half = tile("minus_half", [P, GROUP])
        beta_eps = tile("beta_eps", [P, 1])
        yidx = tile("yidx", [P, 2, GROUP], U32)
        spare = tile("spare_3", [1, 1])

        A_ps = ctx.enter_context(nc.psum_tensor("A_ps", [P, 4, 512], F32))
        T_ps = ctx.enter_context(nc.psum_tensor("T_ps", [P, KD, 512], F32))
        O_ps = ctx.enter_context(nc.psum_tensor("O_ps", [P, 2, 512], F32))

        const_ready = sem("const_ready")
        xn_in = sem("xn_in")
        x2_in = [sem(f"x2_in{n}") for n in range(2)]
        x_in = sem("x_in_3")
        y_in = [sem(f"y_in{n}") for n in range(2)]
        yidx_ready = sem("yidx_ready")
        out_stored = sem("out_stored")
        x_turned, in_done, g_done, hawk_done = sem("x_turned_3"), sem("in_done"), sem("g_done"), sem("hawk_done")
        x2_turned, grow_done, mlp_done = sem("x2_turned"), sem("grow_done"), sem("mlp_done")
        x_hi_ready, v_copied, gate_done, v_hi_ready = sem("x_hi_ready_3"), sem("v_copied"), sem("gate_done"), sem("v_hi_ready")
        alpha_ready, a2_ready, beta_ready, sig_done = sem("alpha_ready"), sem("a2_ready"), sem("beta_ready"), sem("sig_done")
        sg_ready, gh_hi_ready, n2_ready = sem("sg_ready"), sem("gh_hi_ready"), sem("n2_ready")
        x2_hi_ready, gelu2_done, gv_hi_ready = sem("x2_hi_ready"), sem("gelu2_done"), sem("gv_hi_ready")
        xr_ready, x_lo_ready, conv_done, v_lo_ready = sem("xr_ready"), sem("x_lo_ready_3"), sem("conv_done"), sem("v_lo_ready")
        om_ready, scan_done, gh_ready, gh_lo_ready = sem("om_ready"), sem("scan_done"), sem("gh_ready"), sem("gh_lo_ready")
        moe_ready, mlp_added, hawk_added, x2r_ready = sem("moe_ready"), sem("mlp_added"), sem("hawk_added"), sem("x2r_ready")
        x2_lo_ready, gv_ready, gv_lo_ready = sem("x2_lo_ready"), sem("gv_ready"), sem("gv_lo_ready")
        dve_chain = sem("dve_chain_3")
        xg1_ready, xg_ready, r2_ready = sem("xg1_ready"), sem("xg_ready"), sem("r2_ready")
        gated, out_mult, out_done = sem("gated"), sem("out_mult"), sem("out_done")

        w_hi, w_lo, ident = t["wa_hi"], t["wa_lo"], t["ident"]
        block = ctx.enter_context(nc.Block())

        def run(eng, period, chain=None):
            for p in range(4):
                period(p, p % 2)
            n0 = chain.n if chain else 0
            period(4, 0)
            period(5, 1)
            per_turn = chain.n - n0 if chain else 0
            with eng.Fori(3, NB // 2 - 1) as i:
                if chain:
                    chain.repeat(i, 3, per_turn)
                period(2 * i, 0)
                period(2 * i + 1, 1)
            if chain:
                chain.end_turn(NB // 2 - 4, per_turn)
            for p in range(NB - 2, NB + 3):
                period(p, p % 2)

        @block.sync
        def _(sp):
            def load_xn(b):
                if real(b):
                    room(sp, xr_ready, b)
                    sp.dma_start(xn_t[:], rows(xn_dram, b)).then_inc(xn_in, 16)

            def period(p, par):
                if real(p - 3):
                    room(sp, out_done, p - 3)
                    sp.dma_start(x_t[:], rows(x, p - 3)).then_inc(x_in, 16)
                load_xn(p + 1)
                if real(p - 1):
                    room(sp, out_mult, p - 2)
                    sp.dma_start(x2[:, 1 - par], rows(xn_dram, p - 1)).then_inc(x2_in[1 - par], 16)
                if real(p - 3):
                    sp.wait_ge(out_done, p - 2)
                    sp.dma_start(rows(out, p - 3), mix[:]).then_inc(out_stored, 16)

            load_xn(0)
            run(sp, period)
            sp.wait_ge(out_stored, 16 * NB)

        @block.tensor
        def _(pe):
            def product(out, lhs_hi, lhs_lo, rhs_hi, rhs_lo, first, last):
                pe.matmul(out, lhs_hi, rhs_hi, start=first, stop=False)
                pe.matmul(out, lhs_hi, rhs_lo, start=False, stop=False)
                return pe.matmul(out, lhs_lo, rhs_hi, start=False, stop=last)

            def channels(name, m, bank, a_hi, a_lo):
                at, cols, chunks = plan[name]
                for k in range(chunks):
                    w = slice(at + k * cols + m * P, at + k * cols + (m + 1) * P)
                    mm = product(A_ps[:, bank], w_hi[:, w], w_lo[:, w], a_hi[:, k], a_lo[:, k], k == 0, k == chunks - 1)
                return mm

            def tokens(name, q, a_hi, a_lo):
                at, cols, chunks = plan[name]
                for k in range(chunks):
                    w = slice(at + k * cols, at + (k + 1) * cols)
                    a = slice(q * P, (q + 1) * P)
                    mm = product(O_ps[:, q // 2, (q % 2) * D:(q % 2 + 1) * D], a_hi[:, k, a], a_lo[:, k, a],
                                 w_hi[:, w], w_lo[:, w], k == 0, k == chunks - 1)
                return mm

            def turn(src, done):
                for k in range(KD):
                    for q in range(GROUP):
                        tr = pe.transpose(T_ps[:, k, q * P:(q + 1) * P], src[:, q, k * P:(k + 1) * P], ident[:])
                tr.then_inc(done, 1)

            def turn_x(b):
                if real(b):
                    pe.wait_ge(xr_ready, b + 1)
                    room(pe, x2_lo_ready, b - 2)
                    room(pe, x_lo_ready, b)
                    turn(scaled, x_turned)

            def s1(b, ns):
                if not real(b):
                    return
                for n in ns:
                    if n == 0:
                        pe.wait_ge(x_lo_ready, b + 1)
                    if n < 4:
                        room(pe, sig_done, 2 * KV * (b - 1) + 3 + n)
                    else:
                        pe.wait_ge(v_copied, KV * b + n - 3)
                    channels("in", (n + KV) % (2 * KV), n % 4, xT_hi, xT_lo).then_inc(in_done, 1)

            def s2(b, ms):
                if not real(b):
                    return
                for m in ms:
                    if m == 0:
                        pe.wait_ge(v_lo_ready, KV * (b + 1))
                        pe.wait_ge(gate_done, KV * (b + 1))
                    if m < 4:
                        if real(b - 2):
                            pe.wait_ge((gelu2_done, gv_ready)[m % 2], KG * (b - 2) + 3 + m // 2)
                    else:
                        pe.wait_ge(sig_done, 2 * KV * b + m - 3)
                    channels("gates", m, (m + 2) % 4, v_hi, v_lo).then_inc(g_done, 1)

            def s3(b):
                if not real(b):
                    return
                pe.wait_ge(gh_lo_ready, KV * (b + 1))
                for q in range(GROUP):
                    if q % 2 == 0:
                        room(pe, mlp_added, 2 * (b - 2) + q // 2 + 1)
                    mm = tokens("out", q, gh_hi, gh_lo)
                    if q % 2:
                        mm.then_inc(hawk_done, 1)

            def s4(b):
                if real(b):
                    pe.wait_ge(x2r_ready, b + 1)
                    pe.wait_ge(x_lo_ready, min(b + 3, NB) if isinstance(b, int) else b + 3)
                    turn(scaled, x2_turned)

            def s5(b):
                if not real(b):
                    return
                pe.wait_ge(x2_lo_ready, b + 1)
                for n in range(2 * KG):
                    c, half = n // 2, n % 2
                    if n >= 4:
                        pe.wait_ge((gelu2_done, gv_ready)[half], KG * b + c - 1)
                    elif not real(b + 2):
                        if n == 0:
                            pe.wait_ge(sig_done, 2 * KV * NB)
                            pe.wait_ge(gelu2_done, KG * b)
                            pe.wait_ge(gv_ready, KG * b)
                    elif n == 0:
                        pe.wait_ge(v_copied, KV * (b + 3))
                    else:
                        pe.wait_ge(gate_done, KV * (b + 2) + n)
                    channels("grow", c + half * KG, (n + 2) % 4, x2T_hi, x2T_lo).then_inc(grow_done, 1)

            def s6(b):
                if not real(b):
                    return
                pe.wait_ge(gv_lo_ready, KG * (b + 1))
                for q in range(GROUP):
                    if q % 2 == 0:
                        pe.wait_ge(hawk_added, min(2 * b + q // 2 + 3, 2 * NB) if isinstance(b, int) else 2 * b + q // 2 + 3)
                    mm = tokens("shrink", q, gv_hi, gv_lo)
                    if q % 2:
                        mm.then_inc(mlp_done, 1)

            def period(p, par):
                s1(p, range(KV, 2 * KV))
                s5(p - 2)
                s2(p, range(0, 4))
                turn_x(p + 1)
                s2(p, range(4, 2 * KV))
                s3(p - 1)
                s1(p + 1, range(0, KV))
                s6(p - 2)
                s4(p - 1)

            turn_x(0)
            s1(0, range(0, KV))
            run(pe, period)

        @block.scalar
        def _(act):
            def high_x(b):
                if real(b):
                    act.wait_ge(x_turned, b + 1)
                    room(act, in_done, 2 * KV * b)
                    for k in range(KD):
                        ins = act.activation(xT_hi[:, k], T_ps[:, k], ACT.Copy, scale=t["gamma1"][:, k:k + 1])
                    ins.then_inc(x_hi_ready, 1)

            def copy_v(b):
                for c in range(KV if real(b) else 0):
                    act.wait_ge(in_done, 2 * KV * b + c + 1)
                    room(act, conv_done, KV * (b - 1) + c + 1)
                    act.activation(vraw[:, c, HALO:], A_ps[:, c % 4], ACT.Copy).then_inc(v_copied, 1)

            def gelu_gate(b, par):
                for c in range(KV):
                    act.wait_ge(in_done, 2 * KV * b + KV + c + 1)
                    room(act, gh_ready, KV * (b - 2) + c + 1)
                    act.activation(gate[:, par, c], A_ps[:, (KV + c) % 4], ACT.Gelu).then_inc(gate_done, 1)

            def high_v(b, c):
                if real(b):
                    act.wait_ge(conv_done, KV * b + c + 1)
                    room(act, g_done, 2 * KV * b)
                    act.activation(v_hi[:, c], vc[:, c], ACT.Copy).then_inc(v_hi_ready, 1)

            def high_x2(b):
                act.wait_ge(x2_turned, b + 1)
                room(act, grow_done, 2 * KG * b)
                for k in range(KD):
                    ins = act.activation(x2T_hi[:, k], T_ps[:, k], ACT.Copy, scale=t["gamma2"][:, k:k + 1])
                ins.then_inc(x2_hi_ready, 1)

            def gelu(b, c):
                if real(b):
                    act.wait_ge(grow_done, 2 * KG * b + 2 * c + 1)
                    room(act, gv_ready, KG * b + c - 1)
                    act.activation(gelu2[:, c % 2], A_ps[:, (2 * c + 2) % 4], ACT.Gelu).then_inc(gelu2_done, 1)

            def high_gv(b, c):
                if real(b):
                    act.wait_ge(gv_ready, KG * b + c + 1)
                    room(act, mlp_done, 2 * b)
                    act.activation(gv_hi[:, c], gv[:, c % 2], ACT.Copy).then_inc(gv_hi_ready, 1)

            def gates(b, ms):
                if not real(b):
                    return
                for m in ms:
                    act.wait_ge(g_done, 2 * KV * b + m + 1)
                    dst = sigf[:, m] if m < KV else inj[:, m - KV]
                    if m < KV:
                        room(act, alpha_ready, KV * b)
                    else:
                        room(act, scan_done, KV * (b - 1) + m - KV + 1)
                    act.activation(dst, A_ps[:, (m + 2) % 4], ACT.Sigmoid,
                                   bias=t["b_gates"][:, m:m + 1]).then_inc(sig_done, 1)

            def high_gh(b):
                if real(b):
                    for c in range(KV):
                        act.wait_ge(gh_ready, KV * b + c + 1)
                        room(act, hawk_done, 2 * b)
                        act.activation(gh_hi[:, c], beta_h[:, c], ACT.Copy).then_inc(gh_hi_ready, 1)

            def decay(b):
                for c in range(KV):
                    act.wait_ge(sig_done, 2 * KV * b + c + 1)
                    room(act, scan_done, KV * (b - 1) + c + 1)
                    act.activation(alpha[:, c], sigf[:, c], ACT.Exp,
                                   scale=t["log_rate"][:, c:c + 1]).then_inc(alpha_ready, 1)
                for c in range(KV):
                    act.wait_ge(alpha_ready, KV * b + c + 1)
                    room(act, gh_lo_ready, KV * (b - 1) + c + 1)
                    act.activation(beta_h[:, c], alpha[:, c], ACT.Square).then_inc(a2_ready, 1)

            def period(p, par):
                def squares(b, bpar):
                    if real(b):
                        act.wait_ge(hawk_added, 2 * b + 2)
                        act.wait_ge(x_turned, min(b + 3, NB) if isinstance(b, int) else b + 3)
                        for q in range(GROUP):
                            ins = act.activation(scaled[:, q], x2[:, bpar, q], ACT.Square, accum_out=n2[:, q:q + 1])
                        ins.then_inc(n2_ready, 1)

                b = p - 2
                if real(b):
                    high_x2(b)
                if real(p):
                    gelu_gate(p, par)
                high_v(p, 0)
                gelu(b, 0)
                high_v(p, 1)
                gelu(b, 1)
                high_gv(b, 0)
                high_v(p, 2)
                gelu(b, 2)
                high_gv(b, 1)
                gelu(b, 3)
                high_gv(b, 2)
                high_gv(b, 3)
                gates(p, range(0, KV))
                high_gh(p - 1)
                high_x(p + 1)
                gates(p, range(KV, 2 * KV))
                if real(b):
                    act.wait_ge(moe_ready, b + 1)
                    room(act, out_stored, 16 * b)
                    act.activation(mix[:], ya[:], ACT.Sigmoid).then_inc(sg_ready, 1)
                if real(p):
                    decay(p)
                copy_v(p + 1)
                squares(p - 1, 1 - par)
                if real(p):
                    for c in range(KV):
                        act.wait_ge(om_ready, KV * p + c + 1)
                        act.activation(beta_h[:, c], beta_h[:, c], ACT.Sqrt, bias=beta_eps[:]).then_inc(beta_ready, 1)

            act.wait_ge(const_ready, 1)
            high_x(0)
            copy_v(0)
            run(act, period)

        @block.vector
        def _(dve):
            ch = Chain(dve, dve_chain)
            dve.memset(beta_eps[:], BETA_EPS)
            dve.memset(minus_half[:], -0.5)
            ch.link(dve.memset(vraw[:, :, 0:HALO], 0.0))
            dve.memset(hlast[:], 0.0).then_inc(const_ready, 1)

            def scale_x(b):
                if real(b):
                    dve.wait_ge(xn_in, 16 * (b + 1))
                    room(dve, x2_turned, b - 2)
                    room(dve, x_turned, b)
                    for q in range(GROUP):
                        ins = dve.tensor_scalar(scaled[:, q], xn_t[:, q], t["r1"][:, ds(GROUP * b + q, 1)],
                                                None, ALU.mult)
                    ins.then_inc(xr_ready, 1)

            def low(b, gamma, hi, lo, hi_ready, lo_ready, used, value):
                dve.wait_ge(hi_ready, b + 1)
                room(dve, used, value)
                for k in range(KD):
                    ins = dve.scalar_tensor_tensor(lo[:, k], T_ps[:, k], gamma[:, k:k + 1], hi[:, k].bitcast(F32),
                                                   ALU.mult, ALU.subtract)
                ins.then_inc(lo_ready, 1)

            def low_x(b):
                if real(b):
                    low(b, t["gamma1"], xT_hi, xT_lo, x_hi_ready, x_lo_ready, in_done, 2 * KV * b)

            def convolve(b, par, c):
                if real(b):
                    dve.wait_ge(v_copied, KV * b + c + 1)
                    room(dve, xg1_ready, KV * (b - 1) + c + 1)
                    room(dve, v_lo_ready, KV * (b - 1) + c + 1)
                    ch.link(dve.tensor_scalar(vc[:, c], vraw[:, c, 0:B], t["conv_w"][:, c, 0:1], t["conv_b"][:, c:c + 1],
                                              ALU.mult, ALU.add))
                    for k in range(1, HALO + 1):
                        ch.link(dve.scalar_tensor_tensor(vc[:, c], vraw[:, c, k:k + B], t["conv_w"][:, c, k:k + 1],
                                                         vc[:, c], ALU.mult, ALU.add))
                    if par == 0:
                        ins = dve.tensor_copy(vraw[:, c, 0:HALO], vraw[:, c, B:B + HALO])
                    else:
                        ins = dve.memset(vraw[:, c, 0:HALO], 0.0)
                    ins.then_inc(conv_done, 1)

            def mixture(b):
                for n in range(2):
                    dve.wait_ge(y_in[n], 16 * GROUP * (b + 1))
                for q in range(GROUP):
                    ins = dve.tensor_scalar(ya[:, q], ya[:, q], t["wts"][:, 0, ds(GROUP * b + q, 1)], None, ALU.mult)
                ch.link(ins)
                for q in range(GROUP):
                    ins = dve.scalar_tensor_tensor(ya[:, q], yb[:, q], t["wts"][:, 1, ds(GROUP * b + q, 1)], ya[:, q],
                                                   ALU.mult, ALU.add)
                ins.then_inc(moe_ready, 1)

            def low_v(b, c):
                if real(b):
                    dve.wait_ge(v_hi_ready, KV * b + c + 1)
                    room(dve, g_done, 2 * KV * b)
                    dve.tensor_tensor(v_lo[:, c], vc[:, c], v_hi[:, c].bitcast(F32),
                                      ALU.subtract).then_inc(v_lo_ready, 1)

            def add_mlp(b, par):
                for n in range(2):
                    dve.wait_ge(mlp_done, 2 * b + n + 1)
                    xs = x2[:, par, 2 * n:2 * n + 2].rearrange("p q d -> p (q d)")
                    dve.tensor_tensor(xs, O_ps[:, n], xs, ALU.add).then_inc(mlp_added, 1)

            def add_hawk(b, par):
                dve.wait_ge(x2_in[par], 16 * (b // 2 + 1) if isinstance(b, int) else (b - par) * 8 + 16)
                for n in range(2):
                    dve.wait_ge(hawk_done, 2 * b + n + 1)
                    xs = x2[:, par, 2 * n:2 * n + 2].rearrange("p q d -> p (q d)")
                    dve.tensor_tensor(xs, O_ps[:, n], xs, ALU.add).then_inc(hawk_added, 1)

            def recur(b, par):
                for c in range(KV):
                    dve.wait_ge(xg_ready, KV * b + c + 1)
                    dve.tensor_tensor_scan(beta_h[:, c], alpha[:, c], inj[:, c], 0.0 if par == 0 else hlast[:, c:c + 1],
                                           ALU.mult, ALU.add).then_inc(scan_done, 1)
                if par == 0:
                    dve.wait_ge(scan_done, KV * (b + 1))
                    ch.link(dve.tensor_copy(hlast[:], beta_h[:, :, B - 1]))
                for c in range(KV):
                    dve.wait_ge(scan_done, KV * b + c + 1)
                    dve.wait_ge(gate_done, KV * b + c + 1)
                    dve.tensor_tensor(beta_h[:, c], gate[:, par, c], beta_h[:, c], ALU.mult).then_inc(gh_ready, 1)

            def low_gh(b):
                for c in range(KV):
                    dve.wait_ge(gh_hi_ready, KV * b + c + 1)
                    room(dve, hawk_done, 2 * b)
                    dve.tensor_tensor(gh_lo[:, c], beta_h[:, c], gh_hi[:, c].bitcast(F32),
                                      ALU.subtract).then_inc(gh_lo_ready, 1)

            def multiply(b, c):
                if real(b):
                    dve.wait_ge(gelu2_done, KG * b + c + 1)
                    dve.wait_ge(grow_done, 2 * KG * b + 2 * c + 2)
                    room(dve, gv_lo_ready, KG * b + c - 1)
                    dve.tensor_tensor(gv[:, c % 2], A_ps[:, (2 * c + 3) % 4], gelu2[:, c % 2],
                                      ALU.mult).then_inc(gv_ready, 1)

            def low_gv(b, c):
                if real(b):
                    dve.wait_ge(gv_hi_ready, KG * b + c + 1)
                    room(dve, mlp_done, 2 * b)
                    dve.tensor_tensor(gv_lo[:, c], gv[:, c % 2], gv_hi[:, c].bitcast(F32),
                                      ALU.subtract).then_inc(gv_lo_ready, 1)

            def period(p, par):
                b = p - 2
                convolve(p, par, 1)
                if real(b):
                    low(b, t["gamma2"], x2T_hi, x2T_lo, x2_hi_ready, x2_lo_ready, grow_done, 2 * KG * b)
                if real(p - 3):
                    add_mlp(p - 3, 1 - par)
                low_v(p, 0)
                convolve(p, par, 2)
                multiply(b, 0)
                low_v(p, 1)
                multiply(b, 1)
                low_gv(b, 0)
                low_v(p, 2)
                multiply(b, 2)
                low_gv(b, 1)
                multiply(b, 3)
                low_gv(b, 2)
                low_gv(b, 3)
                scale_x(p + 1)
                if real(p - 1):
                    recur(p - 1, 1 - par)
                    low_gh(p - 1)
                if real(b):
                    mixture(b)
                low_x(p + 1)
                if real(p - 1):
                    add_hawk(p - 1, 1 - par)
                if real(p):
                    for c in range(KV):
                        dve.wait_ge(a2_ready, KV * p + c + 1)
                        dve.tensor_scalar(beta_h[:, c], beta_h[:, c], -1.0, 1.0, ALU.mult, ALU.add).then_inc(om_ready, 1)
                convolve(p + 1, 1 - par, 0)
                if real(p - 1):
                    dve.wait_ge(r2_ready, p)
                    for q in range(GROUP):
                        ins = dve.tensor_scalar(scaled[:, q], x2[:, 1 - par, q], r2[:, q:q + 1], float(D) ** 0.5,
                                                ALU.mult, ALU.mult)
                    ins.then_inc(x2r_ready, 1)

            scale_x(0)
            low_x(0)
            convolve(0, 0, 0)
            run(dve, period, ch)

        @block.gpsimd
        def _(pool):
            def period(p, par):
                b = p - 1
                if real(b):
                    for c in range(KV):
                        pool.wait_ge(xg1_ready, KV * b + c + 1)
                        pool.wait_ge(beta_ready, KV * b + c + 1)
                        pool.tensor_tensor(inj[:, c], inj[:, c], beta_h[:, c], ALU.mult).then_inc(xg_ready, 1)
                if real(p - 3):
                    e = p - 3
                    pool.wait_ge(gated, e + 1)
                    pool.wait_ge(mlp_added, 2 * e + 2)
                    pool.tensor_tensor(mix[:], mix[:], x2[:, 1 - par], ALU.mult).then_inc(out_mult, 1)
                    pool.wait_ge(out_mult, e + 1)
                    pool.wait_ge(x_in, 16 * (e + 1))
                    pool.tensor_tensor(mix[:], mix[:], x_t[:], ALU.add).then_inc(out_done, 1)
                if real(p):
                    for c in range(KV):
                        pool.wait_ge(sig_done, 2 * KV * p + KV + c + 1)
                        pool.tensor_tensor(inj[:, c], inj[:, c], vc[:, c], ALU.mult).then_inc(xg1_ready, 1)
                if real(p - 2):
                    pool.wait_ge(sg_ready, p - 1)
                    pool.tensor_tensor(mix[:], mix[:], ya[:], ALU.mult).then_inc(gated, 1)
                if real(b):
                    pool.wait_ge(n2_ready, b + 1)
                    pool.tensor_tensor(r2[:], n2[:], minus_half[:], ALU.pow).then_inc(r2_ready, 1)
                    room(pool, moe_ready, b)
                    room(pool, gated, b)
                    for n in range(2):
                        room(pool, y_in[n], 16 * GROUP * b)
                    pool.tensor_copy(yidx[:], t["slots"][:, :, ds(GROUP * b, GROUP)]).then_inc(yidx_ready, 1)
                    pool.wait_ge(yidx_ready, b + 1)
                    pool.tensor_tensor(spare[:], minus_half[0:1, 0:1], minus_half[0:1, 0:1], ALU.add)
                    for n, dst in enumerate((ya, yb)):
                        for q in range(GROUP):
                            pool.indirect_dma_start(dst[:, q], None, y_dram,
                                                    bass.IndirectOffsetOnAxis(ap=yidx[:, n, q:q + 1], axis=0)
                                                    ).then_inc(y_in[n], 16)

            pool.wait_ge(const_ready, 1)
            run(pool, period)


def build(nc, x, gamma1, W_in, conv_w, conv_b, W_gates, b_gates, forget_base, W_out, gamma2, W_grow, W_shrink,
          router_w, w1, w2, out, xn_dram, y_dram):
    batches, S, D = x.shape
    N = batches * S
    E, _, H = w1.shape
    HID, GHID = W_out.shape[1], W_shrink.shape[1]
    T = 2 * N // P + E
    T = -(-T // RING) * RING
    xf = x.rearrange("b s d -> (b s) d")
    of = out.rearrange("b s d -> (b s) d")
    plan, columns = weight_plan(D, HID, GHID)

    with ExitStack() as ctx:
        def keep(name, shape, dt=F32):
            return ctx.enter_context(nc.sbuf_tensor(name, shape, dt))

        t = dict(tiles=T, E=E, H=H, plan=plan, plan_columns=columns)
        t["ident"] = keep("ident", [P, P])
        t["r1"] = keep("r1", [P, N // P])
        t["slots"] = keep("slots", [P, 2, N // P], U32)
        t["wts"] = keep("wts", [P, 2, N // P])
        t["token_of_slot"] = keep("token_of_slot", [P, T], U32)
        t["tile_expert"] = keep("tile_expert", [1, T], I32)
        t["conv_w"] = keep("conv_w_sb", [P, HID // P, 4])
        t["conv_b"] = keep("conv_b_sb", [P, HID // P])
        t["b_gates"] = keep("b_gates_sb", [P, 2 * HID // P])
        t["forget_base"] = keep("forget_sb", [P, HID // P])
        t["log_rate"] = keep("log_rate", [P, HID // P])
        t["gamma1"] = keep("gamma1_sb", [P, D // P])
        t["gamma2"] = keep("gamma2_sb", [P, D // P])
        t["raw_in"] = ctx.enter_context(nc.semaphore("raw_in"))
        ctx.enter_context(nc.allow_non_contiguous_dma(reason="small vectors, one element a partition"))

        with ExitStack() as moe:
            WE = E * 2 * (D // P) * H
            t["w_hi"] = moe.enter_context(nc.sbuf_tensor("w_hi", [P, WE], F32R))
            t["w_lo"] = moe.enter_context(nc.sbuf_tensor("w_lo", [P, WE], F32R))
            normalise_and_route(nc, None, t, xf, router_w, w1, w2, xn_dram)
            t["raw"] = moe.enter_context(nc.sbuf_tensor("raw", [P, columns], F32))
            loads = []
            for name, w in (("in", W_in), ("gates", W_gates), ("out", W_out), ("grow", W_grow), ("shrink", W_shrink)):
                at, cols, chunks = plan[name]
                loads.append((t["raw"][:, at:at + cols * chunks].rearrange("p (m k) -> p m k", k=chunks * P),
                              w.rearrange("(m p) k -> p m k", p=P)))
            loads.append((t["conv_w"][:], conv_w.rearrange("(c p) o k -> p c (o k)", p=P)))
            for name, v in (("conv_b", conv_b), ("b_gates", b_gates), ("forget_base", forget_base),
                            ("gamma1", gamma1), ("gamma2", gamma2)):
                loads.append((t[name][:], v.rearrange("(c p) -> p c", p=P)))
            experts(nc, t, xn_dram, y_dram, loads)
        t["wa_hi"] = keep("wa_hi", [P, columns], F32R)
        t["wa_lo"] = keep("wa_lo", [P, columns], F32R)
        prepare_weights(nc, t)
        recurrent_and_mix(nc, t, xf, xn_dram, y_dram, of, S // (GROUP * P))


INPUTS = ["L0_attn_x", "L0_attn_gamma1", "L0_attn_W_in", "L0_attn_conv_w", "L0_attn_conv_b", "L0_attn_W_gates",
          "L0_attn_b_gates", "L0_attn_forget_base", "L0_attn_W_out", "L0_attn_gamma2", "L0_attn_W_grow",
          "L0_attn_W_shrink", "L0_ffn_router_w", "L0_ffn_w1", "L0_ffn_w2"]


def kernel(**inputs):
    import numpy as np
    import concourse.bacc as bacc
    from concourse.bass_utils import run_bass_kernel_spmd

    nc = bacc.Bacc("TRN2", target_bir_lowering=False, num_devices=1)
    arrays, args = {}, []
    for name in INPUTS:
        a = np.ascontiguousarray(inputs[name])
        arrays[f"in_{name}"] = a
        args.append(nc.dram_tensor(f"in_{name}", a.shape, mybir.dt.from_np(a.dtype), kind="ExternalInput").ap())
    b, s, d = inputs["L0_attn_x"].shape
    e = inputs["L0_ffn_w1"].shape[0]
    tiles = -(-(2 * b * s // P + e) // RING) * RING
    out = nc.dram_tensor("out_0", (b, s, d), F32, kind="ExternalOutput").ap()
    xn_dram = nc.dram_tensor("xn_rows", (b * s, d), F32, kind="Internal").ap()
    y_dram = nc.dram_tensor("y_rows", (tiles * P, d), F32, kind="Internal").ap()
    build(nc, *args, out, xn_dram, y_dram)
    r = run_bass_kernel_spmd(nc, [arrays], core_ids=[0])
    return r.results[0]["out_0"]
```

```python
from contextlib import ExitStack

import concourse.bass as bass
from concourse import mybir

P = 128
F32 = mybir.dt.float32
F32R = mybir.dt.float32r
BF16 = mybir.dt.bfloat16
F16 = mybir.dt.float16
U32 = mybir.dt.uint32
I32 = mybir.dt.int32
ALU = mybir.AluOpType
ACT = mybir.ActivationFunctionType
AX_X = mybir.AxisListType.X
ds = bass.ds

LN_EPS = 1e-5
BETA_EPS = 1e-6
ALPHA_LOG_SCALE = -8.0
BIG = 3.0e38
CODES = 2048
GROUP = 4
RING = 8


class Chain:

    def __init__(self, eng, sem):
        self.eng, self.sem, self.n, self.base = eng, sem, 0, None

    def link(self, ins):
        ins.then_inc(self.sem, 1)
        self.n += 1
        self.eng.wait_ge(self.sem, self.n if self.base is None else self.base + self.n)

    def repeat(self, i, first, per_turn):
        self.base = (i - first) * per_turn
        self.mark = self.n

    def end_turn(self, turns, per_turn):
        assert self.n - self.mark == per_turn, (self.n - self.mark, per_turn)
        self.base = None
        self.n = self.mark + turns * per_turn


def room(eng, sem, value):
    if not isinstance(value, int) or value > 0:
        eng.wait_ge(sem, value)


class Lease:

    def __init__(self, shared):
        self.shared, self.at = shared, 0

    def view(self, *shape):
        size = 1
        for s in shape:
            size *= s
        flat = self.shared[:, self.at:self.at + size]
        self.at += size
        names = "abc"[:len(shape)]
        if len(shape) == 1:
            return flat
        return flat.rearrange(f"p ({' '.join(names)}) -> p {' '.join(names)}", **dict(zip(names, shape)))


def normalise_and_route(nc, t, x, router_w, w1, w2, xn_dram):
    N, D = x.shape
    E, _, H = w1.shape
    NT = N // P
    NG = NT // GROUP
    KD = D // P
    GC = GROUP * P
    AHEAD = 4
    T = t["tiles"]
    WD = KD * H

    x_v = x.rearrange("(g q p) d -> g p q d", q=GROUP, p=P)
    xn_v = xn_dram.rearrange("(g q p) d -> g p q d", q=GROUP, p=P)
    w1_v = w1.rearrange("e (k p) h -> e p k h", p=P)
    w2_v = w2.rearrange("e (k p) d -> e p k d", p=P)

    with ExitStack() as ctx:
        def sem(name):
            return ctx.enter_context(nc.semaphore(name))

        def tile(name, shape, dt=F32):
            return ctx.enter_context(nc.sbuf_tensor(name, shape, dt))

        lease = Lease(t["shared"])
        xa = lease.view(AHEAD, GROUP, D)
        xn = lease.view(2, GROUP, D)
        stage1, stage2 = lease.view(WD), lease.view(WD)
        xT = tile("xT", [P, 2, KD, GC])
        bn6 = tile("bn6", [P, 2, GROUP, 6])
        mv = tile("mv", [P, 2, GROUP, 2])
        std = tile("std", [P, 2, GROUP])
        sv = tile("sv", [P, 2, GROUP])
        rstd = tile("rstd", [P, 2, GROUP])
        isv = tile("isv", [P, 2, GROUP])
        rrow = tile("rrow", [E, D])
        rT = tile("rT", [P, KD, E])
        lgT = tile("lgT", [E, 2, GC])
        eps = tile("eps", [P, 1])
        logit = tile("logit", [P, NT, E])
        row_f = tile("row_f", [P, P])
        col_f = tile("col_f", [P, 1])
        tri = tile("tri", [P, P], BF16)
        ones = tile("ones", [P, P], BF16)
        iota_e = tile("iota_e", [P, E])
        iota_cap = tile("iota_cap", [P, NT])
        code = tile("code", [P, NT])
        row_h = tile("row_h", [P, P], F16)
        iota_h = tile("iota_h", [P, T], F16)
        one = tile("one", [P, 1])
        minus_b = tile("minus_b", [P, NT])
        offset2 = xT[:, 0].rearrange("p k c -> p (k c)")[:, 0:4 * P].rearrange("p (j n c) -> p j n c", j=2, n=2)
        wk = [tile(f"wk{n}", [P, NT, E]) for n in range(4)]
        oh = [tile(f"oh{n}", [P, NT, E]) for n in range(2)]
        chosen = tile("chosen", [P, NT, E], BF16)
        best = [tile(f"best{n}", [P, NT]) for n in range(2)]
        ix = tile("ix", [P, NT])
        tot = tile("tot", [P, E, NT])
        inc = tile("inc", [P, E, NT])
        zeros_nt = tile("zeros_nt", [P, NT])
        tiles_e = tile("tiles_e", [P, E])
        end_e = t["end_e"]
        start_e = tile("start_e", [P, E])
        slot_f = tile("slot_f", [P, 2, NT])
        a_i = tile("a_i", [P, 2, NT], I32)
        b_i = tile("b_i", [P, 2, NT], I32)
        a_f = tile("a_f", [P, 2, NT])
        b_f = tile("b_f", [P, 2, NT])
        ohb = tile("ohb", [P, 2, 2, 2, P], F16)
        oha = tile("oha", [P, 2, 2, 2, T], F16)
        flat = [w[:].rearrange("p t e -> p (t e)") for w in wk]
        coded, token = (flat[n][:, 0:2 * T].rearrange("p (h t) -> p h t", h=2) for n in (0, 1))
        positive, negative = flat[2][:, 0:T], flat[3][:, 0:T]
        dexp = t["dexp"]
        spare = tile("spare_1", [1, 1])

        x_in = [sem(f"x_in{j}") for j in range(AHEAD)]
        small_in = sem("small_in")
        w1_in, w2_in = sem("w1_in"), sem("w2_in")
        late_in = [sem(f"late_in{n}") for n in range(2 * E - 2 * (NG // AHEAD))]
        w_hi, w_lo = sem("w_hi"), sem("w_lo")
        pool_const, dve_const = sem("pool_const"), sem("dve_const")
        stats_ready, std_ready = sem("stats_ready"), sem("std_ready")
        xn_ready = sem("xn_ready")
        xn_stored = [sem(f"xn_stored{j}") for j in range(2)]
        xT_psum, xT_ready = sem("xT_psum"), sem("xT_ready")
        rT_psum, rT_ready = sem("rT_psum"), sem("rT_ready")
        lgT_psum, lgT_ready = sem("lgT_psum"), sem("lgT_ready")
        lg_psum, logits_copied = sem("lg_psum"), sem("logits_copied")
        chosen_ready, prefix_psum = sem("chosen_ready"), sem("prefix_psum")
        score_gap, gap_exp = sem("score_gap"), sem("gap_exp")
        slots_split, slot_onehot, squared = sem("slots_split"), sem("slot_onehot"), sem("squared")
        tile_onehot, onehot_used = sem("tile_onehot"), sem("onehot_used")
        dve_chain = sem("dve_chain_1")
        routed = sem("routed")

        xT_ps = ctx.enter_context(nc.psum_tensor("xT_ps", [P, 2, KD, GC], F32))
        lg_ps = ctx.enter_context(nc.psum_tensor("lg_ps", [P, 2, GC], F32))
        pf_ps = ctx.enter_context(nc.psum_tensor("pf_ps", [P, 2, NT * E], F32))

        ident = t["ident"]
        block = ctx.enter_context(nc.Block())
        TURNS = NG // AHEAD
        assert NG % AHEAD == 0 and N == 4 * CODES and 0 <= 2 * (E - TURNS) <= AHEAD + 4 and GROUP * D == WD
        late_stage = [xa[:, n].rearrange("p q d -> p (q d)") for n in range(AHEAD)]
        late_stage += [xn[:, n].rearrange("p q d -> p (q d)") for n in range(2)] + [stage1[:], stage2[:]]

        @block.sync
        def _(sp):
            def group_of(view, g):
                return view[g] if isinstance(g, int) else view[ds(g, 1)].rearrange("o p q d -> (o p) q d")

            def expert_in(e):
                for src, dst, landed in ((w1_v, stage1, w1_in), (w2_v, stage2, w2_in)):
                    if not (isinstance(e, int) and e == 0):
                        sp.wait_ge(w_lo, 2 * e)
                    s = group_of(src, e)
                    sp.dma_start(columns(dst[:], s), s).then_inc(landed, 16)

            def columns(flat, like):
                return flat.rearrange("p (k n) -> p k n", k=like.shape[1])

            def turn(i, last):
                for j in range(AHEAD):
                    g = AHEAD * i + j
                    sp.wait_ge(xn_ready, g + 1)
                    if not last:
                        sp.dma_start(xa[:, j], group_of(x_v, g + AHEAD)).then_inc(x_in[j], 16)
                    sp.dma_start(group_of(xn_v, g), xn[:, j % 2]).then_inc(xn_stored[j % 2], 16)
                if not last:
                    expert_in(i + 1)

            for j in range(AHEAD):
                sp.dma_start(xa[:, j], group_of(x_v, j)).then_inc(x_in[j], 16)
                if j == 1:
                    sp.dma_start(rrow[:], router_w).then_inc(small_in, 16)
                    expert_in(0)
            turn(0, False)
            with sp.Fori(1, TURNS - 1) as i:
                turn(i, False)
            turn(TURNS - 1, True)
            for n, m in enumerate(range(2 * TURNS, 2 * E)):
                if n < AHEAD:
                    sp.wait_ge(xn_ready, NG - AHEAD + n + 1)
                elif n < AHEAD + 2:
                    sp.wait_ge(xn_stored[n % 2], 8 * NG)
                    sp.wait_ge(xT_psum, NG)
                else:
                    sp.wait_ge(w_lo, 2 * TURNS)
                s = (w1_v, w2_v)[m % 2][m // 2]
                sp.dma_start(columns(late_stage[n], s), s).then_inc(late_in[n], 16)
            for j in range(2):
                sp.wait_ge(xn_stored[j], 8 * NG)

        @block.gpsimd
        def _(pool):
            pool.iota(row_f[:], pattern=[[1, P]], base=0, channel_multiplier=0, allow_small_or_imprecise_dtypes=True)
            pool.iota(col_f[:], pattern=[[0, 1]], base=0, channel_multiplier=1, allow_small_or_imprecise_dtypes=True)
            pool.iota(iota_e[:], pattern=[[1, E]], base=-E, channel_multiplier=0, allow_small_or_imprecise_dtypes=True)
            pool.iota(iota_cap[:], pattern=[[P, NT]], base=0, channel_multiplier=0, allow_small_or_imprecise_dtypes=True)
            pool.iota(row_h[:], pattern=[[1, P]], base=0, channel_multiplier=0, allow_small_or_imprecise_dtypes=True)
            pool.iota(iota_h[:], pattern=[[1, T]], base=0, channel_multiplier=0, allow_small_or_imprecise_dtypes=True)
            pool.iota(code[:], pattern=[[0, NT * P // CODES], [P, CODES // P]], base=1, channel_multiplier=1,
                      allow_small_or_imprecise_dtypes=True)
            pool.memset(ones[:], 1.0)
            pool.memset(zeros_nt[:], 0.0)
            pool.memset(one[:], 1.0)
            pool.memset(eps[:], LN_EPS).then_inc(pool_const, 1)

            def split_low(i):
                for n, (stage, landed) in enumerate(((stage1, w1_in), (stage2, w2_in))):
                    pool.wait_ge(w_hi, 2 * i + n + 1)
                    at = ds(i * 2 * WD + n * WD, WD)
                    pool.tensor_tensor(t["w_lo"][:, at], stage[:], t["w_hi"][:, at].bitcast(F32),
                                       ALU.subtract).then_inc(w_lo, 1)

            with pool.Fori(0, TURNS) as i:
                split_low(i)
            for n, m in enumerate(range(2 * TURNS, 2 * E)):
                pool.wait_ge(w_hi, m + 1)
                at = slice(m * WD, (m + 1) * WD)
                pool.tensor_tensor(t["w_lo"][:, at], late_stage[n], t["w_hi"][:, at].bitcast(F32),
                                   ALU.subtract).then_inc(w_lo, 1)

        @block.scalar
        def _(act):
            def deviations(g, j, first):
                act.wait_ge(stats_ready, g + 1)
                if not first:
                    act.wait_ge(xn_ready, g - 1)
                act.activation(std[:, j], mv[:, j, :, 1], ACT.Sqrt, bias=eps[:])
                act.activation(sv[:, j], mv[:, j, :, 1], ACT.Sqrt).then_inc(std_ready, 1)

            def copy_logits(g, j):
                act.wait_ge(lgT_psum, g + 1)
                room(act, lg_psum, g - 1)
                act.activation(lgT[:, j], pf_ps[0:E, j, 0:GC], ACT.Copy).then_inc(lgT_ready, 1)

            def turn(i, first, last):
                for j in range(AHEAD):
                    g = AHEAD * i + j
                    if not (last and j == AHEAD - 1):
                        deviations(g + 1, (j + 1) % 2, first and j == 0)
                    act.wait_ge(xT_psum, g + 1)
                    if not (first and j < 2):
                        act.wait_ge(lgT_psum, g - 1)
                    for k in range(KD):
                        ev = act.activation(xT[:, j % 2, k], xT_ps[:, j % 2, k], ACT.Copy)
                    ev.then_inc(xT_ready, 1)
                    if not (first and j == 0):
                        copy_logits(g - 1, (j + 1) % 2)
                    if j in (1, 2):
                        stage, landed = ((stage1, w1_in), (stage2, w2_in))[j - 1]
                        act.wait_ge(landed, 16 * (i + 1))
                        act.activation(t["w_hi"][:, ds(i * 2 * WD + (j - 1) * WD, WD)], stage[:],
                                       ACT.Copy).then_inc(w_hi, 1)

            act.wait_ge(pool_const, 1)
            deviations(0, 0, True)
            turn(0, True, False)
            with act.Fori(1, TURNS - 1) as i:
                turn(i, False, False)
            turn(TURNS - 1, False, True)
            copy_logits(NG - 1, 1)
            for n, m in enumerate(range(2 * TURNS, 2 * E)):
                act.wait_ge(late_in[n], 16)
                act.activation(t["w_hi"][:, m * WD:(m + 1) * WD], late_stage[n], ACT.Copy).then_inc(w_hi, 1)
            act.wait_ge(score_gap, 1)
            act.activation(dexp[:], ix[:], ACT.Exp).then_inc(gap_exp, 1)

            def slots_onehot(i, j, first):
                for n in range(2):
                    ins = act.activation(offset2[:, j, n], row_f[:], ACT.Square,
                                         bias=minus_b[:, ds(2 * (2 * i + j) + n, 1)])
                ins.then_inc(squared, 1)
                act.wait_ge(squared, 2 * i + j + 1)
                if not first:
                    act.wait_ge(onehot_used, 2 * i + j - 1)
                act.activation(ohb[:, j, 1], offset2[:, j], ACT.Relu, scale=-1.0, bias=one[:]).then_inc(slot_onehot, 1)

            act.wait_ge(slots_split, 1)
            slots_onehot(0, 0, True)
            slots_onehot(0, 1, True)
            with act.Fori(1, NT // 4) as i:
                slots_onehot(i, 0, False)
                slots_onehot(i, 1, False)

        @block.tensor
        def _(pe):
            pe.wait_ge(small_in, 16)
            pe.wait_ge(dve_const, 1)
            for k in range(KD):
                tr = pe.transpose(pf_ps[:, 0, k * E:(k + 1) * E], rrow[:, k * P:(k + 1) * P], ident[0:E, 0:E])
            tr.then_inc(rT_psum, 1)

            def transposes(g, j, first):
                pe.wait_ge(xn_ready, g + 1)
                if not first:
                    pe.wait_ge(xT_ready, g - 1)
                for k in range(KD):
                    for q in range(GROUP):
                        tr = pe.transpose(xT_ps[:, j, k, q * P:(q + 1) * P], xn[:, j, q, k * P:(k + 1) * P], ident[:])
                tr.then_inc(xT_psum, 1)

            def logits(g, j):
                pe.wait_ge(xT_ready, g + 1)
                room(pe, lgT_ready, g)
                room(pe, logits_copied, g - 2)
                for k in range(KD):
                    mm = pe.matmul(pf_ps[0:E, j, 0:GC], rT[:, k], xT[:, j, k], start=(k == 0), stop=(k == KD - 1))
                mm.then_inc(lgT_psum, 1)

            def turn_logits(g, j):
                for q in range(GROUP):
                    tr = pe.transpose(lg_ps[:, j, q * E:(q + 1) * E], lgT[:, j, q * P:(q + 1) * P], ident[0:E, 0:E])
                tr.then_inc(lg_psum, 1)

            def pair(i):
                for j in range(2):
                    g = 2 * i + j
                    transposes(g, j, False)
                    logits(g - 1, 1 - j)
                    turn_logits(g - 2, j)

            transposes(0, 0, True)
            pe.wait_ge(rT_ready, 1)
            transposes(1, 1, True)
            logits(0, 0)
            pair(1)
            with pe.Fori(2, NG // 2) as i:
                pair(i)
            logits(NG - 1, 1)
            turn_logits(NG - 2, 0)
            pe.wait_ge(lgT_ready, NG)
            pe.wait_ge(logits_copied, NG - 2)
            turn_logits(NG - 1, 1)

            pe.wait_ge(chosen_ready, 1)
            pe.matmul(pf_ps[:, 0], tri[:], chosen[:], start=True, stop=True)
            pe.matmul(pf_ps[:, 1], ones[:], chosen[:], start=True, stop=True).then_inc(prefix_psum, 1)

            def place(i, j, half, first, last):
                pe.wait_ge(slot_onehot, 2 * i + j + 1)
                pe.wait_ge(tile_onehot, 2 * i + j + 1)
                for n in range(2):
                    for c in range(2):
                        mm = pe.matmul(lg_ps[:, half, 0:T], ohb[:, j, c, n], oha[:, j, c, n],
                                       start=first and n == 0 and c == 0, stop=last and n == 1 and c == 1)
                mm.then_inc(onehot_used, 1)

            for half in range(2):
                start, end = half * NT // 8, (half + 1) * NT // 8
                place(start, 0, half, True, False)
                place(start, 1, half, False, False)
                with pe.Fori(start + 1, end - 1) as i:
                    place(i, 0, half, False, False)
                    place(i, 1, half, False, False)
                place(end - 1, 0, half, False, False)
                place(end - 1, 1, half, False, True)

        @block.vector
        def _(dve):
            ch = Chain(dve, dve_chain)
            dve.wait_ge(pool_const, 1)
            dve.tensor_scalar(ident[:], row_f[:], col_f[:], None, ALU.is_equal).then_inc(dve_const, 1)
            dve.tensor_scalar(tri[:], row_f[:], col_f[:], None, ALU.is_gt)

            def stats(g, i, a):
                dve.wait_ge(x_in[a], 16 * (i + 1))
                j = a % 2
                for q in range(GROUP):
                    ins = dve.bn_stats(bn6[:, j, q], xa[:, a, q])
                ch.link(ins)
                dve.memset(spare[:], 0.0)
                for q in range(GROUP):
                    ins = dve.bn_aggr(mv[:, j, q], bn6[:, j, q])
                ins.then_inc(stats_ready, 1)

            def finish(g, i, a, first):
                j = a % 2
                dve.wait_ge(std_ready, g + 1)
                dve.reciprocal(rstd[:, j], std[:, j])
                ch.link(dve.reciprocal(isv[:, j], sv[:, j]))
                dve.tensor_tensor(t["r1"][:, ds(g * GROUP, GROUP)], std[:, j], isv[:, j], ALU.mult)
                if not first:
                    dve.wait_ge(xn_stored[j], 16 * (AHEAD // 2 * i + a // 2))
                    dve.wait_ge(xT_psum, g - 1)
                for q in range(GROUP):
                    ins = dve.tensor_scalar(xn[:, j, q], xa[:, a, q], mv[:, j, q, 0:1], rstd[:, j, q:q + 1],
                                            ALU.subtract, ALU.mult)
                ins.then_inc(xn_ready, 1)

            def keep_logits(g, j):
                dve.wait_ge(lg_psum, g + 1)
                dve.tensor_copy(logit[:, ds(g * GROUP, GROUP)],
                                lg_ps[:, j, 0:GROUP * E].rearrange("p (q e) -> p q e", q=GROUP)).then_inc(logits_copied, 1)

            stats(0, 0, 0)
            stats(1, 0, 1)
            finish(0, 0, 0, True)
            dve.wait_ge(rT_psum, 1)
            dve.tensor_copy(rT[:], pf_ps[:, 0, 0:KD * E].rearrange("p (k e) -> p k e", k=KD)).then_inc(rT_ready, 1)

            def turn(i, first):
                for j in range(AHEAD):
                    g = AHEAD * i + j
                    ahead, wrap = (j + 2) % AHEAD, (j + 2) // AHEAD
                    stats(g + 2, i + wrap, ahead)
                    finish(g + 1, i + (j + 1) // AHEAD, (j + 1) % AHEAD, first and j == 0)
                    if not (first and j < 3):
                        keep_logits(g - 3, (j + 1) % 2)

            n0 = ch.n
            turn(0, True)
            per_turn = ch.n - n0
            with dve.Fori(1, TURNS - 1) as i:
                ch.repeat(i, 1, per_turn)
                turn(i, False)
            ch.end_turn(TURNS - 2, per_turn)
            for g in range(NG - AHEAD, NG - 1):
                if g + 2 < NG:
                    stats(g + 2, TURNS - 1, (g + 2) % AHEAD)
                finish(g + 1, TURNS - 1, (g + 1) % AHEAD, False)
                keep_logits(g - 3, (g + 1) % 2)
            keep_logits(NG - 4, 0)
            keep_logits(NG - 3, 1)
            keep_logits(NG - 2, 0)
            keep_logits(NG - 1, 1)
            dve.wait_ge(logits_copied, NG)

            def spread_e(ap):
                return ap.unsqueeze(2).to_broadcast([P, NT, E])

            def spread_t(ap):
                return ap.unsqueeze(1).to_broadcast([P, NT, E])

            score = logit
            for n in range(2):
                ch.link(dve.tensor_reduce(best[n][:], score[:], AX_X, ALU.max))
                ch.link(dve.tensor_tensor(wk[0][:], score[:], spread_e(best[n][:]), ALU.is_equal))
                ch.link(dve.scalar_tensor_tensor(wk[1][:], wk[0][:], float(E), spread_t(iota_e[:]), ALU.mult, ALU.subtract))
                ch.link(dve.tensor_reduce(ix[:], wk[1][:], AX_X, ALU.max))
                ch.link(dve.tensor_tensor(wk[2][:], wk[1][:], spread_e(ix[:]), ALU.is_equal))
                ch.link(dve.tensor_tensor(oh[n][:], wk[2][:], wk[0][:], ALU.mult))
                if n == 0:
                    ch.link(dve.tensor_scalar(wk[1][:], oh[0][:], -0.5, -BIG, ALU.add, ALU.mult))
                    ch.link(dve.tensor_tensor(wk[3][:], logit[:], wk[1][:], ALU.min))
                    score = wk[3]
            dve.tensor_tensor(chosen[:], oh[0][:], oh[1][:], ALU.add).then_inc(chosen_ready, 1)
            dve.tensor_tensor(ix[:], best[1][:], best[0][:], ALU.subtract).then_inc(score_gap, 1)

            dve.wait_ge(prefix_psum, 1)
            ch.link(dve.tensor_copy(tot[:], pf_ps[:, 1].rearrange("p (t e) -> p e t", e=E)))
            for e in range(E):
                ins = dve.tensor_tensor_scan(inc[:, e], tot[:, e], zeros_nt[:], 0.0, ALU.add, ALU.add)
            ch.link(ins)
            ch.link(dve.tensor_tensor(wk[1][:].rearrange("p t e -> p (t e)").rearrange("p (e t) -> p e t", e=E),
                                      inc[:, :, NT - 1:NT].to_broadcast([P, E, NT]),
                                      iota_cap[:].unsqueeze(1).to_broadcast([P, E, NT]), ALU.is_gt))
            ch.link(dve.tensor_reduce(tiles_e[:], wk[1][:].rearrange("p t e -> p (t e)").rearrange("p (e t) -> p e t", e=E),
                                      AX_X, ALU.add))
            ch.link(dve.tensor_tensor_scan(end_e[:], tiles_e[:], zeros_nt[:, 0:E], 0.0, ALU.add, ALU.add))
            ch.link(dve.tensor_tensor(start_e[:], end_e[:], tiles_e[:], ALU.subtract))
            ch.link(dve.tensor_tensor(inc[:], inc[:], tot[:], ALU.subtract))
            ch.link(dve.scalar_tensor_tensor(tot[:], start_e[:].unsqueeze(2).to_broadcast([P, E, NT]), float(P),
                                             inc[:], ALU.mult, ALU.add))
            ch.link(dve.tensor_tensor(wk[3][:], pf_ps[:, 0].rearrange("p (t e) -> p t e", e=E),
                                      tot[:].rearrange("p e t -> p t e"), ALU.add))
            for n in range(2):
                ch.link(dve.tensor_tensor(wk[0][:], oh[n][:], wk[3][:], ALU.mult))
                ch.link(dve.tensor_reduce(slot_f[:, n], wk[0][:], AX_X, ALU.add))
            ch.link(dve.tensor_copy(t["slots"][:], slot_f[:]))
            dve.tensor_scalar(a_i[:], t["slots"][:].bitcast(I32), 7, None, ALU.logical_shift_right)
            ch.link(dve.tensor_scalar(b_i[:], t["slots"][:].bitcast(I32), P - 1, None, ALU.bitwise_and))
            dve.tensor_copy(a_f[:], a_i[:])
            ch.link(dve.tensor_copy(b_f[:], b_i[:]))
            dve.tensor_scalar(minus_b[:], b_f[:, 1], -1.0, None, ALU.mult).then_inc(slots_split, 1)

            for n in range(1, NT * P // CODES, 2):
                at = slice(n * (CODES // P), (n + 1) * (CODES // P))
                ins = dve.tensor_scalar(code[:, at], code[:, at], -1.0, None, ALU.mult)
            ch.link(ins)

            def tiles_onehot(i, j, first):
                if not first:
                    dve.wait_ge(onehot_used, 2 * i + j - 1)
                for n in range(2):
                    tt = 2 * (2 * i + j) + n
                    dve.tensor_scalar(ohb[:, j, 0, n], row_h[:], b_f[:, 0, ds(tt, 1)], None, ALU.is_equal)
                    for c in range(2):
                        ins = dve.tensor_scalar(oha[:, j, c, n], iota_h[:], a_f[:, c, ds(tt, 1)], code[:, ds(tt, 1)],
                                                ALU.is_equal, ALU.mult)
                ins.then_inc(tile_onehot, 1)

            tiles_onehot(0, 0, True)
            tiles_onehot(0, 1, True)
            with dve.Fori(1, NT // 4) as i:
                tiles_onehot(i, 0, False)
                tiles_onehot(i, 1, False)

            dve.wait_ge(gap_exp, 1)
            dve.wait_ge(onehot_used, NT // 2)
            for half in range(2):
                base = half * 2 * CODES
                ch.link(dve.tensor_copy(coded[:, half], lg_ps[:, half, 0:T]))
                dve.tensor_scalar(positive, coded[:, half], 0.0, float(base - 1), ALU.is_gt, ALU.mult)
                dve.tensor_scalar(negative, coded[:, half], 0.0, float(base + CODES - 1), ALU.is_lt, ALU.mult)
                ch.link(dve.scalar_tensor_tensor(token[:, half], coded[:, half], -1.0, coded[:, half], ALU.mult, ALU.max))
                ch.link(dve.tensor_tensor(token[:, half], token[:, half], positive, ALU.add))
                ch.link(dve.tensor_tensor(token[:, half], token[:, half], negative, ALU.add))
            dve.tensor_tensor(t["token_of_slot"][:], token[:, 0], token[:, 1], ALU.add).then_inc(routed, 1)
            dve.wait_ge(routed, 1)


def experts(nc, t, xn_dram, y_dram, raw_loads):
    T = t["tiles"]
    D = xn_dram.shape[1]
    KD = D // P
    H = t["H"]
    KH = H // P
    WD = KD * H
    E = t["E"]

    with ExitStack() as ctx:
        def sem(name):
            return ctx.enter_context(nc.semaphore(name))

        def tile(name, shape, dt=F32):
            return ctx.enter_context(nc.sbuf_tensor(name, shape, dt))

        idx = [tile(f"idx{n}", [P, 1], U32) for n in range(RING)]
        xg = [tile(f"xg{n}", [P, D]) for n in range(RING)]
        x_hi = tile("x_hi", [P, 2, D], F32R)
        x_lo = tile("x_lo", [P, 2, D], F32R)
        relu = tile("relu", [P, 2, H])
        h2 = tile("h2", [P, 2, H])
        h_hi = tile("h_hi", [P, 2, H], F32R)
        h_lo = tile("h_lo", [P, 2, H], F32R)
        y_sb = tile("y_sb", [P, RING, D])
        spare = tile("spare_2", [1, RING])
        den = tile("den", [P, t["dexp"].shape[1]])
        iota_a = tile("iota_a", [1, T])
        ended = tile("ended", [1, T, E])
        expert_f = tile("expert_f", [1, T])
        minus_half = tile("minus_half_2", [1, 1])
        x_ps = ctx.enter_context(nc.psum_tensor("x_ps", [P, 2, 512], F32))
        h_ps = ctx.enter_context(nc.psum_tensor("h_ps", [P, 2, 512], F32))
        hT_ps = ctx.enter_context(nc.psum_tensor("hT_ps", [P, 2, 512], F32))
        y_ps = ctx.enter_context(nc.psum_tensor("y_ps", [P, 2, 512], F32))

        raw_in = t["raw_in"]
        idx_ready = sem("idx_ready")
        iota_ready, experts_known, dve_chain = sem("iota_ready"), sem("experts_known"), sem("dve_chain_2")
        gathered = [sem(f"gathered{n}") for n in range(RING)]
        x_turned, h_done, h_turned, y_done = sem("x_turned"), sem("h_done"), sem("h_turned"), sem("y_done")
        x_hi_ready, relu_ready, h_hi_ready = sem("x_hi_ready"), sem("relu_ready"), sem("h_hi_ready")
        x_lo_ready, h2_ready, h_lo_ready, y_copied = sem("x_lo_ready"), sem("h2_ready"), sem("h_lo_ready"), sem("y_copied")
        y_stored = [sem(f"y_stored{n}") for n in range(RING)]
        ident, w_hi, w_lo = t["ident"], t["w_hi"], t["w_lo"]
        block = ctx.enter_context(nc.Block())
        TURNS = T // RING
        assert T % RING == 0


        @block.gpsimd
        def _(pool):
            def pick(a, n, i):
                if not (isinstance(i, int) and i == 0):
                    pool.wait_ge(gathered[n], 16 * i)
                pool.tensor_copy(idx[n][:], t["token_of_slot"][:, ds(a, 1)]).then_inc(idx_ready, 1)

            def gather(a, n, i):
                if not (isinstance(i, int) and i == 0):
                    pool.wait_ge(x_turned, a - RING + 1)
                pool.wait_ge(idx_ready, a + 1)
                pool.tensor_tensor(spare[:, n:n + 1], minus_half[:], minus_half[:], ALU.add)
                pool.indirect_dma_start(xg[n][:], None, xn_dram,
                                        bass.IndirectOffsetOnAxis(ap=idx[n][:], axis=0)).then_inc(gathered[n], 16)

            pool.iota(iota_a[:], pattern=[[1, T]], base=0, channel_multiplier=0,
                      allow_small_or_imprecise_dtypes=True).then_inc(iota_ready, 1)
            pool.memset(minus_half[:], -0.5)
            pick(0, 0, 0)
            for n in range(RING):
                pick(n + 1, (n + 1) % RING, (n + 1) // RING)
                gather(n, n, 0)
            with pool.Fori(1, TURNS - 1) as i:
                for n in range(RING):
                    pick(RING * i + n + 1, (n + 1) % RING, i + (n + 1) // RING)
                    gather(RING * i + n, n, i)
            for n in range(RING):
                if n + 1 < RING:
                    pick(T - RING + n + 1, n + 1, TURNS - 1)
                gather(T - RING + n, n, TURNS - 1)

        @block.tensor
        def _(pe):
            def turn_x(a, n, i):
                pe.wait_ge(gathered[n % RING], 16 * (i + n // RING + 1))
                if not (isinstance(a, int) and a < 2):
                    pe.wait_ge(x_lo_ready, a - 1)
                for k in range(KD):
                    tr = pe.transpose(x_ps[:, n % 2, k * P:(k + 1) * P], xg[n % RING][:, k * P:(k + 1) * P], ident[:])
                tr.then_inc(x_turned, 1)

            def weights_of(a, count):
                _, starts = nc.values_load_multi_w_load_instructions(
                    t["tile_expert"][0:1, ds(a, count)], engines=[mybir.EngineType.PE],
                    min_val=0, max_val=(E - 1) * 2 * WD,
                    skip_runtime_bounds_check_because="block 1 caps the expert at E - 1")
                return starts

            def first_product(a, n, start, passes):
                if 0 in passes:
                    pe.wait_ge(x_lo_ready, a + 1)
                    if not (isinstance(a, int) and a < 2):
                        pe.wait_ge(h2_ready, a - 1)
                for m in passes:
                    k = m // 3
                    x, w = ((x_hi, w_hi), (x_hi, w_lo), (x_lo, w_hi))[m % 3]
                    mm = pe.matmul(h_ps[:, n % 2, 0:H], x[:, n % 2, k * P:(k + 1) * P], w[:, ds(start + k * H, H)],
                                   start=(m == 0), stop=(m == 3 * KD - 1))
                if 3 * KD - 1 in passes:
                    mm.then_inc(h_done, 1)

            def turn_h(a, n):
                pe.wait_ge(h2_ready, a + 1)
                if not (isinstance(a, int) and a < 1):
                    pe.wait_ge(h_lo_ready, 2 * a)
                for k in range(KH):
                    part, at = k // (KH // 2), k % (KH // 2) * P
                    tr = pe.transpose(hT_ps[:, part, at:at + P], h2[:, n % 2, k * P:(k + 1) * P], ident[:])
                    if k % (KH // 2) == KH // 2 - 1:
                        tr.then_inc(h_turned, 1)

            def second_product(a, n, start):
                if not (isinstance(a, int) and a < 2):
                    pe.wait_ge(y_copied, a - 1)
                for k in range(KH):
                    if k % (KH // 2) == 0:
                        pe.wait_ge(h_lo_ready, 2 * a + k // (KH // 2) + 1)
                    at = ds(start + WD + k * D, D)
                    hs = slice(k * P, (k + 1) * P)
                    out = y_ps[:, n % 2, 0:D]
                    pe.matmul(out, h_hi[:, n % 2, hs], w_hi[:, at], start=(k == 0), stop=False)
                    pe.matmul(out, h_hi[:, n % 2, hs], w_lo[:, at], start=False, stop=False)
                    mm = pe.matmul(out, h_lo[:, n % 2, hs], w_hi[:, at], start=False, stop=(k == KH - 1))
                mm.then_inc(y_done, 1)

            def step(a, n, i, starts):
                last = isinstance(a, int) and a + 1 >= T
                if not last:
                    first_product(a + 1, n + 1, starts[n + 1], range(0, 2))
                turn_h(a, n)
                if not (isinstance(a, int) and a + 2 >= T):
                    turn_x(a + 2, n + 2, i)
                if not last:
                    first_product(a + 1, n + 1, starts[n + 1], range(2, 3 * KD))
                second_product(a, n, starts[n])

            turn_x(0, 0, 0)
            turn_x(1, 1, 0)
            pe.wait_ge(experts_known, 1)
            starts = weights_of(0, RING + 1)
            first_product(0, 0, starts[0], range(0, 3 * KD))
            for n in range(RING):
                step(n, n, 0, starts)
            with pe.Fori(1, TURNS - 1) as i:
                starts = weights_of(RING * i, RING + 1)
                for n in range(RING):
                    step(RING * i + n, n, i, starts)
            starts = weights_of(T - RING, RING)
            for n in range(RING):
                step(T - RING + n, n, TURNS - 1, starts)

        @block.scalar
        def _(act):
            def high_x(a, n):
                act.wait_ge(x_turned, a + 1)
                if not (isinstance(a, int) and a < 2):
                    act.wait_ge(h_done, a - 1)
                act.activation(x_hi[:, n % 2], x_ps[:, n % 2, 0:D], ACT.Copy).then_inc(x_hi_ready, 1)

            def relu_h(a, n):
                act.wait_ge(h_done, a + 1)
                if not (isinstance(a, int) and a < 2):
                    act.wait_ge(h2_ready, a - 1)
                act.activation(relu[:, n % 2], h_ps[:, n % 2, 0:H], ACT.Relu).then_inc(relu_ready, 1)

            def high_h(a, n):
                if not (isinstance(a, int) and a < 2):
                    act.wait_ge(y_done, a - 1)
                for part, half in enumerate((slice(0, H // 2), slice(H // 2, H))):
                    act.wait_ge(h_turned, 2 * a + part + 1)
                    act.activation(h_hi[:, n % 2, half], hT_ps[:, part, 0:H // 2], ACT.Copy).then_inc(h_hi_ready, 1)

            def step(a, n):
                high_h(a, n)
                if not (isinstance(a, int) and a + 2 >= T):
                    high_x(a + 2, n + 2)
                if not (isinstance(a, int) and a + 1 >= T):
                    relu_h(a + 1, n + 1)

            high_x(0, 0)
            high_x(1, 1)
            relu_h(0, 0)
            for n in range(RING):
                step(n, n)
            with act.Fori(1, TURNS - 1) as i:
                for n in range(RING):
                    step(RING * i + n, n)
            for n in range(RING):
                step(T - RING + n, n)

        @block.vector
        def _(dve):
            def low_x(a, n):
                dve.wait_ge(x_hi_ready, a + 1)
                if not (isinstance(a, int) and a < 2):
                    dve.wait_ge(h_done, a - 1)
                dve.tensor_tensor(x_lo[:, n % 2], x_ps[:, n % 2, 0:D], x_hi[:, n % 2].bitcast(F32),
                                  ALU.subtract).then_inc(x_lo_ready, 1)

            def square(a, n):
                dve.wait_ge(relu_ready, a + 1)
                if not (isinstance(a, int) and a < 2):
                    dve.wait_ge(h_turned, 2 * a - 2)
                dve.tensor_tensor(h2[:, n % 2], h_ps[:, n % 2, 0:H], relu[:, n % 2], ALU.mult).then_inc(h2_ready, 1)

            def low_h(a, n):
                if not (isinstance(a, int) and a < 2):
                    dve.wait_ge(y_done, a - 1)
                for part, half in enumerate((slice(0, H // 2), slice(H // 2, H))):
                    dve.wait_ge(h_hi_ready, 2 * a + part + 1)
                    dve.tensor_tensor(h_lo[:, n % 2, half], hT_ps[:, part, 0:H // 2], h_hi[:, n % 2, half].bitcast(F32),
                                      ALU.subtract).then_inc(h_lo_ready, 1)

            def copy_y(a, n, i):
                dve.wait_ge(y_done, a + 1)
                if not (isinstance(i, int) and i == 0):
                    dve.wait_ge(y_stored[n], 16 * i)
                dve.tensor_copy(y_sb[:, n], y_ps[:, n % 2, 0:D]).then_inc(y_copied, 1)

            def step(a, n, i):
                low_h(a, n)
                if not (isinstance(a, int) and a + 2 >= T):
                    low_x(a + 2, n + 2)
                if not (isinstance(a, int) and a + 1 >= T):
                    square(a + 1, n + 1)
                copy_y(a, n, i)

            ch = Chain(dve, dve_chain)
            dve.wait_ge(iota_ready, 1)
            ch.link(dve.tensor_tensor(ended[:], t["end_e"][0:1].unsqueeze(1).to_broadcast([1, T, E]),
                                      iota_a[:].unsqueeze(2).to_broadcast([1, T, E]), ALU.is_le))
            ch.link(dve.tensor_reduce(expert_f[:], ended[:], AX_X, ALU.add))
            dve.tensor_scalar(t["tile_expert"][:], expert_f[:], float(E - 1), float(2 * WD), ALU.min,
                              ALU.mult).then_inc(experts_known, 1)
            ch.link(dve.tensor_scalar(den[:], t["dexp"][:], 1.0, None, ALU.add))
            ch.link(dve.reciprocal(t["wts"][:, 0], den[:]))
            dve.tensor_tensor(t["wts"][:, 1], t["wts"][:, 0], t["dexp"][:], ALU.mult)

            low_x(0, 0)
            low_x(1, 1)
            square(0, 0)
            for n in range(RING):
                step(n, n, 0)
            with dve.Fori(1, TURNS - 1) as i:
                for n in range(RING):
                    step(RING * i + n, n, i)
            for n in range(RING):
                step(T - RING + n, n, TURNS - 1)

        @block.sync
        def _(sp):
            def store(a, n):
                sp.wait_ge(y_copied, a + 1)
                sp.dma_start(y_dram[ds(a * P, P), :], y_sb[:, n]).then_inc(y_stored[n], 16)

            for n in range(RING):
                store(n, n)
            for dst, src in raw_loads:
                sp.dma_start(dst, src).then_inc(raw_in, 16)
            with sp.Fori(1, TURNS) as i:
                for n in range(RING):
                    store(RING * i + n, n)
            for n in range(RING):
                sp.wait_ge(y_stored[n], 16 * TURNS)
            sp.wait_ge(raw_in, 16 * len(raw_loads))


def weight_plan(D, HID, GHID):
    plan, at = {}, 0
    for name, cols, chunks in (("in", 2 * HID, D // P), ("gates", 2 * HID, HID // P), ("out", D, HID // P),
                               ("grow", 2 * GHID, D // P), ("shrink", D, GHID // P)):
        plan[name] = (at, cols, chunks)
        at += cols * chunks
    return plan, at


def recurrent_and_mix(nc, t, x, xn_dram, y_dram, out, blocks_per_batch):
    N, D = x.shape
    B = GROUP * P
    NB = N // B
    plan = t["plan"]
    KD = D // P
    KV = plan["gates"][2]
    KG = plan["shrink"][2]
    HALO = 3
    assert blocks_per_batch == 2

    def rows(dram, b):
        v = dram.rearrange("(b q p) d -> b p q d", q=GROUP, p=P)
        return v[b] if isinstance(b, int) else v[ds(b, 1)].rearrange("o p q d -> (o p) q d")

    def real(b):
        return not isinstance(b, int) or 0 <= b < NB

    def draining(p):
        return isinstance(p, int) and p == NB

    with ExitStack() as ctx:
        def sem(name):
            return ctx.enter_context(nc.semaphore(name))

        def tile(name, shape, dt=F32):
            return ctx.enter_context(nc.sbuf_tensor(name, shape, dt))

        xn_t = tile("xn_t", [P, GROUP, D])
        scaled = tile("scaled", [P, GROUP, D])
        xT_hi = tile("xT_hi", [P, KD, B], F32R)
        xT_lo = tile("xT_lo", [P, KD, B], F32R)
        x2T_hi = tile("x2T_hi", [P, KD, B], F32R)
        x2T_lo = tile("x2T_lo", [P, KD, B], F32R)
        vraw = tile("vraw", [P, KV, HALO + B])
        vc = tile("vc", [P, KV, B])
        v_hi = tile("v_hi", [P, KV, B], F32R)
        v_lo = tile("v_lo", [P, KV, B], F32R)
        gate = tile("gate", [P, 2, KV, B])
        sigf = tile("sigf", [P, KV, B])
        alpha = tile("alpha", [P, KV, B])
        beta_h = tile("beta_h", [P, KV, B])
        inj = tile("inj", [P, KV, B])
        gh_hi = tile("gh_hi", [P, KV, B], F32R)
        gh_lo = tile("gh_lo", [P, KV, B], F32R)
        lease = Lease(t["shared"])
        ya, yb, mix, x_t = (lease.view(GROUP, D) for _ in range(4))
        gelu2, gv = lease.view(2, B), lease.view(2, B)
        x2 = lease.view(2, GROUP, D)
        gv_hi = tile("gv_hi", [P, KG, B], F32R)
        gv_lo = tile("gv_lo", [P, KG, B], F32R)
        hlast = tile("hlast", [P, KV])
        n2 = tile("n2", [P, GROUP])
        r2 = tile("r2", [P, GROUP])
        minus_half = tile("minus_half", [P, GROUP])
        beta_eps = tile("beta_eps", [P, 1])
        yidx = tile("yidx", [P, 2, GROUP], U32)
        absf, ex, z, z2, poly = (tile(name, [P, KV]) for name in ("absf", "ex", "z", "z2", "poly"))
        spare = tile("spare_3", [1, 1])

        A_ps = ctx.enter_context(nc.psum_tensor("A_ps", [P, 4, 512], F32))
        T_ps = ctx.enter_context(nc.psum_tensor("T_ps", [P, KD, 512], F32))
        O_ps = ctx.enter_context(nc.psum_tensor("O_ps", [P, 2, 512], F32))

        const_ready = sem("const_ready")
        xn_in = sem("xn_in")
        x2_in = [sem(f"x2_in{n}") for n in range(2)]
        x_in = sem("x_in_3")
        y_in = [sem(f"y_in{n}") for n in range(2)]
        yidx_ready = sem("yidx_ready")
        out_stored = sem("out_stored")
        x_turned, in_done, g_done, hawk_done = sem("x_turned_3"), sem("in_done"), sem("g_done"), sem("hawk_done")
        x2_turned, grow_done, mlp_done = sem("x2_turned"), sem("grow_done"), sem("mlp_done")
        x_hi_ready, v_copied, gate_done, v_hi_ready = sem("x_hi_ready_3"), sem("v_copied"), sem("gate_done"), sem("v_hi_ready")
        alpha_ready, a2_ready, beta_ready, sig_done = sem("alpha_ready"), sem("a2_ready"), sem("beta_ready"), sem("sig_done")
        sg_ready, gh_hi_ready, n2_ready = sem("sg_ready"), sem("gh_hi_ready"), sem("n2_ready")
        x2_hi_ready, gelu2_done, gv_hi_ready = sem("x2_hi_ready"), sem("gelu2_done"), sem("gv_hi_ready")
        xr_ready, x_lo_ready, conv_done, v_lo_ready = sem("xr_ready"), sem("x_lo_ready_3"), sem("conv_done"), sem("v_lo_ready")
        om_ready, scan_done, gh_ready, gh_lo_ready = sem("om_ready"), sem("scan_done"), sem("gh_ready"), sem("gh_lo_ready")
        moe_ready, mlp_added, hawk_added, x2r_ready = sem("moe_ready"), sem("mlp_added"), sem("hawk_added"), sem("x2r_ready")
        x2_lo_ready, gv_ready, gv_lo_ready = sem("x2_lo_ready"), sem("gv_ready"), sem("gv_lo_ready")
        dve_chain = sem("dve_chain_3")
        xg1_ready, xg_ready, r2_ready = sem("xg1_ready"), sem("xg_ready"), sem("r2_ready")
        gated, out_mult, out_done = sem("gated"), sem("out_mult"), sem("out_done")

        w_turned, w_hi_ready, w_lo_ready = sem("w_turned"), sem("w_hi_ready"), sem("w_lo_ready")
        exp_ready, rate_ready = sem("exp_ready"), sem("rate_ready")

        w_hi, w_lo, ident, raw = t["wa_hi"], t["wa_lo"], t["ident"], t["raw"]
        PER = 512 // P
        raw_at = []
        for at, cols, chunks in plan.values():
            raw_at += [at + m * chunks * P + k * P for k in range(chunks) for m in range(cols // P)]
        assert len(raw_at) % PER == 0
        BATCHES = len(raw_at) // PER

        def batches_of(name):
            at, cols, chunks = plan[name]
            return -(-(at + cols * chunks) // 512)

        IN, GATES = batches_of("in"), batches_of("gates")
        assert GATES == IN + 2 + KV
        block = ctx.enter_context(nc.Block())

        def run(eng, period, chain=None, first_period=None):
            if first_period:
                first_period()
            else:
                period(0, 0)
            for p in range(1, 4):
                period(p, p % 2)
            n0 = chain.n if chain else 0
            period(4, 0)
            period(5, 1)
            per_turn = chain.n - n0 if chain else 0
            with eng.Fori(3, NB // 2 - 1) as i:
                if chain:
                    chain.repeat(i, 3, per_turn)
                period(2 * i, 0)
                period(2 * i + 1, 1)
            if chain:
                chain.end_turn(NB // 2 - 4, per_turn)
            for p in range(NB - 2, NB + 3):
                period(p, p % 2)

        @block.sync
        def _(sp):
            def load_xn(b):
                if real(b):
                    room(sp, xr_ready, b)
                    sp.dma_start(xn_t[:], rows(xn_dram, b)).then_inc(xn_in, 16)

            def period(p, par):
                if real(p - 3):
                    room(sp, out_done, p - 3)
                    sp.dma_start(x_t[:], rows(x, p - 3)).then_inc(x_in, 16)
                load_xn(p + 1)
                if real(p - 1):
                    room(sp, out_mult, p - 2)
                    if isinstance(p, int) and p == 1:
                        sp.wait_ge(w_turned, BATCHES)
                    sp.dma_start(x2[:, 1 - par], rows(xn_dram, p - 1)).then_inc(x2_in[1 - par], 16)
                if real(p - 3):
                    sp.wait_ge(out_done, p - 2)
                    sp.dma_start(rows(out, p - 3), mix[:]).then_inc(out_stored, 16)

            load_xn(0)
            run(sp, period)
            sp.wait_ge(out_stored, 16 * NB)

        @block.tensor
        def _(pe):
            def product(out, lhs_hi, lhs_lo, rhs_hi, rhs_lo, first, last):
                pe.matmul(out, lhs_hi, rhs_hi, start=first, stop=False)
                pe.matmul(out, lhs_hi, rhs_lo, start=False, stop=False)
                return pe.matmul(out, lhs_lo, rhs_hi, start=False, stop=last)

            def channels(name, m, bank, a_hi, a_lo):
                at, cols, chunks = plan[name]
                for k in range(chunks):
                    w = slice(at + k * cols + m * P, at + k * cols + (m + 1) * P)
                    mm = product(A_ps[:, bank], w_hi[:, w], w_lo[:, w], a_hi[:, k], a_lo[:, k], k == 0, k == chunks - 1)
                return mm

            def tokens(name, q, a_hi, a_lo):
                at, cols, chunks = plan[name]
                for k in range(chunks):
                    w = slice(at + k * cols, at + (k + 1) * cols)
                    a = slice(q * P, (q + 1) * P)
                    mm = product(O_ps[:, q // 2, (q % 2) * D:(q % 2 + 1) * D], a_hi[:, k, a], a_lo[:, k, a],
                                 w_hi[:, w], w_lo[:, w], k == 0, k == chunks - 1)
                return mm

            def turn(src, done):
                for k in range(KD):
                    for q in range(GROUP):
                        tr = pe.transpose(T_ps[:, k, q * P:(q + 1) * P], src[:, q, k * P:(k + 1) * P], ident[:])
                tr.then_inc(done, 1)

            def prepare(batches):
                for n in batches:
                    room(pe, w_lo_ready, n - 1)
                    for q in range(PER):
                        tr = pe.transpose(O_ps[:, n % 2, q * P:(q + 1) * P], raw[:, raw_at[n * PER + q]:][:, 0:P], ident[:])
                    tr.then_inc(w_turned, 1)

            def turn_x(b):
                if real(b):
                    pe.wait_ge(xr_ready, b + 1)
                    room(pe, x2_lo_ready, b - 2)
                    room(pe, x_lo_ready, b)
                    turn(scaled, x_turned)

            def s1(b, ns):
                if not real(b):
                    return
                for n in ns:
                    if n == 0:
                        pe.wait_ge(x_lo_ready, b + 1)
                        if isinstance(b, int) and b == 0:
                            pe.wait_ge(w_lo_ready, IN)
                    if n < 4:
                        room(pe, sig_done, 2 * KV * (b - 1) + 3 + n)
                    else:
                        pe.wait_ge(v_copied, KV * b + n - 3)
                    channels("in", (n + KV) % (2 * KV), n % 4, xT_hi, xT_lo).then_inc(in_done, 1)

            def s2(b, ms):
                if not real(b):
                    return
                for m in ms:
                    if m == 0:
                        pe.wait_ge(v_lo_ready, KV * (b + 1))
                        pe.wait_ge(gate_done, KV * (b + 1))
                        if isinstance(b, int) and b == 0:
                            pe.wait_ge(w_lo_ready, GATES)
                    if m < 4:
                        if real(b - 2):
                            pe.wait_ge((gelu2_done, gv_ready)[m % 2], KG * (b - 2) + 3 + m // 2)
                    else:
                        pe.wait_ge(sig_done, 2 * KV * b + m - 3)
                    channels("gates", m, (m + 2) % 4, v_hi, v_lo).then_inc(g_done, 1)

            def s3(b):
                if not real(b):
                    return
                pe.wait_ge(gh_lo_ready, KV * (b + 1))
                if isinstance(b, int) and b == 0:
                    pe.wait_ge(w_lo_ready, BATCHES)
                for q in range(GROUP):
                    if q % 2 == 0:
                        room(pe, mlp_added, 2 * (b - 2) + q // 2 + 1)
                    mm = tokens("out", q, gh_hi, gh_lo)
                    if q % 2:
                        mm.then_inc(hawk_done, 1)

            def s4(b):
                if real(b):
                    pe.wait_ge(x2r_ready, b + 1)
                    pe.wait_ge(x_lo_ready, min(b + 3, NB) if isinstance(b, int) else b + 3)
                    turn(scaled, x2_turned)

            def s5(b):
                if not real(b):
                    return
                pe.wait_ge(x2_lo_ready, b + 1)
                for n in range(2 * KG):
                    c, half = n // 2, n % 2
                    if n >= 4:
                        pe.wait_ge((gelu2_done, gv_ready)[half], KG * b + c - 1)
                    elif not real(b + 2):
                        if n == 0:
                            pe.wait_ge(sig_done, 2 * KV * NB)
                            pe.wait_ge(gelu2_done, KG * b)
                            pe.wait_ge(gv_ready, KG * b)
                    elif n == 0:
                        pe.wait_ge(v_copied, KV * (b + 3))
                    else:
                        pe.wait_ge(gate_done, KV * (b + 2) + n)
                    channels("grow", c + half * KG, (n + 2) % 4, x2T_hi, x2T_lo).then_inc(grow_done, 1)

            def s6(b):
                if not real(b):
                    return
                pe.wait_ge(gv_lo_ready, KG * (b + 1))
                for q in range(GROUP):
                    if q % 2 == 0:
                        pe.wait_ge(hawk_added, min(2 * b + q // 2 + 3, 2 * NB) if isinstance(b, int) else 2 * b + q // 2 + 3)
                    mm = tokens("shrink", q, gv_hi, gv_lo)
                    if q % 2:
                        mm.then_inc(mlp_done, 1)

            def period(p, par):
                s1(p, range(KV, 2 * KV))
                s5(p - 2)
                s2(p, range(0, 4))
                turn_x(p + 1)
                s2(p, range(4, 2 * KV))
                s3(p - 1)
                s1(p + 1, range(0, KV))
                s6(p - 2)
                s4(p - 1)

            def first_period():
                s1(0, range(KV, 2 * KV))
                s2(0, [0])
                prepare(range(GATES, GATES + 2))
                s2(0, [1])
                turn_x(1)
                prepare(range(GATES + 2, GATES + 4))
                s2(0, [2])
                prepare(range(GATES + 4, GATES + 6))
                s2(0, [3])
                prepare(range(GATES + 6, BATCHES))
                s2(0, range(4, 2 * KV))
                s1(1, range(0, KV))

            prepare(range(0, IN))
            turn_x(0)
            prepare(range(IN, IN + 2))
            for c in range(KV):
                s1(0, [c])
                prepare([IN + 2 + c])
            run(pe, period, first_period=first_period)

        @block.scalar
        def _(act):
            def high_x(b):
                if real(b):
                    act.wait_ge(x_turned, b + 1)
                    room(act, in_done, 2 * KV * b)
                    for k in range(KD):
                        ins = act.activation(xT_hi[:, k], T_ps[:, k], ACT.Copy, scale=t["gamma1"][:, k:k + 1])
                    ins.then_inc(x_hi_ready, 1)

            def copy_v(b, chunks=range(KV)):
                for c in chunks if real(b) else ():
                    act.wait_ge(in_done, 2 * KV * b + c + 1)
                    room(act, conv_done, KV * (b - 1) + c + 1)
                    act.activation(vraw[:, c, HALO:], A_ps[:, c % 4], ACT.Copy).then_inc(v_copied, 1)

            def gelu_gate(b, par):
                for c in range(KV):
                    act.wait_ge(in_done, 2 * KV * b + KV + c + 1)
                    room(act, gh_ready, KV * (b - 2) + c + 1)
                    act.activation(gate[:, par, c], A_ps[:, (KV + c) % 4], ACT.Gelu).then_inc(gate_done, 1)

            def high_v(b, c):
                if real(b):
                    act.wait_ge(conv_done, KV * b + c + 1)
                    room(act, g_done, 2 * KV * b)
                    act.activation(v_hi[:, c], vc[:, c], ACT.Copy).then_inc(v_hi_ready, 1)

            def high_x2(b):
                act.wait_ge(x2_turned, b + 1)
                room(act, grow_done, 2 * KG * b)
                for k in range(KD):
                    ins = act.activation(x2T_hi[:, k], T_ps[:, k], ACT.Copy, scale=t["gamma2"][:, k:k + 1])
                ins.then_inc(x2_hi_ready, 1)

            def gelu(b, c):
                if real(b):
                    act.wait_ge(grow_done, 2 * KG * b + 2 * c + 1)
                    room(act, gv_ready, KG * b + c - 1)
                    act.activation(gelu2[:, c % 2], A_ps[:, (2 * c + 2) % 4], ACT.Gelu).then_inc(gelu2_done, 1)

            def high_gv(b, c):
                if real(b):
                    act.wait_ge(gv_ready, KG * b + c + 1)
                    room(act, mlp_done, 2 * b)
                    act.activation(gv_hi[:, c], gv[:, c % 2], ACT.Copy).then_inc(gv_hi_ready, 1)

            def gates(b, ms):
                if not real(b):
                    return
                for m in ms:
                    act.wait_ge(g_done, 2 * KV * b + m + 1)
                    dst = sigf[:, m] if m < KV else inj[:, m - KV]
                    if m < KV:
                        room(act, alpha_ready, KV * b)
                    else:
                        room(act, scan_done, KV * (b - 1) + m - KV + 1)
                    act.activation(dst, A_ps[:, (m + 2) % 4], ACT.Sigmoid,
                                   bias=t["b_gates"][:, m:m + 1]).then_inc(sig_done, 1)

            def high_gh(b):
                if real(b):
                    for c in range(KV):
                        act.wait_ge(gh_ready, KV * b + c + 1)
                        room(act, hawk_done, 2 * b)
                        act.activation(gh_hi[:, c], beta_h[:, c], ACT.Copy).then_inc(gh_hi_ready, 1)

            def decay(b):
                if isinstance(b, int) and b == 0:
                    act.wait_ge(rate_ready, 1)
                for c in range(KV):
                    act.wait_ge(sig_done, 2 * KV * b + c + 1)
                    room(act, scan_done, KV * (b - 1) + c + 1)
                    act.activation(alpha[:, c], sigf[:, c], ACT.Exp,
                                   scale=t["log_rate"][:, c:c + 1]).then_inc(alpha_ready, 1)
                for c in range(KV):
                    act.wait_ge(alpha_ready, KV * b + c + 1)
                    room(act, gh_lo_ready, KV * (b - 1) + c + 1)
                    act.activation(beta_h[:, c], alpha[:, c], ACT.Square).then_inc(a2_ready, 1)

            def root(b):
                for c in range(KV):
                    act.wait_ge(om_ready, KV * b + c + 1)
                    act.activation(beta_h[:, c], beta_h[:, c], ACT.Sqrt, bias=beta_eps[:]).then_inc(beta_ready, 1)

            def prepare(batches):
                for n in batches:
                    act.wait_ge(w_turned, n + 1)
                    act.activation(w_hi[:, n * 512:(n + 1) * 512], O_ps[:, n % 2], ACT.Copy).then_inc(w_hi_ready, 1)

            def period(p, par):
                def squares(b, bpar):
                    if real(b):
                        act.wait_ge(hawk_added, 2 * b + 2)
                        act.wait_ge(x_turned, min(b + 3, NB) if isinstance(b, int) else b + 3)
                        for q in range(GROUP):
                            ins = act.activation(scaled[:, q], x2[:, bpar, q], ACT.Square, accum_out=n2[:, q:q + 1])
                        ins.then_inc(n2_ready, 1)

                b = p - 2
                if real(b):
                    high_x2(b)
                if real(p):
                    gelu_gate(p, par)
                high_v(p, 0)
                gelu(b, 0)
                high_v(p, 1)
                gelu(b, 1)
                high_gv(b, 0)
                if draining(p):
                    high_gh(p - 1)
                high_v(p, 2)
                gelu(b, 2)
                high_gv(b, 1)
                gelu(b, 3)
                high_gv(b, 2)
                high_gv(b, 3)
                gates(p, range(0, KV))
                if not draining(p):
                    high_gh(p - 1)
                high_x(p + 1)
                gates(p, range(KV, 2 * KV))
                if real(b):
                    act.wait_ge(moe_ready, b + 1)
                    room(act, out_stored, 16 * b)
                    act.activation(mix[:], ya[:], ACT.Sigmoid).then_inc(sg_ready, 1)
                if real(p):
                    decay(p)
                copy_v(p + 1)
                squares(p - 1, 1 - par)
                if real(p):
                    root(p)

            def first_period():
                gelu_gate(0, 0)
                for c in range(KV):
                    high_v(0, c)
                prepare(range(GATES, GATES + 2))
                gates(0, [0])
                high_x(1)
                prepare(range(GATES + 2, GATES + 4))
                gates(0, [1])
                prepare(range(GATES + 4, GATES + 6))
                gates(0, [2])
                prepare(range(GATES + 6, BATCHES))
                gates(0, range(KV, 2 * KV))
                decay(0)
                copy_v(1)
                root(0)

            prepare(range(0, IN))
            high_x(0)
            prepare(range(IN, IN + 2))
            act.wait_ge(const_ready, 1)
            for c in range(KV):
                copy_v(0, [c])
                prepare([IN + 2 + c])
            act.activation(absf[:], t["forget_base"][:], ACT.Abs).then_inc(exp_ready, 1)
            act.wait_ge(exp_ready, 1)
            act.activation(ex[:], absf[:], ACT.Exp, scale=-1.0).then_inc(exp_ready, 1)
            run(act, period, first_period=first_period)

        @block.vector
        def _(dve):
            ch = Chain(dve, dve_chain)
            dve.memset(beta_eps[:], BETA_EPS)
            dve.memset(minus_half[:], -0.5)
            ch.link(dve.memset(vraw[:, :, 0:HALO], 0.0))
            dve.memset(hlast[:], 0.0).then_inc(const_ready, 1)

            def prepare(batches):
                for n in batches:
                    at = slice(n * 512, (n + 1) * 512)
                    dve.wait_ge(w_hi_ready, n + 1)
                    dve.tensor_tensor(w_lo[:, at], O_ps[:, n % 2], w_hi[:, at].bitcast(F32),
                                      ALU.subtract).then_inc(w_lo_ready, 1)

            def rates():
                dve.wait_ge(exp_ready, 2)
                ch.link(dve.tensor_scalar(z[:], ex[:], 2.0, None, ALU.add))
                ch.link(dve.reciprocal(z2[:], z[:]))
                ch.link(dve.tensor_tensor(z[:], ex[:], z2[:], ALU.mult))
                ch.link(dve.tensor_tensor(z2[:], z[:], z[:], ALU.mult))
                ch.link(dve.tensor_scalar(poly[:], z2[:], 1.0 / 17, 1.0 / 15, ALU.mult, ALU.add))
                for odd in (13, 11, 9, 7, 5, 3, 1):
                    ch.link(dve.tensor_tensor(poly[:], poly[:], z2[:], ALU.mult))
                    ch.link(dve.tensor_scalar(poly[:], poly[:], 1.0 / odd, None, ALU.add))
                ch.link(dve.tensor_tensor(poly[:], poly[:], z[:], ALU.mult))
                ch.link(dve.tensor_scalar(z[:], t["forget_base"][:], 0.0, None, ALU.max))
                ch.link(dve.scalar_tensor_tensor(poly[:], poly[:], 2.0, z[:], ALU.mult, ALU.add))
                dve.tensor_scalar(t["log_rate"][:], poly[:], ALPHA_LOG_SCALE, None, ALU.mult).then_inc(rate_ready, 1)

            def scale_x(b):
                if real(b):
                    dve.wait_ge(xn_in, 16 * (b + 1))
                    room(dve, x2_turned, b - 2)
                    room(dve, x_turned, b)
                    for q in range(GROUP):
                        ins = dve.tensor_scalar(scaled[:, q], xn_t[:, q], t["r1"][:, ds(GROUP * b + q, 1)],
                                                None, ALU.mult)
                    ins.then_inc(xr_ready, 1)

            def low(b, gamma, hi, lo, hi_ready, lo_ready, used, value):
                dve.wait_ge(hi_ready, b + 1)
                room(dve, used, value)
                for k in range(KD):
                    ins = dve.scalar_tensor_tensor(lo[:, k], T_ps[:, k], gamma[:, k:k + 1], hi[:, k].bitcast(F32),
                                                   ALU.mult, ALU.subtract)
                ins.then_inc(lo_ready, 1)

            def low_x(b):
                if real(b):
                    low(b, t["gamma1"], xT_hi, xT_lo, x_hi_ready, x_lo_ready, in_done, 2 * KV * b)

            def convolve(b, par, c):
                if real(b):
                    dve.wait_ge(v_copied, KV * b + c + 1)
                    room(dve, xg1_ready, KV * (b - 1) + c + 1)
                    room(dve, v_lo_ready, KV * (b - 1) + c + 1)
                    ch.link(dve.tensor_scalar(vc[:, c], vraw[:, c, 0:B], t["conv_w"][:, c, 0:1], t["conv_b"][:, c:c + 1],
                                              ALU.mult, ALU.add))
                    for k in range(1, HALO + 1):
                        ch.link(dve.scalar_tensor_tensor(vc[:, c], vraw[:, c, k:k + B], t["conv_w"][:, c, k:k + 1],
                                                         vc[:, c], ALU.mult, ALU.add))
                    if par == 0:
                        ins = dve.tensor_copy(vraw[:, c, 0:HALO], vraw[:, c, B:B + HALO])
                    else:
                        ins = dve.memset(vraw[:, c, 0:HALO], 0.0)
                    ins.then_inc(conv_done, 1)

            def mixture(b):
                for n in range(2):
                    dve.wait_ge(y_in[n], 16 * GROUP * (b + 1))
                for q in range(GROUP):
                    ins = dve.tensor_scalar(ya[:, q], ya[:, q], t["wts"][:, 0, ds(GROUP * b + q, 1)], None, ALU.mult)
                ch.link(ins)
                for q in range(GROUP):
                    ins = dve.scalar_tensor_tensor(ya[:, q], yb[:, q], t["wts"][:, 1, ds(GROUP * b + q, 1)], ya[:, q],
                                                   ALU.mult, ALU.add)
                ins.then_inc(moe_ready, 1)

            def low_v(b, c):
                if real(b):
                    dve.wait_ge(v_hi_ready, KV * b + c + 1)
                    room(dve, g_done, 2 * KV * b)
                    dve.tensor_tensor(v_lo[:, c], vc[:, c], v_hi[:, c].bitcast(F32),
                                      ALU.subtract).then_inc(v_lo_ready, 1)

            def add_mlp(b, par):
                for n in range(2):
                    dve.wait_ge(mlp_done, 2 * b + n + 1)
                    xs = x2[:, par, 2 * n:2 * n + 2].rearrange("p q d -> p (q d)")
                    dve.tensor_tensor(xs, O_ps[:, n], xs, ALU.add).then_inc(mlp_added, 1)

            def add_hawk(b, par):
                dve.wait_ge(x2_in[par], 16 * (b // 2 + 1) if isinstance(b, int) else (b - par) * 8 + 16)
                for n in range(2):
                    dve.wait_ge(hawk_done, 2 * b + n + 1)
                    xs = x2[:, par, 2 * n:2 * n + 2].rearrange("p q d -> p (q d)")
                    dve.tensor_tensor(xs, O_ps[:, n], xs, ALU.add).then_inc(hawk_added, 1)

            def recur(b, par):
                for c in range(KV):
                    dve.wait_ge(xg_ready, KV * b + c + 1)
                    dve.tensor_tensor_scan(beta_h[:, c], alpha[:, c], inj[:, c], 0.0 if par == 0 else hlast[:, c:c + 1],
                                           ALU.mult, ALU.add).then_inc(scan_done, 1)
                if par == 0:
                    dve.wait_ge(scan_done, KV * (b + 1))
                    ch.link(dve.tensor_copy(hlast[:], beta_h[:, :, B - 1]))
                for c in range(KV):
                    dve.wait_ge(scan_done, KV * b + c + 1)
                    dve.wait_ge(gate_done, KV * b + c + 1)
                    dve.tensor_tensor(beta_h[:, c], gate[:, par, c], beta_h[:, c], ALU.mult).then_inc(gh_ready, 1)

            def low_gh(b):
                for c in range(KV):
                    dve.wait_ge(gh_hi_ready, KV * b + c + 1)
                    room(dve, hawk_done, 2 * b)
                    dve.tensor_tensor(gh_lo[:, c], beta_h[:, c], gh_hi[:, c].bitcast(F32),
                                      ALU.subtract).then_inc(gh_lo_ready, 1)

            def multiply(b, c):
                if real(b):
                    dve.wait_ge(gelu2_done, KG * b + c + 1)
                    dve.wait_ge(grow_done, 2 * KG * b + 2 * c + 2)
                    room(dve, gv_lo_ready, KG * b + c - 1)
                    dve.tensor_tensor(gv[:, c % 2], A_ps[:, (2 * c + 3) % 4], gelu2[:, c % 2],
                                      ALU.mult).then_inc(gv_ready, 1)

            def low_gv(b, c):
                if real(b):
                    dve.wait_ge(gv_hi_ready, KG * b + c + 1)
                    room(dve, mlp_done, 2 * b)
                    dve.tensor_tensor(gv_lo[:, c], gv[:, c % 2], gv_hi[:, c].bitcast(F32),
                                      ALU.subtract).then_inc(gv_lo_ready, 1)

            def one_minus(b):
                if real(b):
                    for c in range(KV):
                        dve.wait_ge(a2_ready, KV * b + c + 1)
                        dve.tensor_scalar(beta_h[:, c], beta_h[:, c], -1.0, 1.0, ALU.mult, ALU.add).then_inc(om_ready, 1)

            def first_period():
                convolve(0, 0, 1)
                low_v(0, 0)
                convolve(0, 0, 2)
                low_v(0, 1)
                low_v(0, 2)
                scale_x(1)
                prepare(range(GATES, GATES + 2))
                low_x(1)
                prepare(range(GATES + 2, GATES + 4))
                rates()
                prepare(range(GATES + 4, BATCHES))
                one_minus(0)
                convolve(1, 1, 0)

            def period(p, par):
                b = p - 2
                convolve(p, par, 1)
                if real(b):
                    low(b, t["gamma2"], x2T_hi, x2T_lo, x2_hi_ready, x2_lo_ready, grow_done, 2 * KG * b)
                if real(p - 3):
                    add_mlp(p - 3, 1 - par)
                low_v(p, 0)
                convolve(p, par, 2)
                multiply(b, 0)
                low_v(p, 1)
                multiply(b, 1)
                low_gv(b, 0)
                if draining(p):
                    recur(p - 1, 1 - par)
                    low_gh(p - 1)
                low_v(p, 2)
                multiply(b, 2)
                low_gv(b, 1)
                multiply(b, 3)
                low_gv(b, 2)
                low_gv(b, 3)
                scale_x(p + 1)
                if real(p - 1) and not draining(p):
                    recur(p - 1, 1 - par)
                    low_gh(p - 1)
                if real(b):
                    mixture(b)
                low_x(p + 1)
                if real(p - 1):
                    add_hawk(p - 1, 1 - par)
                one_minus(p)
                convolve(p + 1, 1 - par, 0)
                if real(p - 1):
                    dve.wait_ge(r2_ready, p)
                    for q in range(GROUP):
                        ins = dve.tensor_scalar(scaled[:, q], x2[:, 1 - par, q], r2[:, q:q + 1], float(D) ** 0.5,
                                                ALU.mult, ALU.mult)
                    ins.then_inc(x2r_ready, 1)

            prepare(range(0, IN))
            scale_x(0)
            low_x(0)
            prepare(range(IN, IN + 2))
            convolve(0, 0, 0)
            prepare(range(IN + 2, GATES))
            run(dve, period, ch, first_period)

        @block.gpsimd
        def _(pool):
            def period(p, par):
                b = p - 1
                if real(b):
                    for c in range(KV):
                        pool.wait_ge(xg1_ready, KV * b + c + 1)
                        pool.wait_ge(beta_ready, KV * b + c + 1)
                        pool.tensor_tensor(inj[:, c], inj[:, c], beta_h[:, c], ALU.mult).then_inc(xg_ready, 1)
                if real(p - 3):
                    e = p - 3
                    pool.wait_ge(gated, e + 1)
                    pool.wait_ge(mlp_added, 2 * e + 2)
                    pool.tensor_tensor(mix[:], mix[:], x2[:, 1 - par], ALU.mult).then_inc(out_mult, 1)
                    pool.wait_ge(out_mult, e + 1)
                    pool.wait_ge(x_in, 16 * (e + 1))
                    pool.tensor_tensor(mix[:], mix[:], x_t[:], ALU.add).then_inc(out_done, 1)
                if real(p):
                    for c in range(KV):
                        pool.wait_ge(sig_done, 2 * KV * p + KV + c + 1)
                        pool.tensor_tensor(inj[:, c], inj[:, c], vc[:, c], ALU.mult).then_inc(xg1_ready, 1)
                if real(p - 2):
                    pool.wait_ge(sg_ready, p - 1)
                    pool.tensor_tensor(mix[:], mix[:], ya[:], ALU.mult).then_inc(gated, 1)
                if real(b):
                    pool.wait_ge(n2_ready, b + 1)
                    pool.tensor_tensor(r2[:], n2[:], minus_half[:], ALU.pow).then_inc(r2_ready, 1)
                    room(pool, moe_ready, b)
                    room(pool, gated, b)
                    for n in range(2):
                        room(pool, y_in[n], 16 * GROUP * b)
                    pool.tensor_copy(yidx[:], t["slots"][:, :, ds(GROUP * b, GROUP)]).then_inc(yidx_ready, 1)
                    pool.wait_ge(yidx_ready, b + 1)
                    pool.tensor_tensor(spare[:], minus_half[0:1, 0:1], minus_half[0:1, 0:1], ALU.add)
                    for n, dst in enumerate((ya, yb)):
                        for q in range(GROUP):
                            pool.indirect_dma_start(dst[:, q], None, y_dram,
                                                    bass.IndirectOffsetOnAxis(ap=yidx[:, n, q:q + 1], axis=0)
                                                    ).then_inc(y_in[n], 16)

            pool.wait_ge(const_ready, 1)
            run(pool, period)


def build(nc, x, gamma1, W_in, conv_w, conv_b, W_gates, b_gates, forget_base, W_out, gamma2, W_grow, W_shrink,
          router_w, w1, w2, out, xn_dram, y_dram):
    batches, S, D = x.shape
    N = batches * S
    E, _, H = w1.shape
    HID, GHID = W_out.shape[1], W_shrink.shape[1]
    T = 2 * N // P + E
    T = -(-T // RING) * RING
    xf = x.rearrange("b s d -> (b s) d")
    of = out.rearrange("b s d -> (b s) d")
    plan, columns = weight_plan(D, HID, GHID)

    with ExitStack() as ctx:
        def keep(name, shape, dt=F32):
            return ctx.enter_context(nc.sbuf_tensor(name, shape, dt))

        t = dict(tiles=T, E=E, H=H, plan=plan)
        t["ident"] = keep("ident", [P, P])
        t["r1"] = keep("r1", [P, N // P])
        t["slots"] = keep("slots", [P, 2, N // P], U32)
        t["wts"] = keep("wts", [P, 2, N // P])
        t["dexp"] = keep("dexp", [P, N // P])
        t["end_e"] = keep("end_e", [P, E])
        t["token_of_slot"] = keep("token_of_slot", [P, T], U32)
        t["tile_expert"] = keep("tile_expert", [1, T], I32)
        t["conv_w"] = keep("conv_w_sb", [P, HID // P, 4])
        t["conv_b"] = keep("conv_b_sb", [P, HID // P])
        t["b_gates"] = keep("b_gates_sb", [P, 2 * HID // P])
        t["forget_base"] = keep("forget_sb", [P, HID // P])
        t["log_rate"] = keep("log_rate", [P, HID // P])
        t["gamma1"] = keep("gamma1_sb", [P, D // P])
        t["gamma2"] = keep("gamma2_sb", [P, D // P])
        t["raw_in"] = ctx.enter_context(nc.semaphore("raw_in"))
        ctx.enter_context(nc.allow_non_contiguous_dma(reason="small vectors, one element a partition"))

        t["shared"] = keep("shared", [P, 8 * GROUP * D])
        assert columns <= 8 * GROUP * D

        with ExitStack() as moe:
            WE = E * 2 * (D // P) * H
            t["w_hi"] = moe.enter_context(nc.sbuf_tensor("w_hi", [P, WE], F32R))
            t["w_lo"] = moe.enter_context(nc.sbuf_tensor("w_lo", [P, WE], F32R))
            normalise_and_route(nc, t, xf, router_w, w1, w2, xn_dram)
            t["raw"] = t["shared"][:, 0:columns]
            loads = []
            for name, w in (("in", W_in), ("gates", W_gates), ("out", W_out), ("grow", W_grow), ("shrink", W_shrink)):
                at, cols, chunks = plan[name]
                loads.append((t["raw"][:, at:at + cols * chunks].rearrange("p (m k) -> p m k", k=chunks * P),
                              w.rearrange("(m p) k -> p m k", p=P)))
            loads.append((t["conv_w"][:], conv_w.rearrange("(c p) o k -> p c (o k)", p=P)))
            for name, v in (("conv_b", conv_b), ("b_gates", b_gates), ("forget_base", forget_base),
                            ("gamma1", gamma1), ("gamma2", gamma2)):
                loads.append((t[name][:], v.rearrange("(c p) -> p c", p=P)))
            experts(nc, t, xn_dram, y_dram, loads)
        t["wa_hi"] = keep("wa_hi", [P, columns], F32R)
        t["wa_lo"] = keep("wa_lo", [P, columns], F32R)
        recurrent_and_mix(nc, t, xf, xn_dram, y_dram, of, S // (GROUP * P))


INPUTS = ["L0_attn_x", "L0_attn_gamma1", "L0_attn_W_in", "L0_attn_conv_w", "L0_attn_conv_b", "L0_attn_W_gates",
          "L0_attn_b_gates", "L0_attn_forget_base", "L0_attn_W_out", "L0_attn_gamma2", "L0_attn_W_grow",
          "L0_attn_W_shrink", "L0_ffn_router_w", "L0_ffn_w1", "L0_ffn_w2"]


def kernel(**inputs):
    import numpy as np
    import concourse.bacc as bacc
    from concourse.bass_utils import run_bass_kernel_spmd

    nc = bacc.Bacc("TRN2", target_bir_lowering=False, num_devices=1)
    arrays, args = {}, []
    for name in INPUTS:
        a = np.ascontiguousarray(inputs[name])
        arrays[f"in_{name}"] = a
        args.append(nc.dram_tensor(f"in_{name}", a.shape, mybir.dt.from_np(a.dtype), kind="ExternalInput").ap())
    b, s, d = inputs["L0_attn_x"].shape
    e = inputs["L0_ffn_w1"].shape[0]
    tiles = -(-(2 * b * s // P + e) // RING) * RING
    out = nc.dram_tensor("out_0", (b, s, d), F32, kind="ExternalOutput").ap()
    xn_dram = nc.dram_tensor("xn_rows", (b * s, d), F32, kind="Internal").ap()
    y_dram = nc.dram_tensor("y_rows", (tiles * P, d), F32, kind="Internal").ap()
    build(nc, *args, out, xn_dram, y_dram)
    r = run_bass_kernel_spmd(nc, [arrays], core_ids=[0])
    return r.results[0]["out_0"]
```
